# Optimizing a Trainium2 kernel written in Bass

```python
import numpy as np
import jax
import jax.numpy as jnp

def _softmax(x, axis=-1):
    return jax.nn.softmax(x, axis=axis)

def _gelu(x):
    return jax.nn.gelu(x, approximate=True)

def _silu(x):
    return jax.nn.silu(x)

def _sigmoid(x):
    return jax.nn.sigmoid(x)

def _layernorm(x, axis=-1, eps=1e-05):
    m = jnp.mean(x, axis=axis, keepdims=True)
    v = jnp.var(x, axis=axis, keepdims=True)
    return (x - m) / jnp.sqrt(v + eps)

def _scatter_add(tgt, idx, src, axis=0):
    return tgt.at[idx].add(src)

def _segment_sum(src, seg, n):
    return jax.ops.segment_sum(src, seg, n)
kernel_name = 'mk_recurrent_d2_jaxref_r8_9a9610'

def setup_inputs(seed: int=0):
    np.random.seed(seed)
    _w = jnp.asarray

    def _L0_attn_setup():
        import jax, jax.numpy as jnp
        import numpy as np
        from math import sqrt
        N_HEAD = 16
        W_SCALE = 0.02

        def _reference_tuple_inner(x, W_dq, W_uq, W_dkv, W_uk, W_uv, W_o):
            B, T, C = x.shape
            nh = N_HEAD
            hs = C // nh
            n_kvl = W_dkv.shape[0]
            k_eff = (W_dq.T @ W_uq.T @ W_uk).reshape(nh, hs, n_kvl)
            v_eff = jnp.transpose((W_uv.T @ W_o.T).reshape(n_kvl, nh, hs), (1, 0, 2))
            c_kv = x @ W_dkv.T
            q = x @ W_dq.T @ W_uq.T
            q = q.reshape(B, T, nh, hs)
            q_lat = jnp.einsum('bqhd,hdl->bhql', q, k_eff)
            attn = jnp.einsum('bhql,bkl->bhqk', q_lat, c_kv) / sqrt(hs)
            causal = jnp.tril(jnp.ones((T, T), dtype=bool))
            attn = jnp.where(causal[None, None], attn, -jnp.inf)
            attn = jax.nn.softmax(attn, axis=-1)
            y_lat = jnp.einsum('bhqk,bkl->bhql', attn, c_kv)
            y = jnp.einsum('bhql,hld->bqhd', y_lat, v_eff).reshape(B, T, C)
            return (y, c_kv)
        key = jax.random.key(seed)
        ks = jax.random.split(key, 7)
        B, T, C = (2, 256, 128)
        QL, KVL = (64, 64)
        return {'x': jax.random.normal(ks[0], (B, T, C), dtype=jnp.float32), 'W_dq': jax.random.normal(ks[1], (QL, C), dtype=jnp.float32) * W_SCALE, 'W_uq': jax.random.normal(ks[2], (C, QL), dtype=jnp.float32) * W_SCALE, 'W_dkv': jax.random.normal(ks[3], (KVL, C), dtype=jnp.float32) * W_SCALE, 'W_uk': jax.random.normal(ks[4], (C, KVL), dtype=jnp.float32) * W_SCALE, 'W_uv': jax.random.normal(ks[5], (C, KVL), dtype=jnp.float32) * W_SCALE, 'W_o': jax.random.normal(ks[6], (C, C), dtype=jnp.float32) * W_SCALE}
    _L0_attn_in = _L0_attn_setup()

    def _L0_ffn_setup():
        import jax, jax.numpy as jnp
        import numpy as np
        D_MODEL = 128
        D_FF = 512
        N_EXPERTS = 8
        D_EXPERT = D_FF // N_EXPERTS
        TOP_K = 2
        LB_WEIGHT = 0.01
        B, S = (4, 256)

        def _top_k_softmax(logits, k):
            vals, _ = jax.lax.top_k(logits, k)
            thresh = vals[..., -1:]
            masked = jnp.where(logits >= thresh, logits, -jnp.inf)
            return jax.nn.softmax(masked, axis=-1)
        key = jax.random.key(seed)
        ks = jax.random.split(key, 8)
        x = jax.random.normal(ks[0], (B, S, D_MODEL), dtype=jnp.float32)
        w1 = jax.random.normal(ks[1], (N_EXPERTS, D_MODEL, D_EXPERT), dtype=jnp.float32) * (1.0 / np.sqrt(D_MODEL))
        b1 = jnp.zeros((N_EXPERTS, D_EXPERT), dtype=jnp.float32)
        w2 = jax.random.normal(ks[2], (N_EXPERTS, D_EXPERT, D_MODEL), dtype=jnp.float32) * (1.0 / np.sqrt(D_EXPERT))
        b2 = jnp.zeros((N_EXPERTS, D_MODEL), dtype=jnp.float32)
        centroids = jax.random.normal(ks[3], (N_EXPERTS, D_MODEL), dtype=jnp.float32) * 0.02
        w_route = jax.random.normal(ks[4], (N_EXPERTS, D_MODEL), dtype=jnp.float32) * (1.0 / np.sqrt(D_MODEL))
        return {'x': x, 'w1': w1, 'b1': b1, 'w2': w2, 'b2': b2, 'centroids': centroids, 'w_route': w_route}
    _L0_ffn_in = _L0_ffn_setup()

    def _L1_attn_setup():
        import jax, jax.numpy as jnp
        import numpy as np
        TTT_LR = 0.01
        LN_EPS = 1e-05
        key = jax.random.key(seed)
        ks = jax.random.split(key, 4)
        B, S, D, DS = (4, 256, 128, 64)
        sc = 1.0 / np.sqrt(D).astype(np.float32)
        return {'x': jax.random.normal(ks[0], (B, S, D), dtype=jnp.float32), 'Wk': jax.random.normal(ks[1], (DS, D), dtype=jnp.float32) * sc, 'bk': jnp.zeros((DS,), jnp.float32), 'Wv': jax.random.normal(ks[2], (D, D), dtype=jnp.float32) * sc, 'bv': jnp.zeros((D,), jnp.float32), 'Wq': jax.random.normal(ks[3], (DS, D), dtype=jnp.float32) * sc, 'bq': jnp.zeros((DS,), jnp.float32), 'gamma': jnp.ones((D,), jnp.float32), 'beta': jnp.zeros((D,), jnp.float32)}
    _L1_attn_in = _L1_attn_setup()

    def _L1_ffn_setup():
        import jax, jax.numpy as jnp
        import numpy as np
        key = jax.random.key(seed)
        kx, kw = jax.random.split(key)
        x = jax.random.normal(kx, (32, 512, 128), dtype=jnp.float32)
        weight = jax.random.normal(kw, (128, 128), dtype=jnp.float32) * 0.01
        return {'x': x, 'weight': weight}
    _L1_ffn_in = _L1_ffn_setup()
    _d = {'L0_attn_x': _L0_attn_in['x'], 'L0_attn_W_dq': _L0_attn_in['W_dq'], 'L0_attn_W_uq': _L0_attn_in['W_uq'], 'L0_attn_W_dkv': _L0_attn_in['W_dkv'], 'L0_attn_W_uk': _L0_attn_in['W_uk'], 'L0_attn_W_uv': _L0_attn_in['W_uv'], 'L0_attn_W_o': _L0_attn_in['W_o'], 'L0_ffn_w1': _L0_ffn_in['w1'], 'L0_ffn_b1': _L0_ffn_in['b1'], 'L0_ffn_w2': _L0_ffn_in['w2'], 'L0_ffn_b2': _L0_ffn_in['b2'], 'L0_ffn_centroids': _L0_ffn_in['centroids'], 'L0_ffn_w_route': _L0_ffn_in['w_route'], 'L1_attn_Wk': _L1_attn_in['Wk'], 'L1_attn_bk': _L1_attn_in['bk'], 'L1_attn_Wv': _L1_attn_in['Wv'], 'L1_attn_bv': _L1_attn_in['bv'], 'L1_attn_Wq': _L1_attn_in['Wq'], 'L1_attn_bq': _L1_attn_in['bq'], 'L1_attn_gamma': _L1_attn_in['gamma'], 'L1_attn_beta': _L1_attn_in['beta'], 'L1_ffn_weight': _L1_ffn_in['weight']}
    _x0 = _d['L0_attn_x']
    _d['L0_attn_x'] = jax.random.normal(jax.random.fold_in(jax.random.key(seed), 1), (8, 512, 128), dtype=_x0.dtype)
    del _x0
    return _d

def reference(L0_attn_x, L0_attn_W_dq, L0_attn_W_uq, L0_attn_W_dkv, L0_attn_W_uk, L0_attn_W_uv, L0_attn_W_o, L0_ffn_w1, L0_ffn_b1, L0_ffn_w2, L0_ffn_b2, L0_ffn_centroids, L0_ffn_w_route, L1_attn_Wk, L1_attn_bk, L1_attn_Wv, L1_attn_bv, L1_attn_Wq, L1_attn_bq, L1_attn_gamma, L1_attn_beta, L1_ffn_weight):

    def _L0_attn_ref(x, W_dq, W_uq, W_dkv, W_uk, W_uv, W_o):
        import jax, jax.numpy as jnp
        import numpy as np
        from math import sqrt
        N_HEAD = 16
        W_SCALE = 0.02

        def _reference_tuple_inner(x, W_dq, W_uq, W_dkv, W_uk, W_uv, W_o):
            B, T, C = x.shape
            nh = N_HEAD
            hs = C // nh
            n_kvl = W_dkv.shape[0]
            k_eff = (W_dq.T @ W_uq.T @ W_uk).reshape(nh, hs, n_kvl)
            v_eff = jnp.transpose((W_uv.T @ W_o.T).reshape(n_kvl, nh, hs), (1, 0, 2))
            c_kv = x @ W_dkv.T
            q = x @ W_dq.T @ W_uq.T
            q = q.reshape(B, T, nh, hs)
            q_lat = jnp.einsum('bqhd,hdl->bhql', q, k_eff)
            attn = jnp.einsum('bhql,bkl->bhqk', q_lat, c_kv) / sqrt(hs)
            causal = jnp.tril(jnp.ones((T, T), dtype=bool))
            attn = jnp.where(causal[None, None], attn, -jnp.inf)
            attn = jax.nn.softmax(attn, axis=-1)
            y_lat = jnp.einsum('bhqk,bkl->bhql', attn, c_kv)
            y = jnp.einsum('bhql,hld->bqhd', y_lat, v_eff).reshape(B, T, C)
            return (y, c_kv)
        return _reference_tuple_inner(x, W_dq, W_uq, W_dkv, W_uk, W_uv, W_o)[0]

    def _L0_ffn_ref(x, w1, b1, w2, b2, centroids, w_route):
        import jax, jax.numpy as jnp
        import numpy as np
        D_MODEL = 128
        D_FF = 512
        N_EXPERTS = 8
        D_EXPERT = D_FF // N_EXPERTS
        TOP_K = 2
        LB_WEIGHT = 0.01
        B, S = (4, 256)

        def _top_k_softmax(logits, k):
            vals, _ = jax.lax.top_k(logits, k)
            thresh = vals[..., -1:]
            masked = jnp.where(logits >= thresh, logits, -jnp.inf)
            return jax.nn.softmax(masked, axis=-1)
        eps = 1e-12
        x_norm = x / jnp.maximum(jnp.linalg.norm(x, axis=-1, keepdims=True), eps)
        c_norm = centroids / jnp.maximum(jnp.linalg.norm(centroids, axis=-1, keepdims=True), eps)
        cos_scores = jnp.einsum('bsd,ed->bse', x_norm, c_norm)
        route_scores = jnp.einsum('bsd,ed->bse', x, w_route)
        logits = cos_scores + route_scores
        gates = _top_k_softmax(logits, TOP_K)
        h = jax.nn.gelu(jnp.einsum('bsd,edh->bseh', x, w1) + b1, approximate=False)
        expert_out = jnp.einsum('bseh,ehd->bsed', h, w2) + b2
        out = jnp.einsum('bse,bsed->bsd', gates, expert_out)
        return out

    def _L1_attn_ref(x, Wk, bk, Wv, bv, Wq, bq, gamma, beta):
        import jax, jax.numpy as jnp
        import numpy as np
        TTT_LR = 0.01
        LN_EPS = 1e-05
        B, S, D = x.shape
        DS = Wk.shape[0]
        mu = jnp.mean(x, axis=-1, keepdims=True)
        var = jnp.mean((x - mu) ** 2, axis=-1, keepdims=True)
        h = (x - mu) * jax.lax.rsqrt(var + LN_EPS) * gamma + beta
        keys = jnp.einsum('bsd,ed->bse', h, Wk) + bk
        values = jnp.einsum('bsd,ed->bse', h, Wv) + bv
        queries = jnp.einsum('bsd,ed->bse', h, Wq) + bq

        def step(W, qkv):
            q_t, k_t, v_t = qkv
            y_t = jnp.einsum('bds,bs->bd', W, q_t)
            pred = jnp.einsum('bds,bs->bd', W, k_t)
            err = pred - v_t
            W = W - TTT_LR * err[:, :, None] * k_t[:, None, :]
            return (W, y_t)
        W0 = jnp.zeros((B, D, DS), x.dtype)
        qs = jnp.swapaxes(queries, 0, 1)
        ks_ = jnp.swapaxes(keys, 0, 1)
        vs = jnp.swapaxes(values, 0, 1)
        _, ys = jax.lax.scan(step, W0, (qs, ks_, vs))
        y = jnp.swapaxes(ys, 0, 1)
        return x + y

    def _L1_ffn_ref(x, weight):
        import jax, jax.numpy as jnp
        import numpy as np
        b_weight = jnp.sign(weight)
        return jnp.einsum('bsi,oi->bso', x, b_weight)
    x = L0_attn_x
    xn = _layernorm(x, axis=-1)
    s = _L0_attn_ref(xn, L0_attn_W_dq, L0_attn_W_uq, L0_attn_W_dkv, L0_attn_W_uk, L0_attn_W_uv, L0_attn_W_o)
    g = _silu(_L0_ffn_ref(xn, L0_ffn_w1, L0_ffn_b1, L0_ffn_w2, L0_ffn_b2, L0_ffn_centroids, L0_ffn_w_route))
    x = x + s * g
    xn = _layernorm(x, axis=-1)
    s = _L1_attn_ref(xn, L1_attn_Wk, L1_attn_bk, L1_attn_Wv, L1_attn_bv, L1_attn_Wq, L1_attn_bq, L1_attn_gamma, L1_attn_beta)
    g = _silu(_L1_ffn_ref(xn, L1_ffn_weight))
    x = x + s * g
    return x

_drawn_inputs = setup_inputs


def setup_inputs(seed=0):
    import zlib

    import numpy as np

    out = dict(_drawn_inputs(seed))
    spreads = {'L0_ffn_b1': (0.0, 0.8),
     'L0_ffn_b2': (0.0, 0.8),
     'L1_attn_bk': (0.0, 0.1),
     'L1_attn_bv': (0.0, 0.1),
     'L1_attn_bq': (0.0, 0.1),
     'L1_attn_gamma': (1.0, 0.2),
     'L1_attn_beta': (0.0, 0.1)}
    factors = {'L0_attn_W_dq': 8.0,
     'L0_attn_W_uq': 8.0,
     'L0_attn_W_dkv': 8.0,
     'L0_attn_W_uk': 8.0,
     'L0_attn_W_uv': 8.0,
     'L0_attn_W_o': 8.0,
     'L0_ffn_w1': 8.0,
     'L0_ffn_w2': 8.0,
     'L0_ffn_centroids': 8.0,
     'L0_ffn_w_route': 8.0}
    for name, (base, spread) in spreads.items():
        noise = np.random.default_rng([zlib.crc32(name.encode()), seed]).standard_normal(out[name].shape)
        drawn = base * np.exp(spread * noise) if base else spread * noise
        out[name] = jnp.asarray(drawn.astype(out[name].dtype))
    for name, factor in factors.items():
        out[name] = (out[name] * factor).astype(out[name].dtype)
    return out
```

```python
from contextlib import ExitStack

import concourse.bass as bass
from concourse import mybir

ALU = mybir.AluOpType
ACT = mybir.ActivationFunctionType
F32 = mybir.dt.float32
BF16 = mybir.dt.bfloat16
AX_X = mybir.AxisListType.X

P = 128
HEADS, HD = 16, 8
EXPERTS, HID = 8, 64
DS = 64
LR = 0.01
LN_EPS = 1e-5
NORM_EPS = 1e-12
NEG = -1e30
PARTS = 3
PAIRS = PARTS * PARTS * HD
MAXROW = 96
GROUPS, GH = 4, 4
UNITS = 10
LEVELS = 7

A_FILLS = 16
A_XNT, A_Q, A_K, A_LOGIT, A_GT, A_H, A_GB, A_OUT, A_V, A_MT = 0, 1, 2, 3, 4, 5, 9, 13, 14, 15
C0_FILLS, C1_FILLS = 25, 12
C0_XN2T, C0_KT, C0_VK, C0_GRAM = 0, 1, 2, 3
C1_HT, C1_QT, C1_VK, C1_KQ, C1_FFN, C1_Y = 0, 1, 2, 3, 10, 11


def c0_a(k):
    return 4 + 2 * (k - 1)


def c0_d(k):
    return 5 + 2 * (k - 1)


def c1_dt(k):
    return 4 + (k - 1)


def c0_r(c):
    return 17 + 3 * (c - 1)


def c0_u(c):
    return 15 if c == 0 else 18 + 3 * (c - 1)


def c0_s(c):
    return 16 if c == 0 else 19 + 3 * (c - 1)


PLAN = {
    (0, 0): ["ln2_stats", "ln1_stats"], (0, 1): ["ln2_norm"], (0, 2): ["ln3_stats", "ln1_norm"], (0, 3): ["xnt", "c_xn2t"],
    (0, 4): ["q", "ln3_norm"], (0, 5): ["k", "c_ht"], (0, 6): ["pv0", "c_kt"], (0, 7): ["logits", "c_qt"],
    (0, 8): ["c_vk"], (0, 9): ["pv1", "gates"],
    (1, 0): ["c_gram"], (1, 1): ["gt"], (1, 2): ["pv2"], (1, 3): ["lev_a1", "h0"], (1, 4): ["yt"], (1, 5): ["lev_d1", "h1"],
    (1, 6): ["pv0"], (1, 7): ["lev_a2", "h2"], (1, 8): ["lev_d2"], (1, 9): ["pv1", "h3", "gelu"],
    (2, 1): ["lev_a3", "gb0"], (2, 2): ["pv2"], (2, 3): ["lev_d3", "gb1"], (2, 4): ["yt"],
    (2, 5): ["lev_a4", "gb2"], (2, 6): ["pv0"], (2, 7): ["lev_d4", "gb3"], (2, 8): ["lev_a5"], (2, 9): ["pv1"],
    (3, 0): ["out"], (3, 1): ["lev_d5"], (3, 2): ["pv2"], (3, 3): ["lev_a6"], (3, 4): ["yt"], (3, 5): ["lev_d6"],
    (3, 6): ["pv0", "c_ffn"], (3, 7): ["c_u0"], (3, 8): ["c_y0"], (3, 9): ["pv1", "c_r1"],
    (4, 0): ["c_u1"], (4, 1): ["c_y1"], (4, 2): ["pv2", "c_r2"], (4, 3): ["c_u2", "v"], (4, 4): ["yt", "c_y2"],
    (4, 5): ["x1", "c_r3"], (4, 6): ["c_u3"], (4, 7): ["c_y3"], (4, 8): ["c_out"], (4, 9): ["m_rows"],
}

PLAN_NEXT = ("ln1_stats", "ln1_norm", "xnt", "q", "k", "v", "logits", "gates", "gt", "h0", "h1", "h2", "h3", "gelu",
             "gb0", "gb1", "gb2", "gb3", "out", "m_rows")
PLAN_CURRENT = ("pv0", "pv1", "pv2", "yt", "x1")


class Seq:

    def __init__(self, pair, c):
        self.pair, self.c, self.parity = pair, c, c % 2

    def count(self, per, k):
        if self.pair is None:
            return self.c * per + k + 1
        return self.pair * (2 * per) + (self.c * per + k + 1)

    def index(self):
        return self.c if self.pair is None else self.pair * 2 + self.c


def after(eng, sem, value):
    if not (isinstance(value, int) and value <= 1):
        eng.wait_ge(sem, value)


def two_layers(nc, x_in, W_dq, W_uq, W_dkv, W_uk, W_uv, W_o, w1_in, b1_in, w2_in, b2_in, cent_in, route_in,
               Wk_in, bk_in, Wv_in, bv_in, Wq_in, bq_in, gamma_in, beta_in, sign_in, out):
    SEQS, TOK, D = x_in.shape
    NT = TOK // P
    QL = W_dq.shape[0]
    KVL = W_dkv.shape[0]
    NC = EXPERTS * HID // P
    assert D == P and NT == 4 and SEQS % 2 == 0 and NC == 4

    with ExitStack() as ctx:
        def sb(name, shape, dt=F32):
            return ctx.enter_context(nc.sbuf_tensor(name, shape, dt))

        def psum(name, shape, dt=F32):
            return ctx.enter_context(nc.psum_tensor(name, shape, dt))

        def sem(name):
            return ctx.enter_context(nc.semaphore(name))

        ps_s = psum("ps_s", [P, 2, 512])
        ps_e = psum("ps_e", [P, 2, 512])
        ps_v = psum("ps_v", [P, 512])
        ps_a = psum("ps_a", [P, 512])
        ps_c0 = psum("ps_c0", [P, 512])
        ps_c1 = psum("ps_c1", [P, 512])

        ident = sb("ident", [P, P])
        identb = sb("identb", [P, P], BF16)
        negmask = sb("negmask", [P, P], BF16)
        lowmask0 = sb("lowmask0", [P, P])
        upmask = sb("upmask", [P, LEVELS, P])
        strict = sb("strict", [P, P])
        pick = sb("pick", [MAXROW, NC, P], BF16)
        halfpow = sb("halfpow", [P, 4])
        ones_row = sb("ones_row", [1, P])
        fence = sb("fence", [1, P])
        nat = {n: sb("nat_" + n, s) for n, s in (
            ("dq", [QL, P]), ("uq", [P, QL]), ("dkv", [KVL, P]), ("uk", [P, KVL]), ("uv", [P, KVL]), ("o", [P, P]),
            ("wk", [DS, P]), ("wv", [P, P]), ("wq", [DS, P]), ("sg", [P, P]), ("cent", [EXPERTS, P]))}
        uqT = sb("uqT", [QL, P])
        oT = sb("oT", [P, P])
        wqeT = sb("wqeT", [P, P])
        keffT = sb("keffT", [KVL, P])
        veff = sb("veff", [KVL, P])
        w_q = sb("w_q", [P, P])
        w_k = sb("w_k", [P, P])
        w_v = sb("w_v", [P, P])
        rw = sb("rw", [2 * EXPERTS, P])
        rwT = sb("rwT", [P, 2 * EXPERTS])
        cent_ss = sb("cent_ss", [EXPERTS, 1])
        cent_sq = sb("cent_sq", [EXPERTS, P])
        cent_rn = sb("cent_rn", [EXPERTS, 2])
        w1s = sb("w1s", [P, EXPERTS, HID])
        vecs = sb("vecs", [NC + 4, P])
        vecT = sb("vecT", [P, NC + 4])
        w2s = sb("w2s", [P, NC, P])
        b2f = sb("b2f", [MAXROW, P])
        b2r = sb("b2r", [MAXROW, 2, P])
        b2p = sb("b2p", [MAXROW, PARTS, P], BF16)
        wkT = sb("wkT", [P, P])
        wqT = sb("wqT", [P, P])
        wvk = sb("wvk", [P, 2 * P])
        sgT = sb("sgT", [P, P])
        bq_lr = sb("bq_lr", [P, 1])
        vkrow = sb("vkrow", [1, 2 * P])
        vkbias = sb("vkbias", [P, 2 * P])

        x_sb = [sb(f"x_sb{p}", [P, NT, P]) for p in range(2)]
        x1 = [sb(f"x1_{p}", [P, NT, P]) for p in range(2)]
        gate_out = [sb(f"gate_out{p}", [P, NT, P]) for p in range(2)]
        qst = [sb(f"qst{p}", [P, HEADS, TOK], BF16) for p in range(2)]
        kst = [sb(f"kst{p}", [P, HEADS, TOK], BF16) for p in range(2)]
        vaug = sb("vaug", [P, NT, HEADS, 32])
        stats = [sb(f"stats{n}", [P, NT, 6]) for n in range(3)]
        mv = [sb(f"mv{n}", [P, NT, 2]) for n in range(3)]
        vare = [sb(f"vare{n}", [P, NT]) for n in range(3)]
        rstd = [sb(f"rstd{n}", [P, NT]) for n in range(3)]
        xn = sb("xn", [P, NT, P])
        xnT = sb("xnT", [P, TOK])
        ss = sb("ss", [P, NT])
        ssm = sb("ssm", [P, NT])
        rn = sb("rn", [P, NT])
        parts = [sb(n, [P, PARTS, TOK], BF16) for n in ("qparts", "kparts")]
        rest = [xn[:, :, :].rearrange("p i d -> p (i d)"), sb("krest", [P, TOK])[:, :]]
        coss = sb("coss", [P, NT, EXPERTS])
        logit = sb("logit", [P, NT, EXPERTS])
        top8 = sb("top8", [P, NT, EXPERTS])
        keep = sb("keep", [P, NT, EXPERTS])
        dlt = sb("dlt", [P, NT, EXPERTS])
        ex = sb("ex", [P, NT, EXPERTS])
        gm = sb("gm", [P, NT, EXPERTS])
        gsum = sb("gsum", [P, NT])
        grec = sb("grec", [P, NT])
        gate = sb("gate", [P, NT, EXPERTS])
        grest = sb("grest", [P, NT, EXPERTS])
        gparts = sb("gparts", [P, NT, PARTS, EXPERTS], BF16)
        gT = sb("gT", [MAXROW, TOK], BF16)
        hid = sb("hid", [P, NC, TOK])
        tG = sb("tG", [P, TOK])
        cand = sb("cand", [P, NT, HEADS, 3])
        nm = sb("nm", [P, NT, HEADS])
        nmrest = sb("nmrest", [P, NT, HEADS])
        mparts = sb("mparts", [P, NT, PARTS, 32], BF16)
        mrow = sb("mrow", [PARTS * 32, TOK], BF16)
        prob = sb("prob", [P, UNITS, 512])
        yT = sb("yT", [P, TOK])
        rden = sb("rden", [P, NT, GH])
        att = sb("att", [P, NT, P])
        xn2 = sb("xn2", [P, NT, P])
        hn = sb("hn", [P, NT, P])
        gram = hn
        xn2T = sb("xn2T", [P, TOK])
        hT = sb("hT", [P, TOK])
        kT = sb("kT", [P, TOK])
        qT = sb("qT", [P, TOK])
        vk = sb("vk", [P, NT, 2 * P])
        kq = sb("kq", [P, NT, P])
        pair_up = [sb(f"pair_up{p}", [P, NT, P]) for p in range(2)]
        inv = [sb(f"inv{p}", [P, NT, P]) for p in range(2)]
        invT = [sb(f"invT{p}", [P, NT, P]) for p in range(2)]
        ablk = sb("ablk", [P, NT, P])
        rhs = sb("rhs", [P, P])
        u_sb = sb("u_sb", [P, P])
        state = sb("state", [P, P])
        tF = sb("tF", [P, TOK])
        sy = sb("sy", [P, NT, P])
        syg = sb("syg", [P, NT, P])
        out_sb = sb("out_sb", [P, NT, P])

        max_scratch = nc.dram_tensor("max_scratch", (PARTS * 32, TOK), BF16).ap()
        scratch = nc.dram_tensor("split_scratch", (2, PARTS, P, TOK), BF16).ap()

        names = """const_ready mask_step loaded prep_pe prep_out prep_out2 prep_sign stack_zeroed
        x_loaded scratch_written stack_loaded mscratch_written mrow_loaded stored
        a_filled a_emptied c0_filled c0_emptied c1_filled c1_emptied pv_used yt_filled v_emptied
        s_filled s_emptied e_filled e_emptied
        stats0 stats1 stats2 mv0 mv1 mv2 var0 var1 var2 rstd0 rstd1 rstd2 norm0 norm1 norm2
        ss_ready ssm_ready rn_ready hi_ready mid_ready parts_ready
        cos_ready top_ready keep_ready dlt_ready ex_ready gm_ready gsum_ready grec_ready gate_ready
        ghi_ready grest_ready gmid_ready gparts_ready gelu_ready tg_ready
        nm_ready mhi_ready mrest_ready mmid_ready mparts_ready
        rden_ready attg_ready x1_ready
        dtmp_ready inv1_ready pair_ready tf_ready syg_ready out_ready""".split()
        S = {n: sem(n) for n in names}


        block = ctx.enter_context(nc.Block())

        fences = [0]

        def settled(eng, sem, value):
            eng.wait_ge(sem, value)
            if not isinstance(value, int):
                fences[0] += 1
                spot = fence[0:1, fences[0]:fences[0] + 1]
                eng.tensor_tensor(spot, ident[0:1, 0:1], ident[0:1, 0:1], ALU.mult)

        def bcast(ap, axis, n):
            ap = ap.unsqueeze(axis)
            shape = list(ap.shape)
            shape[axis] = n
            return ap.to_broadcast(shape)

        def run(eng, pieces, unit):
            def iteration(nxt, cur, prev):
                if "start" in pieces and nxt is not None:
                    pieces["start"](nxt)
                for step in range(GROUPS + 1):
                    for u in range(UNITS):
                        unit(cur if step < GROUPS else None, step, nxt if step > 0 else None, step - 1, u)
                        for name in PLAN.get((step, u), []):
                            of = nxt if name in PLAN_NEXT else cur if name in PLAN_CURRENT else prev
                            if of is not None and name in pieces:
                                if name in ("pv0", "pv1"):
                                    pieces[name](of, step if u >= 5 else step - 1)
                                elif name in ("pv2", "yt"):
                                    pieces[name](of, step - 1)
                                else:
                                    pieces[name](of)

            def last(prev):
                for step in range(GROUPS + 1):
                    for u in range(UNITS):
                        for name in PLAN.get((step, u), []):
                            if name not in PLAN_NEXT + PLAN_CURRENT and name in pieces:
                                pieces[name](prev)

            def first(nxt):
                iteration(nxt, None, None)

            first(Seq(None, 0))
            iteration(Seq(None, 1), Seq(None, 0), None)
            with eng.Fori(0, (SEQS - 2) // 2) as pair:
                for odd in range(2):
                    iteration(Seq(pair, 2 + odd), Seq(pair, 1 + odd), Seq(pair, odd))
            iteration(None, Seq(None, SEQS - 1), Seq(None, SEQS - 2))
            last(Seq(None, SEQS - 1))

        x_view = x_in.rearrange("b (i p) d -> b p i d", p=P)
        out_view = out.rearrange("b (i p) d -> b p i d", p=P)

        def row(v):
            return v.rearrange("(o d) -> o d", o=1)

        loads = [
            (nat["dq"][:, :], W_dq), (nat["uq"][:, :], W_uq), (nat["dkv"][:, :], W_dkv), (nat["uk"][:, :], W_uk),
            (nat["uv"][:, :], W_uv), (nat["o"][:, :], W_o), (nat["cent"][:, :], cent_in), (rw[EXPERTS:2 * EXPERTS, :], route_in),
            (w1s[:, :, :], w1_in.rearrange("e d f -> d e f")),
            (w2s[:, :, :], w2_in.rearrange("(c a) f d -> (a f) c d", a=2)),
            (nat["wk"][:, :], Wk_in), (nat["wv"][:, :], Wv_in), (nat["wq"][:, :], Wq_in), (nat["sg"][:, :], sign_in),
        ]
        zero_loads = [(b2f[EXPERTS * r:EXPERTS * (r + 1), :], b2_in) for r in range(PARTS)] + [
            (vecs[0:NC, :], b1_in.rearrange("(c a) f -> c (a f)", a=2)), (vecs[NC:NC + 1, :], row(gamma_in)),
            (vecs[NC + 1:NC + 2, :], row(beta_in)), (vecs[NC + 2:NC + 3, 0:DS], row(bk_in)), (vecs[NC + 3:NC + 4, 0:DS], row(bq_in)),
            (vkrow[:, 0:P], row(bv_in)), (vkrow[:, P:P + DS], row(bk_in))]
        LOADED = 16 * (len(loads) + len(zero_loads))

        @block.sync
        def _(sp):
            for dst, src in loads:
                sp.dma_start(dst, src).then_inc(S["loaded"], 16)
            sp.wait_ge(S["stack_zeroed"], 1)
            for dst, src in zero_loads:
                sp.dma_start(dst, src).then_inc(S["loaded"], 16)

            def start(b):
                after(sp, S["x1_ready"], b.count(1, -1))
                sp.dma_start(x_sb[b.parity][:, :, :], x_view[b.index()] if b.pair is None else
                             x_view[bass.ds(b.index(), 1)].rearrange("o p i d -> (o p) i d")).then_inc(S["x_loaded"], 16)

            def k(b):
                for n in range(2):
                    after(sp, S["stack_loaded"], b.count(192, 0))
                    sp.wait_ge(S["parts_ready"], b.count(2, n + 1))
                    sp.dma_start(scratch[n].rearrange("r s q -> s r q"), parts[n][:, :, :]).then_inc(S["scratch_written"], 16)
                after(sp, S["e_filled"], b.count(GROUPS * UNITS, -GROUPS * UNITS))
                sp.wait_ge(S["scratch_written"], b.count(32, 32))
                q_rows = scratch[0].rearrange("r (d h) q -> (r d) (h q)", d=HD)
                k_rows = scratch[1].rearrange("r (d h) q -> (r d) (h q)", d=HD)
                n3 = PARTS * HD
                for s in range(PARTS):
                    sp.dma_start(qst[b.parity][n3 * s:n3 * s + n3, :, :].rearrange("p h q -> p (h q)"), q_rows,
                                 max_dma_last_dim=4096).then_inc(S["stack_loaded"], 16)
                    for r in range(PARTS):
                        lo = n3 * s + HD * r
                        sp.dma_start(kst[b.parity][lo:lo + HD, :, :].rearrange("p h q -> p (h q)"), k_rows[HD * s:HD * s + HD, :],
                                     max_dma_last_dim=4096).then_inc(S["stack_loaded"], 16)

            def m_rows(b):
                sp.wait_ge(S["a_emptied"], b.count(A_FILLS, A_MT + 1))
                sp.dma_start(max_scratch, mrow[:, :]).then_inc(S["mscratch_written"], 16)
                sp.wait_ge(S["mscratch_written"], b.count(16, 16))
                sp.dma_start(qst[b.parity][MAXROW:MAXROW + PARTS, :, :].rearrange("r h q -> r (h q)"),
                             max_scratch.rearrange("(r h) q -> r h q", r=PARTS)[:, 0:HEADS, :].rearrange("r h q -> r (h q)"), max_dma_last_dim=2048).then_inc(S["mrow_loaded"], 16)

            def c_out(b):
                sp.wait_ge(S["out_ready"], b.count(1, 1))
                sp.dma_start(out_view[b.index()] if b.pair is None else
                             out_view[bass.ds(b.index(), 1)].rearrange("o p i d -> (o p) i d"), out_sb[:, :, :]).then_inc(S["stored"], 16)

            run(sp, {"start": start, "k": k, "m_rows": m_rows, "c_out": c_out}, lambda *a: None)
            sp.wait_ge(S["stored"], 16 * SEQS + 1)

        @block.gpsimd
        def _(pool):
            g = nc.gpsimd
            steps = [0]

            def chain(ins):
                steps[0] += 1
                ins.then_inc(S["mask_step"], 1)
                pool.wait_ge(S["mask_step"], steps[0])

            chain(g.memset(b2f[:, :], 0.0))
            chain(g.memset(vecs[:, :], 0.0))
            chain(g.memset(vkrow[:, :], 0.0))
            for p in range(2):
                chain(g.memset(qst[p][64:P, :, :], 0.0))
                chain(g.memset(kst[p][64:P, :, :], 0.0))
                chain(g.memset(kst[p][MAXROW:MAXROW + PARTS, :, :], 1.0))
            g.memset(halfpow[:, :], -0.5).then_inc(S["stack_zeroed"], 1)
            chain(g.memset(ident[:, :], 0.0))
            chain(g.affine_select(out=ident[:, :], in_=ident[:, :], compare_op=ALU.not_equal, fill=1.0, base=0,
                                  pattern=[[-1, P]], channel_multiplier=1))
            chain(g.tensor_copy(identb[:, :], ident[:, :]))
            chain(g.memset(ones_row[:, :], 1.0))
            g.memset(state[:, :], 0.0).then_inc(S["const_ready"], 1)
            chain(g.memset(vaug[:, :, :, :], 0.0))
            chain(g.memset(vaug[:, :, :, HD:HD + 1], 1.0))
            chain(g.memset(cand[:, :, :, :], -3e38))
            chain(g.memset(gT[:, :], 0.0))
            chain(g.memset(mparts[:, :, :, :], 0.0))
            chain(g.memset(pick[:, :, :], 0.0))
            for r in range(PARTS):
                chain(g.affine_select(out=pick[:, :, :].rearrange("p c (a f) -> p c a f", a=2),
                                      in_=pick[:, :, :].rearrange("p c (a f) -> p c a f", a=2),
                                      compare_op=ALU.not_equal, fill=1.0, base=-EXPERTS * r,
                                      pattern=[[-2, NC], [-1, 2], [0, HID]], channel_multiplier=1))
            chain(g.memset(negmask[:, :], 0.0))
            chain(g.affine_select(out=negmask[:, :], in_=negmask[:, :], compare_op=ALU.is_ge, fill=NEG, base=0,
                                  pattern=[[-1, P]], channel_multiplier=1))
            chain(g.memset(strict[:, :], 1.0))
            chain(g.affine_select(out=strict[:, :], in_=strict[:, :], compare_op=ALU.is_gt, fill=0.0, base=0,
                                  pattern=[[1, P]], channel_multiplier=-1))
            chain(g.memset(lowmask0[:, :], 0.0))
            low = lowmask0[:, :].rearrange("p (n a) -> p n a", a=2)[:, :, 0]
            chain(g.memset(low, LR))
            chain(g.affine_select(out=low, in_=low, compare_op=ALU.is_equal, fill=0.0, base=-1,
                                  pattern=[[-2, P // 2]], channel_multiplier=1))
            chain(g.memset(upmask[:, :, :], 0.0))
            for lv in range(LEVELS):
                s = 1 << lv
                nb = P // (2 * s)
                half = upmask[:, lv, :].rearrange("p (n a w) -> p n a w", a=2, w=s)[:, :, 1, :]
                chain(g.memset(half, LR))
                chain(g.affine_select(out=half, in_=half, compare_op=ALU.is_ge, fill=0.0, base=0,
                                      pattern=[[-2 * s, nb], [0, s]], channel_multiplier=1))
                chain(g.affine_select(out=half, in_=half, compare_op=ALU.is_ge, fill=0.0, base=s - 1,
                                      pattern=[[2 * s, nb], [0, s]], channel_multiplier=-1))
            g.memset(wkT[:, DS:P], 0.0).then_inc(S["const_ready"], 1)
            g.memset(wqT[:, DS:P], 0.0).then_inc(S["const_ready"], 1)
            g.memset(wvk[:, P + DS:2 * P], 0.0).then_inc(S["const_ready"], 1)
            pool.wait_ge(S["ss_ready"], 1)
            chain(g.tensor_scalar(cent_rn[:, 0:1], cent_ss[:, :], NORM_EPS * NORM_EPS, None, ALU.max))
            g.tensor_tensor(cent_rn[:, 1:2], cent_rn[:, 0:1], halfpow[0:EXPERTS, 0:1], ALU.pow).then_inc(S["rn_ready"], 1)

            def ln_rstd(n, b):
                settled(pool, S[f"mv{n}"], b.count(NT, NT))
                g.tensor_scalar(vare[n][:, :], mv[n][:, :, 1], LN_EPS, None, ALU.add).then_inc(S[f"var{n}"], 1)
                pool.wait_ge(S[f"var{n}"], b.count(1, 1))
                g.tensor_tensor(rstd[n][:, :], vare[n][:, :], halfpow[:, :], ALU.pow).then_inc(S[f"rstd{n}"], 1)

            def split_rest(n, b):
                settled(pool, S["a_emptied"], b.count(A_FILLS, A_Q + n + 1))
                g.tensor_copy(parts[n][:, 1, :], rest[n]).then_inc(S["mid_ready"], 1)
                pool.wait_ge(S["mid_ready"], b.count(2, n + 1))
                g.tensor_tensor(parts[n][:, 2, :], rest[n], parts[n][:, 1, :], ALU.subtract).then_inc(S["parts_ready"], 1)

            def token_norms(b):
                settled(pool, S["ss_ready"], b.count(NT, NT))
                g.tensor_scalar(ssm[:, :], ss[:, :], NORM_EPS * NORM_EPS, None, ALU.max).then_inc(S["ssm_ready"], 1)
                pool.wait_ge(S["ssm_ready"], b.count(1, 1))
                g.tensor_tensor(rn[:, :], ssm[:, :], halfpow[:, :], ALU.pow).then_inc(S["rn_ready"], 1)

            def gates(b):
                settled(pool, S["gate_ready"], b.count(1, 1))
                g.tensor_copy(gparts[:, :, 0, :], gate[:, :, :]).then_inc(S["ghi_ready"], 1)
                pool.wait_ge(S["ghi_ready"], b.count(1, 1))
                g.tensor_tensor(grest[:, :, :], gate[:, :, :], gparts[:, :, 0, :], ALU.subtract).then_inc(S["grest_ready"], 1)
                settled(pool, S["grest_ready"], b.count(1, 1))
                g.tensor_copy(gparts[:, :, 1, :], grest[:, :, :]).then_inc(S["gmid_ready"], 1)
                pool.wait_ge(S["gmid_ready"], b.count(1, 1))
                g.tensor_tensor(gparts[:, :, 2, :], grest[:, :, :], gparts[:, :, 1, :], ALU.subtract).then_inc(S["gparts_ready"], 1)

            def m_rows(b):
                settled(pool, S["nm_ready"], b.count(1, 1))
                g.tensor_copy(mparts[:, :, 0, 0:HEADS], nm[:, :, :]).then_inc(S["mhi_ready"], 1)
                pool.wait_ge(S["mhi_ready"], b.count(1, 1))
                g.tensor_tensor(nmrest[:, :, :], nm[:, :, :], mparts[:, :, 0, 0:HEADS], ALU.subtract).then_inc(S["mrest_ready"], 1)
                settled(pool, S["mrest_ready"], b.count(1, 1))
                g.tensor_copy(mparts[:, :, 1, 0:HEADS], nmrest[:, :, :]).then_inc(S["mmid_ready"], 1)
                pool.wait_ge(S["mmid_ready"], b.count(1, 1))
                g.tensor_tensor(mparts[:, :, 2, 0:HEADS], nmrest[:, :, :], mparts[:, :, 1, 0:HEADS], ALU.subtract).then_inc(S["mparts_ready"], 1)

            def x1_piece(b):
                p = b.parity
                pool.wait_ge(S["v_emptied"], b.count(2 * GROUPS, 2 * GROUPS))
                g.tensor_tensor(att[:, :, :], att[:, :, :], gate_out[p][:, :, :], ALU.mult).then_inc(S["attg_ready"], 1)
                pool.wait_ge(S["attg_ready"], b.count(1, 1))
                after(pool, S["out_ready"], b.count(1, -1))
                g.tensor_tensor(x1[p][:, :, :], x_sb[p][:, :, :], att[:, :, :], ALU.add).then_inc(S["x1_ready"], 1)

            def c_gram(b):
                eye = bcast(ident[:, :], 1, NT)
                pool.wait_ge(S["c0_emptied"], b.count(C0_FILLS, C0_GRAM + 1))
                for n, (mask, dst) in enumerate(((lowmask0[:, :], inv[1]), (upmask[:, 0, :], invT[1]))):
                    g.tensor_tensor((sy, syg)[n][:, :, :], gram[:, :, :], bcast(mask, 1, NT), ALU.mult).then_inc(S["dtmp_ready"], 1)
                    pool.wait_ge(S["dtmp_ready"], b.count(2, n + 1))
                    g.tensor_tensor(dst[:, :, :], eye, (sy, syg)[n][:, :, :], ALU.subtract).then_inc(S["inv1_ready"], 1)
                pairs(b, 1)
                pairs(b, 2)

            def pairs(b, lv):
                if lv < LEVELS:
                    if lv > 2:
                        pool.wait_ge(S["c0_filled"], b.count(C0_FILLS, c0_a(lv - 2) + 1))
                    g.tensor_tensor(pair_up[lv % 2][:, :, :], gram[:, :, :], bcast(upmask[:, lv, :], 1, NT), ALU.mult)\
                        .then_inc(S["pair_ready"], 1)

            def c_out(b):
                pool.wait_ge(S["c1_emptied"], b.count(C1_FILLS, C1_Y + 1))
                g.tensor_tensor(syg[:, :, :], sy[:, :, :], tF[:, :].rearrange("p (i d) -> p i d", i=NT), ALU.mult)\
                    .then_inc(S["syg_ready"], 1)
                pool.wait_ge(S["syg_ready"], b.count(1, 1))
                after(pool, S["stored"], b.count(16, 0))
                g.tensor_tensor(out_sb[:, :, :], x1[b.parity][:, :, :], syg[:, :, :], ALU.add).then_inc(S["out_ready"], 1)

            levels = {f"lev_d{lv}": lambda b, lv=lv: pairs(b, lv + 2) for lv in range(1, LEVELS)}
            run(pool, levels | {"ln1_norm": lambda b: ln_rstd(0, b), "ln2_norm": lambda b: ln_rstd(1, b), "ln3_norm": lambda b: ln_rstd(2, b),
                       "q": lambda b: split_rest(0, b), "k": lambda b: split_rest(1, b), "xnt": token_norms, "gates": gates,
                       "m_rows": m_rows, "x1": x1_piece, "c_gram": c_gram, "c_out": c_out}, lambda *a: None)

        @block.tensor
        def _(pe):
            mm, tr = nc.tensor.matmul, nc.tensor.transpose
            pe.wait_ge(S["const_ready"], 1)
            pe.wait_ge(S["loaded"], LOADED)
            done = [0]

            def prep(ins, need=None):
                done[0] += 1
                ins.then_inc(S["prep_pe"], 1)

            def ready(n):
                pe.wait_ge(S["prep_out"], n)

            prep(tr(ps_a[0:QL, 0:P], nat["uq"][:, :], ident[:, :]))
            prep(tr(ps_c0[:, 0:P], nat["o"][:, :], ident[:, :]))
            ready(2)
            prep(mm(ps_c1[:, 0:P], uqT[:, :], nat["dq"][:, :], start=True, stop=True))
            prep(mm(ps_a[:, 0:P], nat["dq"][:, :], uqT[:, :], start=True, stop=True))
            prep(mm(ps_c0[0:KVL, 0:P], nat["uv"][:, :], oT[:, :], start=True, stop=True))
            ready(5)
            prep(mm(ps_c1[0:KVL, 0:P], nat["uk"][:, :], wqeT[:, :], start=True, stop=True))
            prep(mm(ps_c0[:, 0:P], nat["dkv"][:, :], veff[:, :], start=True, stop=True))
            ready(7)
            prep(mm(ps_a[:, 0:P], nat["dkv"][:, :], keffT[:, :], start=True, stop=True))
            prep(tr(ps_c0[:, 0:DS], nat["wk"][:, :], ident[0:DS, 0:DS]))
            prep(tr(ps_c1[:, 0:DS], nat["wq"][:, :], ident[0:DS, 0:DS]))
            prep(tr(ps_v[:, 0:NC + 4], vecs[:, :], ident[0:NC + 4, 0:NC + 4]))
            ready(12)
            prep(tr(ps_a[:, 0:P], nat["wv"][:, :], ident[:, :]))
            prep(tr(ps_c0[:, 0:P], nat["sg"][:, :], ident[:, :]))
            prep(mm(ps_c1[:, 0:2 * P], ones_row[:, :], vkrow[:, :], start=True, stop=True))
            ready(17)
            prep(tr(ps_a[:, 0:2 * EXPERTS], rw[:, :], ident[0:2 * EXPERTS, 0:2 * EXPERTS]))
            ready(PREP_OUT)
            pe.wait_ge(S["const_ready"], 4)

            def a_fill(b, n):
                after(pe, S["a_emptied"], b.count(A_FILLS, n))

            def c0_fill(b, n):
                after(pe, S["c0_emptied"], b.count(C0_FILLS, n))

            def c1_fill(b, n):
                after(pe, S["c1_emptied"], b.count(C1_FILLS, n))

            def tok(i):
                return slice(i * P, (i + 1) * P)

            def xnt(b):
                a_fill(b, A_XNT)
                pe.wait_ge(S["norm0"], b.count(NT, NT))
                for i in range(NT):
                    last = tr(ps_a[:, tok(i)], xn[:, i, :], ident[:, :])
                last.then_inc(S["a_filled"], 1)

            def qk(b, n):
                a_fill(b, A_Q + n)
                mm(ps_a[:, :], (w_q, w_k)[n][:, :], xnT[:, :], start=True, stop=True).then_inc(S["a_filled"], 1)

            def v(b):
                a_fill(b, A_V)
                for i in range(NT):
                    last = mm(ps_a[:, tok(i)], xnT[:, tok(i)], w_v[:, :], start=True, stop=True)
                last.then_inc(S["a_filled"], 1)

            def logits(b):
                a_fill(b, A_LOGIT)
                for i in range(NT):
                    last = mm(ps_a[:, 16 * i:16 * i + 16], xnT[:, tok(i)], rwT[:, :], start=True, stop=True)
                last.then_inc(S["a_filled"], 1)

            def gt(b):
                a_fill(b, A_GT)
                pe.wait_ge(S["gparts_ready"], b.count(1, 1))
                for i in range(NT):
                    last = tr(ps_a[:, :].bitcast(BF16)[0:PARTS * EXPERTS, tok(i)],
                              gparts[:, i, :, :].rearrange("p r e -> p (r e)"), identb[:, :])
                last.then_inc(S["a_filled"], 1)

            def h(b, c):
                a_fill(b, A_H + c)
                mm(ps_a[:, :], w1s[:, 2 * c:2 * c + 2, :].rearrange("p e f -> p (e f)"), xnT[:, :], start=True, stop=True)\
                    .then_inc(S["a_filled"], 1)

            def gb(b, c):
                a_fill(b, A_GB + c)
                mm(ps_a[:, :], pick[:, c, :], gT[:, :], start=True, stop=True).then_inc(S["a_filled"], 1)

            def out_piece(b):
                a_fill(b, A_OUT)
                for i in range(NT):
                    for c in range(NC):
                        mm(ps_a[:, tok(i)], hid[:, c, tok(i)], w2s[:, c, :], start=(i == 0 and c == 0), stop=False,
                           skip_group_check=True)
                    for r in range(PARTS):
                        last = mm(ps_a[:, tok(i)], gT[:, tok(i)], b2p[:, r, :], start=False, stop=(r == PARTS - 1),
                                  skip_group_check=True)
                last.then_inc(S["a_filled"], 1)

            def m_rows(b):
                a_fill(b, A_MT)
                pe.wait_ge(S["mparts_ready"], b.count(1, 1))
                for i in range(NT):
                    last = tr(ps_a[:, :].bitcast(BF16)[0:PARTS * 32, tok(i)],
                              mparts[:, i, :, :].rearrange("p r h -> p (r h)"), identb[:, :])
                last.then_inc(S["a_filled"], 1)

            def unit(cur, grp, nxt, mgrp, u):
                if cur is not None:
                    e_unit(cur, grp, u)
                if nxt is not None:
                    s_unit(nxt, mgrp, u)

            def e_unit(b, grp, u):
                q, k = qst[b.parity], kst[b.parity]
                bank = u % 2
                after(pe, S["e_emptied"], b.count(GROUPS * UNITS, UNITS * grp + u - 1))
                if grp == 0 and u == 0:
                    pe.wait_ge(S["stack_loaded"], b.count(192, 192))
                    pe.wait_ge(S["mrow_loaded"], b.count(16, 16))
                todo = [(u, 0, 0)] if u < 4 else [(u - 4, 1, 0), (u - 4, 3, 384)] if u < 8 else \
                    [(2 * (u - 8), 2, 0), (2 * (u - 8) + 1, 2, 256)]
                if u < 4:
                    diag = ps_e[:, bank, 0:P].rearrange("p (a c) -> p a c", a=1)
                else:
                    step = 384 if u < 8 else 256
                    diag = ps_e[:, bank, :].rearrange("p (a c) -> p a c", c=P)[:, 0:step // P + 1:step // P, :]
                mm(diag, negmask[:, :], bcast(identb[:, :], 1, len(todo)), start=True, stop=False, skip_group_check=True)
                for hh, j, at in todo:
                    hd = GH * grp + hh
                    last = mm(ps_e[:, bank, at:at + TOK - P * j], k[:, hd, tok(j)], q[:, hd, P * j:TOK],
                              start=False, stop=True, skip_group_check=True)
                last.then_inc(S["e_filled"], 1)

            def s_unit(b, grp, u):
                q, k = qst[b.parity], kst[b.parity]
                bank = u % 2
                after(pe, S["s_emptied"], b.count(GROUPS * UNITS, UNITS * grp + u - 1))
                if grp == 0 and u == 0:
                    pe.wait_ge(S["stack_loaded"], b.count(192, 192))
                diag = u < NT
                if diag:
                    mm(ps_s[:, bank, :].rearrange("p (a c) -> p a c", a=GH), identb[:, :], bcast(negmask[:, :], 1, GH),
                       start=True, stop=False, skip_group_check=True)
                i, keys, hds = S_UNIT[u]
                for n, hh in enumerate(hds):
                    w = keys[1] - keys[0]
                    hd = GH * grp + hh
                    last = mm(ps_s[:, bank, w * n:w * (n + 1)], q[0:MAXROW, hd, tok(i)], k[0:MAXROW, hd, keys[0]:keys[1]],
                              start=(n == 0 and not diag), stop=True, skip_group_check=True)
                last.then_inc(S["s_filled"], 1)

            def pv(b, grp, piece):
                if piece == 0:
                    after(pe, S["v_emptied"], b.count(2 * GROUPS, 2 * grp))
                    if grp == 0:
                        pe.wait_ge(S["a_emptied"], b.count(A_FILLS, A_V + 1))
                pe.wait_ge(S["e_emptied"], b.count(GROUPS * UNITS, UNITS * grp + (4, 8, 10)[piece]))
                for j, u0, at in (((0, 0, 0),), ((1, 4, 0), (3, 4, 384)), ((2, 8, 0),))[piece]:
                    for hh in range(GH):
                        u, o = (u0 + hh, at) if j != 2 else (u0 + hh // 2, 256 * (hh % 2))
                        last = mm(ps_v[32 * hh:32 * hh + 32, P * j:TOK], vaug[:, j, GH * grp + hh, :],
                                  prob[:, u, o:o + TOK - P * j], start=(j == 0), stop=(j == 2), skip_group_check=True)
                last.then_inc(S["pv_used"], 1)

            def yt(b, grp):
                pe.wait_ge(S["v_emptied"], b.count(2 * GROUPS, 2 * grp + 1))
                for i in range(NT):
                    last = tr(ps_v[:, tok(i)], yT[:, tok(i)], ident[:, :])
                last.then_inc(S["yt_filled"], 1)

            def c_xn2t(b):
                c0_fill(b, C0_XN2T)
                pe.wait_ge(S["norm1"], b.count(NT, NT))
                for i in range(NT):
                    last = tr(ps_c0[:, tok(i)], xn2[:, i, :], ident[:, :])
                last.then_inc(S["c0_filled"], 1)

            def c_ht(b):
                c1_fill(b, C1_HT)
                pe.wait_ge(S["norm2"], b.count(NT, NT))
                for i in range(NT):
                    last = tr(ps_c1[:, tok(i)], hn[:, i, :], ident[:, :])
                last.then_inc(S["c1_filled"], 1)

            def c_kt(b):
                c0_fill(b, C0_KT)
                pe.wait_ge(S["c1_emptied"], b.count(C1_FILLS, C1_HT + 1))
                mm(ps_c0[:, :], wkT[:, :], hT[:, :], start=True, stop=True).then_inc(S["c0_filled"], 1)

            def c_qt(b):
                c1_fill(b, C1_QT)
                mm(ps_c1[:, :], wqT[:, :], hT[:, :], start=True, stop=True).then_inc(S["c1_filled"], 1)

            def c_vk(b):
                for bank, fill, filled, n in ((ps_c0, c0_fill, "c0_filled", C0_VK), (ps_c1, c1_fill, "c1_filled", C1_VK)):
                    fill(b, n)
                    for m in range(2):
                        i = m if bank is ps_c0 else 2 + m
                        last = mm(bank[:, 2 * P * m:2 * P * (m + 1)], hT[:, tok(i)], wvk[:, :], start=True, stop=True)
                    last.then_inc(S[filled], 1)

            def c_gram(b):
                c0_fill(b, C0_GRAM)
                for i in range(NT):
                    last = mm(ps_c0[:, tok(i)], kT[:, tok(i)], kT[:, tok(i)], start=True, stop=True)
                last.then_inc(S["c0_filled"], 1)
                c1_fill(b, C1_KQ)
                for i in range(NT):
                    last = mm(ps_c1[:, tok(i)], kT[:, tok(i)], qT[:, tok(i)], start=True, stop=True)
                last.then_inc(S["c1_filled"], 1)

            def lev_a(b, lv):
                c0_fill(b, c0_a(lv))
                pe.wait_ge(S["pair_ready"], b.count(LEVELS - 1, lv))
                if lv == 1:
                    pe.wait_ge(S["inv1_ready"], b.count(2, 2))
                for i in range(NT):
                    last = mm(ps_c0[:, tok(i)], pair_up[lv % 2][:, i, :], inv[lv % 2][:, i, :], start=True, stop=True)
                last.then_inc(S["c0_filled"], 1)

            def lev_d(b, lv):
                c1_fill(b, c1_dt(lv))
                pe.wait_ge(S["c0_emptied"], b.count(C0_FILLS, c0_a(lv) + 1))
                for i in range(NT):
                    last = mm(ps_c1[:, tok(i)], ablk[:, i, :], invT[lv % 2][:, i, :], start=True, stop=True)
                last.then_inc(S["c1_filled"], 1)
                if lv < LEVELS - 1:
                    c0_fill(b, c0_d(lv))
                    for i in range(NT):
                        last = mm(ps_c0[:, tok(i)], invT[lv % 2][:, i, :], ablk[:, i, :], start=True, stop=True)
                    last.then_inc(S["c0_filled"], 1)

            def c_ffn(b):
                c1_fill(b, C1_FFN)
                for i in range(NT):
                    last = mm(ps_c1[:, tok(i)], xn2T[:, tok(i)], sgT[:, :], start=True, stop=True)
                last.then_inc(S["c1_filled"], 1)

            def c_r(b, c):
                c0_fill(b, c0_r(c))
                mm(ps_c0[:, 0:P], kT[:, tok(c)], state[:, :], start=True, stop=True).then_inc(S["c0_filled"], 1)

            def c_u(b, c):
                c0_fill(b, c0_u(c))
                if c == 0:
                    pe.wait_ge(S["c1_emptied"], b.count(C1_FILLS, c1_dt(LEVELS - 1) + 1))
                mm(ps_c0[:, 0:P], invT[LEVELS % 2][:, c, :], vk[:, 0, 0:P] if c == 0 else rhs[:, :], start=True, stop=True)\
                    .then_inc(S["c0_filled"], 1)

            def c_y(b, c):
                if c == 0:
                    c1_fill(b, C1_Y)
                pe.wait_ge(S["c0_emptied"], b.count(C0_FILLS, c0_u(c) + 1))
                if c > 0:
                    mm(ps_c1[:, tok(c)], qT[:, tok(c)], state[:, :], start=False, stop=False, skip_group_check=True)
                last = mm(ps_c1[:, tok(c)], kq[:, c, :], u_sb[:, :], start=(c == 0), stop=True, skip_group_check=True)
                if c == NT - 1:
                    last.then_inc(S["c1_filled"], 1)
                else:
                    mm(ps_c0[:, 0:P], vk[:, c, P:2 * P], u_sb[:, :], start=True, stop=True).then_inc(S["c0_filled"], 1)

            pieces = {"xnt": xnt, "q": lambda b: qk(b, 0), "k": lambda b: qk(b, 1), "v": v, "logits": logits, "gt": gt,
                      "out": out_piece, "m_rows": m_rows, "pv0": lambda b, grp: pv(b, grp, 0), "pv1": lambda b, grp: pv(b, grp, 1), "pv2": lambda b, grp: pv(b, grp, 2), "yt": yt, "c_xn2t": c_xn2t, "c_ht": c_ht, "c_kt": c_kt,
                      "c_qt": c_qt, "c_vk": c_vk, "c_gram": c_gram, "c_ffn": c_ffn}
            for c in range(NC):
                pieces[f"h{c}"] = lambda b, c=c: h(b, c)
                pieces[f"gb{c}"] = lambda b, c=c: gb(b, c)
            for lv in range(1, LEVELS):
                pieces[f"lev_a{lv}"] = lambda b, lv=lv: lev_a(b, lv)
                pieces[f"lev_d{lv}"] = lambda b, lv=lv: lev_d(b, lv)
            for c in range(NT):
                pieces[f"c_r{c}"] = lambda b, c=c: c_r(b, c)
                pieces[f"c_u{c}"] = lambda b, c=c: c_u(b, c)
                pieces[f"c_y{c}"] = lambda b, c=c: c_y(b, c)
            run(pe, pieces, unit)

        @block.scalar
        def _(act):
            af = nc.scalar.activation
            copy = nc.scalar.copy
            sqrt_hd = float(HD) ** 0.5
            for n in names:
                if n not in ONCE:
                    act.sem_inc(S[n], 1)
            act.wait_ge(S["loaded"], LOADED)
            af(cent_sq[:, :], nat["cent"][:, :], ACT.Square, accum_out=cent_ss[:, :]).then_inc(S["ss_ready"], 1)

            def prep(n, dst, src, scale=None):
                act.wait_ge(S["prep_pe"], n)
                (copy(dst, src) if scale is None else nc.scalar.mul(dst, src, scale)).then_inc(S["prep_out"], 1)

            perm = lambda w: w.rearrange("c (h d) -> c d h", d=HD)
            perm_out = lambda w: w.rearrange("c (d h) -> c d h", d=HD)
            prep(1, uqT[:, :], ps_a[0:QL, 0:P])
            prep(2, oT[:, :], ps_c0[:, 0:P])
            prep(3, wqeT[:, :], ps_c1[:, 0:P])
            prep(4, perm_out(w_q[:, :]), perm(ps_a[:, 0:P]), 1.0 / sqrt_hd)
            prep(5, veff[:, :], ps_c0[0:KVL, 0:P])
            prep(6, keffT[:, :], ps_c1[0:KVL, 0:P])
            prep(7, w_v[:, :], ps_c0[:, 0:P])
            prep(8, perm_out(w_k[:, :]), perm(ps_a[:, 0:P]))
            prep(9, wkT[:, 0:DS], ps_c0[:, 0:DS])
            prep(9, wvk[:, P:P + DS], ps_c0[:, 0:DS])
            prep(10, wqT[:, 0:DS], ps_c1[:, 0:DS])
            prep(11, vecT[:, :], ps_v[:, 0:NC + 4])
            act.wait_ge(S["prep_out"], 12)
            nc.scalar.mul(bq_lr[:, :], vecT[:, NC + 3:NC + 4], LR).then_inc(S["prep_out"], 1)
            prep(12, wvk[:, 0:P], ps_a[:, 0:P])
            act.wait_ge(S["prep_pe"], 13)
            af(sgT[:, :], ps_c0[:, 0:P], ACT.Sign).then_inc(S["prep_sign"], 1)
            act.wait_ge(S["prep_sign"], 1)
            nc.scalar.mul(sgT[:, :], sgT[:, :], 0.5).then_inc(S["prep_out"], 1)
            prep(14, vkbias[:, :], ps_c1[:, 0:2 * P])
            act.wait_ge(S["rn_ready"], 1)
            nc.scalar.mul(rw[0:EXPERTS, :], nat["cent"][:, :], cent_rn[:, 1:2]).then_inc(S["prep_out"], 1)
            prep(15, rwT[:, :], ps_a[:, 0:2 * EXPERTS])

            def a_full(b, n):
                act.wait_ge(S["a_filled"], b.count(A_FILLS, n + 1))

            def c0_full(b, n):
                act.wait_ge(S["c0_filled"], b.count(C0_FILLS, n + 1))

            def c1_full(b, n):
                act.wait_ge(S["c1_filled"], b.count(C1_FILLS, n + 1))

            def xnt(b):
                act.wait_ge(S["norm0"], b.count(NT, NT))
                after(act, S["rn_ready"], b.count(1, 0))
                for i in range(NT):
                    af(tG[:, i * P:(i + 1) * P], xn[:, i, :], ACT.Square, accum_out=ss[:, i:i + 1]).then_inc(S["ss_ready"], 1)
                a_full(b, A_XNT)
                copy(xnT[:, :], ps_a[:, :]).then_inc(S["a_emptied"], 1)

            def split_hi(b, n):
                a_full(b, A_Q + n)
                after(act, S["scratch_written"], b.count(32, 0))
                copy(parts[n][:, 0, :], ps_a[:, :]).then_inc(S["hi_ready"], 1)

            def v(b):
                a_full(b, A_V)
                after(act, S["pv_used"], b.count(3 * GROUPS, 0))
                copy(vaug[:, :, :, 0:HD], ps_a[:, :].rearrange("p (i h d) -> p i h d", i=NT, h=HEADS))\
                    .then_inc(S["a_emptied"], 1)

            def gates(b):
                act.wait_ge(S["dlt_ready"], b.count(1, 1))
                af(ex[:, :, :], dlt[:, :, :], ACT.Exp).then_inc(S["ex_ready"], 1)

            def gt(b):
                a_full(b, A_GT)
                copy(gT[0:PARTS * EXPERTS, :], ps_a[:, :].bitcast(BF16)[0:PARTS * EXPERTS, 0:TOK]).then_inc(S["a_emptied"], 1)

            def h(b, c):
                a_full(b, A_H + c)
                after(act, S["gelu_ready"], b.count(1, 0))
                af(hid[:, c, :], ps_a[:, :], ACT.Identity, bias=vecT[:, c:c + 1]).then_inc(S["a_emptied"], 1)

            def gelu(b):
                act.wait_ge(S["a_emptied"], b.count(A_FILLS, A_H + NC))
                af(hid[:, :, :], hid[:, :, :], ACT.Gelu).then_inc(S["gelu_ready"], 1)

            def out_piece(b):
                a_full(b, A_OUT)
                af(tG[:, :], ps_a[:, :], ACT.Tanh).then_inc(S["tg_ready"], 1)

            def m_rows(b):
                a_full(b, A_MT)
                after(act, S["mscratch_written"], b.count(16, 0))
                copy(mrow[:, :], ps_a[:, :].bitcast(BF16)[0:PARTS * 32, 0:TOK]).then_inc(S["a_emptied"], 1)

            def unit(cur, grp, nxt, mgrp, u):
                if cur is None:
                    return
                act.wait_ge(S["e_filled"], cur.count(GROUPS * UNITS, UNITS * grp + u + 1))
                if u in (0, 4, 8):
                    after(act, S["pv_used"], cur.count(3 * GROUPS, 3 * (grp - 1) + u // 4 + 1))
                af(prob[:, u, :], ps_e[:, u % 2, :], ACT.Exp).then_inc(S["e_emptied"], 1)

            def pv(b, grp):
                act.wait_ge(S["pv_used"], b.count(3 * GROUPS, 3 * grp + 3))
                copy(yT[:, :], ps_v[:, :]).then_inc(S["v_emptied"], 1)

            def c_xn2t(b):
                c0_full(b, C0_XN2T)
                copy(xn2T[:, :], ps_c0[:, :]).then_inc(S["c0_emptied"], 1)

            def c_ht(b):
                c1_full(b, C1_HT)
                af(hT[:, :], ps_c1[:, :], ACT.Identity, bias=vecT[:, NC + 1:NC + 2], scale=vecT[:, NC:NC + 1]).then_inc(S["c1_emptied"], 1)

            def c_kt(b):
                c0_full(b, C0_KT)
                af(kT[:, :], ps_c0[:, :], ACT.Identity, bias=vecT[:, NC + 2:NC + 3]).then_inc(S["c0_emptied"], 1)

            def c_qt(b):
                c1_full(b, C1_QT)
                af(qT[:, :], ps_c1[:, :], ACT.Identity, bias=bq_lr[:, :], scale=LR).then_inc(S["c1_emptied"], 1)

            def c_gram(b):
                c0_full(b, C0_GRAM)
                copy(gram[:, :, :].rearrange("p i d -> p (i d)"), ps_c0[:, :]).then_inc(S["c0_emptied"], 1)

            def lev_a(b, lv):
                c0_full(b, c0_a(lv))
                copy(ablk[:, :, :].rearrange("p i d -> p (i d)"), ps_c0[:, :]).then_inc(S["c0_emptied"], 1)

            def c_ffn(b):
                c1_full(b, C1_FFN)
                after(act, S["syg_ready"], b.count(1, 0))
                af(tF[:, :], ps_c1[:, :], ACT.Tanh).then_inc(S["tf_ready"], 1)

            def c_u(b, c):
                c0_full(b, c0_u(c))
                copy(u_sb[:, :], ps_c0[:, 0:P]).then_inc(S["c0_emptied"], 1)

            pieces = {"xnt": xnt, "q": lambda b: split_hi(b, 0), "k": lambda b: split_hi(b, 1), "v": v, "gates": gates, "gt": gt,
                      "gelu": gelu, "out": out_piece, "m_rows": m_rows, "pv2": pv, "c_xn2t": c_xn2t, "c_ht": c_ht, "c_kt": c_kt,
                      "c_qt": c_qt, "c_gram": c_gram, "c_ffn": c_ffn}
            for c in range(NC):
                pieces[f"h{c}"] = lambda b, c=c: h(b, c)
                pieces[f"c_u{c}"] = lambda b, c=c: c_u(b, c)
            for lv in range(1, LEVELS):
                pieces[f"lev_a{lv}"] = lambda b, lv=lv: lev_a(b, lv)
            run(act, pieces, unit)

        @block.vector
        def _(dve):
            vec = nc.vector
            dve.wait_ge(S["loaded"], LOADED)
            vec.tensor_scalar(w2s[:, :, :], w2s[:, :, :], 0.5, None, ALU.mult).then_inc(S["prep_out2"], 1)
            vec.tensor_scalar(b2r[:, 0, :], b2f[:, :], 0.5, None, ALU.mult).then_inc(S["prep_out2"], 1)
            dve.wait_ge(S["prep_out2"], 2)
            vec.tensor_copy(b2p[:, 0, :], b2r[:, 0, :]).then_inc(S["prep_out2"], 1)
            dve.wait_ge(S["prep_out2"], 3)
            vec.tensor_tensor(b2r[:, 1, :], b2r[:, 0, :], b2p[:, 0, :], ALU.subtract).then_inc(S["prep_out2"], 1)
            dve.wait_ge(S["prep_out2"], 4)
            vec.tensor_copy(b2p[:, 1, :], b2r[:, 1, :]).then_inc(S["prep_out2"], 1)
            dve.wait_ge(S["prep_out2"], 5)
            vec.tensor_tensor(b2p[:, 2, :], b2r[:, 1, :], b2p[:, 1, :], ALU.subtract).then_inc(S["prep_out2"], 1)
            dve.wait_ge(S["const_ready"], 4)
            dve.wait_ge(S["prep_out"], PREP_OUT)

            def a_full(b, n):
                dve.wait_ge(S["a_filled"], b.count(A_FILLS, n + 1))

            def c0_full(b, n):
                dve.wait_ge(S["c0_filled"], b.count(C0_FILLS, n + 1))

            def c1_full(b, n):
                dve.wait_ge(S["c1_filled"], b.count(C1_FILLS, n + 1))

            def ln_stats(n, b):
                if n == 0:
                    dve.wait_ge(S["x_loaded"], b.count(16, 16))
                    src = x_sb[b.parity]
                elif n == 1:
                    dve.wait_ge(S["x1_ready"], b.count(1, 1))
                    src = x1[b.parity]
                else:
                    dve.wait_ge(S["norm1"], b.count(NT, NT))
                    src = xn2
                for i in range(NT):
                    vec.bn_stats(stats[n][:, i, :], src[:, i, :]).then_inc(S[f"stats{n}"], 1)
                settled(dve, S[f"stats{n}"], b.count(NT, NT))
                for i in range(NT):
                    vec.bn_aggr(mv[n][:, i, :], stats[n][:, i, :]).then_inc(S[f"mv{n}"], 1)

            def ln_norm(n, b):
                src, dst = ((x_sb[b.parity], xn), (x1[b.parity], xn2), (xn2, hn))[n]
                dve.wait_ge(S[f"rstd{n}"], b.count(1, 1))
                if n == 0:
                    after(dve, S["a_filled"], b.count(A_FILLS, -A_FILLS + A_XNT + 1))
                    after(dve, S["ss_ready"], b.count(NT, 0))
                elif n == 1:
                    after(dve, S["c1_emptied"], b.count(C1_FILLS, 0))
                else:
                    after(dve, S["c1_filled"], b.count(C1_FILLS, 0))
                for i in range(NT):
                    vec.tensor_scalar(dst[:, i, :], src[:, i, :], mv[n][:, i, 0:1], rstd[n][:, i:i + 1], ALU.subtract, ALU.mult)\
                        .then_inc(S[f"norm{n}"], 1)

            def split_rest(b, n):
                dve.wait_ge(S["hi_ready"], b.count(2, n + 1))
                after(dve, S["parts_ready"], b.count(2, 0))
                vec.tensor_tensor(rest[n], ps_a[:, :], parts[n][:, 0, :], ALU.subtract).then_inc(S["a_emptied"], 1)

            def logits(b):
                a_full(b, A_LOGIT)
                dve.wait_ge(S["rn_ready"], b.count(1, 1))
                lg = ps_a[:, 0:2 * EXPERTS * NT].rearrange("p (i e) -> p i e", i=NT)
                vec.tensor_tensor(coss[:, :, :], lg[:, :, 0:EXPERTS], bcast(rn[:, :], 2, EXPERTS), ALU.mult).then_inc(S["cos_ready"], 1)
                dve.wait_ge(S["cos_ready"], b.count(1, 1))
                vec.tensor_tensor(logit[:, :, :], lg[:, :, EXPERTS:2 * EXPERTS], coss[:, :, :], ALU.add).then_inc(S["a_emptied"], 1)
                settled(dve, S["a_emptied"], b.count(A_FILLS, A_LOGIT + 1))
                for i in range(NT):
                    vec.max(top8[:, i, :], logit[:, i, :]).then_inc(S["top_ready"], 1)

            def gates(b):
                dve.wait_ge(S["top_ready"], b.count(NT, NT))
                vec.tensor_tensor(dlt[:, :, :], logit[:, :, :], top8[:, :, 0:1].to_broadcast([P, NT, EXPERTS]), ALU.subtract)\
                    .then_inc(S["dlt_ready"], 1)
                vec.tensor_tensor(keep[:, :, :], logit[:, :, :], top8[:, :, 1:2].to_broadcast([P, NT, EXPERTS]), ALU.is_ge)\
                    .then_inc(S["keep_ready"], 1)
                dve.wait_ge(S["keep_ready"], b.count(1, 1))
                dve.wait_ge(S["ex_ready"], b.count(1, 1))
                vec.tensor_tensor(gm[:, :, :], ex[:, :, :], keep[:, :, :], ALU.mult).then_inc(S["gm_ready"], 1)
                dve.wait_ge(S["gm_ready"], b.count(1, 1))
                vec.tensor_reduce(gsum[:, :], gm[:, :, :], AX_X, ALU.add).then_inc(S["gsum_ready"], 1)
                dve.wait_ge(S["gsum_ready"], b.count(1, 1))
                vec.reciprocal(grec[:, :], gsum[:, :]).then_inc(S["grec_ready"], 1)
                dve.wait_ge(S["grec_ready"], b.count(1, 1))
                vec.tensor_tensor(gate[:, :, :], gm[:, :, :], bcast(grec[:, :], 2, EXPERTS), ALU.mult).then_inc(S["gate_ready"], 1)

            def gb(b, c):
                a_full(b, A_GB + c)
                dve.wait_ge(S["gelu_ready"], b.count(1, 1))
                vec.tensor_tensor(hid[:, c, :], hid[:, c, :], ps_a[:, :], ALU.mult).then_inc(S["a_emptied"], 1)

            def out_piece(b):
                dve.wait_ge(S["tg_ready"], b.count(1, 1))
                after(dve, S["attg_ready"], b.count(1, -1))
                vec.scalar_tensor_tensor(out=gate_out[b.parity][:, :, :].rearrange("p i d -> p (i d)"), in0=tG[:, :], scalar=1.0,
                                         in1=ps_a[:, :], op0=ALU.add, op1=ALU.mult).then_inc(S["a_emptied"], 1)

            def unit(cur, grp, nxt, mgrp, u):
                if nxt is None:
                    return
                i, keys, hds = S_UNIT[u]
                if mgrp == 0 and u == 0:
                    after(dve, S["nm_ready"], nxt.count(1, 0))
                dve.wait_ge(S["s_filled"], nxt.count(GROUPS * UNITS, UNITS * mgrp + u + 1))
                h0 = GH * mgrp + hds[0]
                vec.tensor_reduce(cand[:, i, h0:h0 + len(hds), S_SLOT[u]],
                                  ps_s[:, u % 2, :].rearrange("p (a c) -> p a c", a=len(hds)), AX_X, ALU.max)\
                    .then_inc(S["s_emptied"], 1)

            def m_rows(b):
                dve.wait_ge(S["s_emptied"], b.count(GROUPS * UNITS, GROUPS * UNITS))
                after(dve, S["mparts_ready"], b.count(1, 0))
                vec.tensor_reduce(nm[:, :, :], cand[:, :, :, :], AX_X, ALU.max, negate=True).then_inc(S["nm_ready"], 1)

            def yt(b, grp):
                dve.wait_ge(S["yt_filled"], b.count(GROUPS, grp + 1))
                y = ps_v[:, :].rearrange("p (i h e) -> p i h e", i=NT, h=GH)
                if grp == 0:
                    after(dve, S["attg_ready"], b.count(1, 0))
                after(dve, S["v_emptied"], b.count(2 * GROUPS, 2 * grp))
                vec.reciprocal(rden[:, :, :], y[:, :, :, HD]).then_inc(S["rden_ready"], 1)
                dve.wait_ge(S["rden_ready"], b.count(GROUPS, grp + 1))
                w = GH * HD
                vec.tensor_tensor(att[:, :, w * grp:w * (grp + 1)].rearrange("p i (h d) -> p i h d", h=GH), y[:, :, :, 0:HD],
                                  bcast(rden[:, :, :], 3, HD), ALU.mult).then_inc(S["v_emptied"], 1)

            def c_vk(b):
                bias = bcast(vkbias[:, :], 1, 2)
                c0_full(b, C0_VK)
                vec.tensor_tensor(vk[:, 0:2, :], ps_c0[:, :].rearrange("p (i d) -> p i d", i=2), bias, ALU.add).then_inc(S["c0_emptied"], 1)
                c1_full(b, C1_VK)
                vec.tensor_tensor(vk[:, 2:4, :], ps_c1[:, :].rearrange("p (i d) -> p i d", i=2), bias, ALU.add).then_inc(S["c1_emptied"], 1)

            def c_gram(b):
                c1_full(b, C1_KQ)
                vec.tensor_tensor(kq[:, :, :], ps_c1[:, :].rearrange("p (i d) -> p i d", i=NT), bcast(strict[:, :], 1, NT), ALU.mult)\
                    .then_inc(S["c1_emptied"], 1)

            def lev_d(b, lv):
                old, new = lv % 2, (lv + 1) % 2
                flat = lambda t: t[:, :, :].rearrange("p i d -> p (i d)")
                if lv == 1:
                    dve.wait_ge(S["inv1_ready"], b.count(2, 2))
                c1_full(b, c1_dt(lv))
                vec.tensor_tensor(flat(invT[new]), flat(invT[old]), ps_c1[:, :], ALU.subtract).then_inc(S["c1_emptied"], 1)
                if lv < LEVELS - 1:
                    c0_full(b, c0_d(lv))
                    vec.tensor_tensor(flat(inv[new]), flat(inv[old]), ps_c0[:, :], ALU.subtract).then_inc(S["c0_emptied"], 1)

            def c_ffn(b):
                dve.wait_ge(S["tf_ready"], b.count(1, 1))
                after(dve, S["syg_ready"], b.count(1, 0))
                vec.scalar_tensor_tensor(out=tF[:, :], in0=tF[:, :], scalar=1.0, in1=ps_c1[:, :], op0=ALU.add, op1=ALU.mult)\
                    .then_inc(S["c1_emptied"], 1)

            def c_r(b, c):
                c0_full(b, c0_r(c))
                vec.scalar_tensor_tensor(out=rhs[:, :], in0=ps_c0[:, 0:P], scalar=-LR, in1=vk[:, c, 0:P], op0=ALU.mult, op1=ALU.add)\
                    .then_inc(S["c0_emptied"], 1)

            def c_y(b, c):
                if c == 0:
                    c0_full(b, c0_s(c))
                    vec.tensor_copy(state[:, :], ps_c0[:, 0:P]).then_inc(S["c0_emptied"], 1)
                elif c < NT - 1:
                    c0_full(b, c0_s(c))
                    vec.tensor_tensor(state[:, :], state[:, :], ps_c0[:, 0:P], ALU.add).then_inc(S["c0_emptied"], 1)
                else:
                    c1_full(b, C1_Y)
                    after(dve, S["syg_ready"], b.count(1, 0))
                    vec.tensor_tensor(sy[:, :, :], ps_c1[:, :].rearrange("p (i d) -> p i d", i=NT), xn2[:, :, :], ALU.add)\
                        .then_inc(S["c1_emptied"], 1)

            pieces = {"ln1_stats": lambda b: ln_stats(0, b), "ln2_stats": lambda b: ln_stats(1, b), "ln3_stats": lambda b: ln_stats(2, b),
                      "ln1_norm": lambda b: ln_norm(0, b), "ln2_norm": lambda b: ln_norm(1, b), "ln3_norm": lambda b: ln_norm(2, b),
                      "q": lambda b: split_rest(b, 0), "k": lambda b: split_rest(b, 1), "logits": logits, "gates": gates,
                      "out": out_piece, "m_rows": m_rows, "yt": yt, "c_vk": c_vk, "c_gram": c_gram, "c_ffn": c_ffn}
            for c in range(NC):
                pieces[f"gb{c}"] = lambda b, c=c: gb(b, c)
                pieces[f"c_r{c}"] = lambda b, c=c: c_r(b, c)
                pieces[f"c_y{c}"] = lambda b, c=c: c_y(b, c)
            for lv in range(1, LEVELS):
                pieces[f"lev_d{lv}"] = lambda b, lv=lv: lev_d(b, lv)
            run(dve, pieces, unit)


ONCE = ("const_ready", "mask_step", "loaded", "prep_pe", "prep_out", "prep_out2", "prep_sign", "stack_zeroed",
        "ss_ready", "rn_ready")
PREP_OUT = 18
S_UNIT = [(i, (P * i, P * i + P), (0, 1, 2, 3)) for i in range(4)] + [
    (1, (0, 128), (0, 1, 2, 3)), (2, (0, 256), (0, 1)), (2, (0, 256), (2, 3)),
    (3, (0, 256), (0, 1)), (3, (0, 256), (2, 3)), (3, (256, 384), (0, 1, 2, 3))]
S_SLOT = [0, 0, 0, 0, 1, 1, 1, 1, 1, 2]

_INS = ["L0_attn_x", "L0_attn_W_dq", "L0_attn_W_uq", "L0_attn_W_dkv", "L0_attn_W_uk", "L0_attn_W_uv", "L0_attn_W_o",
        "L0_ffn_w1", "L0_ffn_b1", "L0_ffn_w2", "L0_ffn_b2", "L0_ffn_centroids", "L0_ffn_w_route",
        "L1_attn_Wk", "L1_attn_bk", "L1_attn_Wv", "L1_attn_bv", "L1_attn_Wq", "L1_attn_bq", "L1_attn_gamma", "L1_attn_beta",
        "L1_ffn_weight"]


def kernel(**inputs):
    import numpy as _np
    import concourse.bacc as _bacc
    from concourse import mybir as _mybir
    from concourse.bass_utils import run_bass_kernel_spmd as _run

    nc = _bacc.Bacc("TRN2", target_bir_lowering=False, num_devices=1)
    arrays, args = {}, []
    for name in _INS:
        a = _np.ascontiguousarray(inputs[name])
        arrays[f"in_{name}_dram"] = a
        args.append(nc.dram_tensor(f"in_{name}_dram", a.shape, _mybir.dt.from_np(a.dtype), kind="ExternalInput").ap())
    shape = tuple(inputs["L0_attn_x"].shape)
    args.append(nc.dram_tensor("out_dram", shape, _mybir.dt.float32, kind="ExternalOutput").ap())
    nc.disable_value_cache = True
    two_layers(nc, *args)
    r = _run(nc, [arrays], core_ids=[0])
    return r.results[0]["out_dram"]
```

```python
from contextlib import ExitStack

import concourse.bass as bass
from concourse import mybir

ALU = mybir.AluOpType
ACT = mybir.ActivationFunctionType
F32 = mybir.dt.float32
BF16 = mybir.dt.bfloat16
AX_X = mybir.AxisListType.X

P = 128
HEADS, HD = 16, 8
EXPERTS, HID = 8, 64
DS = 64
VK = 128 + DS
LR = 0.01
LN_EPS = 1e-5
NORM_EPS = 1e-12
NEG = -1e30
PARTS = 3
PAIRS = PARTS * PARTS * HD
MAXROW = 96
GROUPS, GH = 4, 4
UNITS = 10
LEVELS = 7

A_FILLS = 15
A_XNT, A_Q, A_K = -10, -9, -8
A_LOGIT, A_GT, A_H, A_V = 3, 4, 8, 12
A_GB, A_OUT = 13, 17
C0_FILLS, C1_FILLS = 25, 12
C0_XN2T, C0_KT, C0_VK, C0_GRAM = 0, 1, 2, 3
C1_HT, C1_QT, C1_VK, C1_KQ, C1_FFN, C1_Y = 0, 1, 2, 3, 4, 11


def c0_a(k):
    return 4 + 2 * (k - 1)


def c0_d(k):
    return 5 + 2 * (k - 1)


def c1_dt(k):
    return 5 + (k - 1)


def c0_r(c):
    return 17 + 3 * (c - 1)


def c0_u(c):
    return 15 if c == 0 else 18 + 3 * (c - 1)


def c0_s(c):
    return 16 if c == 0 else 19 + 3 * (c - 1)


PLAN = {
    (0, 0): ["ln2_stats"], (0, 1): ["ln2_norm"], (0, 2): ["gb0"], (0, 3): ["ln3_stats", "c_xn2t", "gb1"], (0, 4): ["ln3_norm"],
    (0, 5): ["gb2"], (0, 6): ["pv0", "c_ht"], (0, 7): ["gb3"], (0, 8): ["c_kt", "c_qt"], (0, 9): ["pv1", "out"],
    (1, 0): ["load_x", "c_vk"], (1, 1): ["c_gram"], (1, 2): ["pv2", "logits"], (1, 3): ["gates", "c_ffn"], (1, 4): ["yt", "lev_a1"],
    (1, 5): ["gt"], (1, 6): ["pv0", "lev_d1"], (1, 8): ["lev_a2"], (1, 9): ["pv1"],
    (2, 0): ["lev_d2"], (2, 1): ["ln1_stats"], (2, 2): ["pv2", "lev_a3"], (2, 3): ["ln1_norm"], (2, 4): ["yt", "lev_d3"],
    (2, 5): ["xnt"], (2, 6): ["pv0", "lev_a4"], (2, 7): ["q"], (2, 8): ["lev_d4"], (2, 9): ["pv1", "k"],
    (3, 0): ["lev_a5"], (3, 2): ["pv2", "lev_d5"], (3, 4): ["yt", "lev_a6"], (3, 6): ["pv0", "lev_d6"], (3, 8): ["c_u0"],
    (3, 9): ["pv1", "c_y0"],
    (4, 0): ["m_parts", "stacks", "c_r1", "h0"], (4, 1): ["pv2", "c_u1", "h1"], (4, 2): ["c_y1", "h2"], (4, 3): ["yt", "c_r2", "h3"],
    (4, 4): ["m_rows", "c_u2"], (4, 5): ["x1", "c_y2"], (4, 6): ["c_r3", "v"], (4, 7): ["c_u3"], (4, 8): ["c_y3", "gelu"],
    (4, 9): ["c_out"],
}
PLAN_SECOND = ("load_x", "ln1_stats", "ln1_norm", "xnt", "q", "k", "stacks")
PLAN_NEXT = ("logits", "gates", "gt", "h0", "h1", "h2", "h3", "gelu", "v", "m_parts", "m_rows")
PLAN_CURRENT = ("gb0", "gb1", "gb2", "gb3", "out", "pv0", "pv1", "pv2", "yt", "x1")
SEQUENCES = 8


class Seq:

    def __init__(self, pair, c):
        self.pair, self.c, self.parity = pair, c, c % 2

    def count(self, per, k):
        if self.pair is None:
            return self.c * per + k + 1
        return self.pair * (2 * per) + (self.c * per + k + 1)

    def index(self):
        return self.c if self.pair is None else self.pair * 2 + self.c


def a_number(b, n):
    if b.pair is None and b.c == 0 and n < 0:
        return n - A_XNT
    if b.pair is None and b.c == SEQUENCES - 1 and n >= A_H:
        return n - 3
    return n


def after(eng, sem, value):
    if not (isinstance(value, int) and value <= 1):
        eng.wait_ge(sem, value)


def two_layers(nc, x_in, W_dq, W_uq, W_dkv, W_uk, W_uv, W_o, w1_in, b1_in, w2_in, b2_in, cent_in, route_in,
               Wk_in, bk_in, Wv_in, bv_in, Wq_in, bq_in, gamma_in, beta_in, sign_in, out):
    SEQS, TOK, D = x_in.shape
    NT = TOK // P
    QL = W_dq.shape[0]
    KVL = W_dkv.shape[0]
    NC = EXPERTS * HID // P
    assert D == P and NT == 4 and SEQS == SEQUENCES and NC == 4

    with ExitStack() as ctx:
        def sb(name, shape, dt=F32):
            return ctx.enter_context(nc.sbuf_tensor(name, shape, dt))

        def psum(name, shape, dt=F32):
            return ctx.enter_context(nc.psum_tensor(name, shape, dt))

        def sem(name):
            return ctx.enter_context(nc.semaphore(name))

        ps_s = psum("ps_s", [P, 2, 512])
        ps_e = psum("ps_e", [P, 2, 512])
        ps_v = psum("ps_v", [P, 512])
        ps_a = psum("ps_a", [P, 512])
        ps_c0 = psum("ps_c0", [P, 512])
        ps_c1 = psum("ps_c1", [P, 512])

        ident = sb("ident", [P, P])
        identb = sb("identb", [P, P], BF16)
        negmask = sb("negmask", [P, P], BF16)
        lowmask0 = sb("lowmask0", [P, P])
        upmask = sb("upmask", [P, LEVELS, P])
        strict = sb("strict", [P, P])
        pick = sb("pick", [MAXROW, NC, P], BF16)
        halfpow = sb("halfpow", [P, 4])
        ones_row = sb("ones_row", [1, P])
        fence = sb("fence", [1, P])
        nat = {n: sb("nat_" + n, s) for n, s in (
            ("dq", [QL, P]), ("uq", [P, QL]), ("dkv", [KVL, P]), ("uk", [P, KVL]), ("uv", [P, KVL]), ("o", [P, P]),
            ("wk", [DS, P]), ("wv", [P, P]), ("wq", [DS, P]), ("sg", [P, P]), ("cent", [EXPERTS, P]))}
        uqT = sb("uqT", [QL, P])
        oT = sb("oT", [P, P])
        wqeT = sb("wqeT", [P, P])
        keffT = sb("keffT", [KVL, P])
        veff = sb("veff", [KVL, P])
        w_q = sb("w_q", [P, P])
        w_k = sb("w_k", [P, P])
        w_v = sb("w_v", [P, P])
        rw = sb("rw", [2 * EXPERTS, P])
        rwT = sb("rwT", [P, 2 * EXPERTS])
        cent_ss = sb("cent_ss", [EXPERTS, 1])
        cent_sq = sb("cent_sq", [EXPERTS, P])
        cent_rn = sb("cent_rn", [EXPERTS, 2])
        w1s = sb("w1s", [P, EXPERTS, HID])
        vecs = sb("vecs", [NC + 4, P])
        vecT = sb("vecT", [P, NC + 4])
        w2s = sb("w2s", [P, NC, P])
        b2f = sb("b2f", [MAXROW, P])
        b2r = sb("b2r", [MAXROW, 2, P])
        b2p = sb("b2p", [MAXROW, PARTS, P], BF16)
        wkT = sb("wkT", [P, P])
        wqT = sb("wqT", [P, P])
        wvk = sb("wvk", [P, VK])
        sgT = sb("sgT", [P, P])
        bq_lr = sb("bq_lr", [P, 1])
        vkrow = sb("vkrow", [1, VK])
        vkbias = sb("vkbias", [P, VK])

        x_res = sb("x_res", [P, NT, P])
        x1 = [sb(f"x1_{p}", [P, NT, P]) for p in range(2)]
        gate_out = sb("gate_out", [P, NT, P])
        qst = [sb(f"qst{p}", [P, HEADS, TOK], BF16) for p in range(2)]
        kst = [sb(f"kst{p}", [P, HEADS, TOK], BF16) for p in range(2)]
        vaug = sb("vaug", [P, NT, HEADS, 32])
        stats = [sb(f"stats{n}", [P, NT, 6]) for n in range(3)]
        mv = [sb(f"mv{n}", [P, NT, 2]) for n in range(3)]
        vare = [sb(f"vare{n}", [P, NT]) for n in range(3)]
        rstd = [sb(f"rstd{n}", [P, NT]) for n in range(3)]
        xn = sb("xn", [P, NT, P])
        xnT = [sb(f"xnT{p}", [P, TOK]) for p in range(2)]
        ss = sb("ss", [P, NT])
        ssm = sb("ssm", [P, NT])
        rn = sb("rn", [P, NT])
        parts = [sb(n, [P, PARTS, TOK], BF16) for n in ("qparts", "kparts")]
        rest = [xn[:, :, :].rearrange("p i d -> p (i d)"), sb("krest", [P, TOK])[:, :]]
        coss = sb("coss", [P, NT, EXPERTS])
        logit = sb("logit", [P, NT, EXPERTS])
        top8 = sb("top8", [P, NT, EXPERTS])
        keep = sb("keep", [P, NT, EXPERTS])
        dlt = sb("dlt", [P, NT, EXPERTS])
        ex = sb("ex", [P, NT, EXPERTS])
        gm = sb("gm", [P, NT, EXPERTS])
        gsum = sb("gsum", [P, NT])
        grec = sb("grec", [P, NT])
        gate = sb("gate", [P, NT, EXPERTS])
        grest = sb("grest", [P, NT, EXPERTS])
        gparts = sb("gparts", [P, NT, PARTS, EXPERTS], BF16)
        gT = sb("gT", [MAXROW, TOK], BF16)
        hid = sb("hid", [P, NC, TOK])
        tG = sb("tG", [P, TOK])
        cand = sb("cand", [P, NT, HEADS, 3])
        nm = sb("nm", [P, NT, HEADS])
        nmrest = sb("nmrest", [P, NT, HEADS])
        mparts = sb("mparts", [P, NT, PARTS, 32], BF16)
        mrow = sb("mrow", [PARTS * 32, TOK], BF16)
        prob = sb("prob", [P, UNITS, 512])
        yT = sb("yT", [P, TOK])
        rden = sb("rden", [P, NT, GH])
        att = sb("att", [P, NT, P])
        xn2 = sb("xn2", [P, NT, P])
        hn = sb("hn", [P, NT, P])
        gram = hn
        xn2T = sb("xn2T", [P, TOK])
        hT = sb("hT", [P, TOK])
        kT = sb("kT", [P, TOK])
        qT = sb("qT", [P, TOK])
        vk = sb("vk", [P, NT, VK])
        kq = sb("kq", [P, NT, P])
        pair_up = [sb(f"pair_up{p}", [P, NT, P]) for p in range(2)]
        inv = [sb(f"inv{p}", [P, NT, P]) for p in range(2)]
        invT = [sb(f"invT{p}", [P, NT, P]) for p in range(2)]
        ablk = sb("ablk", [P, NT, P])
        rhs = sb("rhs", [P, P])
        u_sb = sb("u_sb", [P, P])
        state = sb("state", [P, P])
        tF = sb("tF", [P, TOK])
        sy = sb("sy", [P, NT, P])
        syg = sb("syg", [P, NT, P])
        out_sb = sb("out_sb", [P, NT, P])

        max_scratch = nc.dram_tensor("max_scratch", (PARTS * 32, TOK), BF16).ap()
        scratch = nc.dram_tensor("split_scratch", (2, PARTS, P, TOK), BF16).ap()

        names = """const_ready mask_step loaded prep_pe prep_out prep_out2 prep_sign small_zeroed kst_zeroed vaug_zeroed
        x_loaded res_loaded scratch_written stack_loaded mscratch_written mrow_loaded stored
        a_filled a_emptied c0_filled c0_emptied c1_filled c1_emptied pv_used yt_filled v_emptied
        s_filled s_emptied e_filled e_emptied
        stats0 stats1 stats2 mv0 mv1 mv2 var0 var1 var2 rstd0 rstd1 rstd2 norm0 norm1 norm2
        ss_ready ssm_ready rn_ready hi_ready mid_ready parts_ready
        cos_ready top_ready keep_ready dlt_ready ex_ready gm_ready gsum_ready grec_ready gate_ready
        ghi_ready grest_ready gmid_ready gparts_ready gelu_ready tg_ready
        mrow_filled mrow_ready nm_ready mhi_ready mrest_ready mmid_ready mparts_ready
        rden_ready attg_ready x1_ready
        dtmp_ready inv1_ready pair_ready tf_ready syg_ready out_ready""".split()
        S = {n: sem(n) for n in names}


        block = ctx.enter_context(nc.Block())

        fences = [0]

        def settled(eng, sem, value):
            eng.wait_ge(sem, value)
            if not isinstance(value, int):
                fences[0] += 1
                spot = fence[0:1, fences[0]:fences[0] + 1]
                eng.tensor_tensor(spot, ident[0:1, 0:1], ident[0:1, 0:1], ALU.mult)

        def bcast(ap, axis, n):
            ap = ap.unsqueeze(axis)
            shape = list(ap.shape)
            shape[axis] = n
            return ap.to_broadcast(shape)

        def run(eng, pieces, unit):
            def iteration(second, nxt, cur, prev):
                for step in range(GROUPS + 1):
                    for u in range(UNITS):
                        if step < GROUPS:
                            unit(cur, nxt, step, u)
                        for name in PLAN.get((step, u), []):
                            of = second if name in PLAN_SECOND else nxt if name in PLAN_NEXT else \
                                cur if name in PLAN_CURRENT else prev
                            if of is not None and name in pieces:
                                if name in ("pv0", "pv1"):
                                    pieces[name](of, step)
                                elif name in ("pv2", "yt"):
                                    pieces[name](of, step - 1)
                                else:
                                    pieces[name](of)

            seqs = [Seq(None, c) for c in range(SEQS)]
            iteration(seqs[0], None, None, None)
            iteration(seqs[1], seqs[0], None, None)
            iteration(seqs[2], seqs[1], seqs[0], None)
            with eng.Fori(0, (SEQS - 4) // 2) as pair:
                for odd in range(2):
                    iteration(*(Seq(pair, ahead + odd) for ahead in (3, 2, 1, 0)))
            iteration(*seqs[:SEQS - 5:-1])
            iteration(None, *seqs[:SEQS - 4:-1])
            iteration(None, None, *seqs[:SEQS - 3:-1])
            iteration(None, None, None, seqs[SEQS - 1])

        x_view = x_in.rearrange("b (i p) d -> b p i d", p=P)
        out_view = out.rearrange("b (i p) d -> b p i d", p=P)

        def row(v):
            return v.rearrange("(o d) -> o d", o=1)

        loads = [
            (nat["dq"][:, :], W_dq), (nat["uq"][:, :], W_uq), (nat["dkv"][:, :], W_dkv), (nat["uk"][:, :], W_uk),
            (nat["uv"][:, :], W_uv), (nat["o"][:, :], W_o), (nat["cent"][:, :], cent_in), (rw[EXPERTS:2 * EXPERTS, :], route_in),
            (w1s[:, :, :], w1_in.rearrange("e d f -> d e f")),
            (w2s[:, :, :], w2_in.rearrange("(c a) f d -> (a f) c d", a=2)),
            (nat["wk"][:, :], Wk_in), (nat["wv"][:, :], Wv_in), (nat["wq"][:, :], Wq_in), (nat["sg"][:, :], sign_in),
        ]
        zero_loads = [(b2f[EXPERTS * r:EXPERTS * (r + 1), :], b2_in) for r in range(PARTS)] + [
            (vecs[0:NC, :], b1_in.rearrange("(c a) f -> c (a f)", a=2)), (vecs[NC:NC + 1, :], row(gamma_in)),
            (vecs[NC + 1:NC + 2, :], row(beta_in)), (vecs[NC + 2:NC + 3, 0:DS], row(bk_in)), (vecs[NC + 3:NC + 4, 0:DS], row(bq_in)),
            (vkrow[:, 0:P], row(bv_in)), (vkrow[:, P:P + DS], row(bk_in))]
        LOADED = 16 * (len(loads) + len(zero_loads))

        @block.sync
        def _(sp):
            for dst, src in loads:
                sp.dma_start(dst, src).then_inc(S["loaded"], 16)
            sp.wait_ge(S["small_zeroed"], 1)
            for dst, src in zero_loads:
                sp.dma_start(dst, src).then_inc(S["loaded"], 16)

            def dram(view, b):
                if b.pair is None:
                    return view[b.index()]
                return view[bass.ds(b.index(), 1)].rearrange("o p i d -> (o p) i d")

            def load_residual(b):
                after(sp, S["x1_ready"], b.count(1, 0))
                sp.dma_start(x_res[:, :, :], dram(x_view, b)).then_inc(S["res_loaded"], 16)

            def load_x(b):
                after(sp, S["parts_ready"], b.count(2, 0))
                sp.dma_start(xn[:, :, :], dram(x_view, b)).then_inc(S["x_loaded"], 16)

            def write_parts(b, n):
                after(sp, S["stack_loaded"], b.count(192, 0))
                sp.wait_ge(S["parts_ready"], b.count(2, n + 1))
                sp.dma_start(scratch[n].rearrange("r s q -> s r q"), parts[n][:, :, :]).then_inc(S["scratch_written"], 16)

            def load_stacks(b):
                sp.wait_ge(S["kst_zeroed"], 1)
                sp.wait_ge(S["vaug_zeroed"], 1)
                after(sp, S["e_filled"], b.count(GROUPS * UNITS, -GROUPS * UNITS))
                sp.wait_ge(S["scratch_written"], b.count(32, 32))
                q_rows = scratch[0].rearrange("r (d h) q -> (r d) (h q)", d=HD)
                k_rows = scratch[1].rearrange("r (d h) q -> (r d) (h q)", d=HD)
                n3 = PARTS * HD
                for s in range(PARTS):
                    sp.dma_start(qst[b.parity][n3 * s:n3 * s + n3, :, :].rearrange("p h q -> p (h q)"), q_rows,
                                 max_dma_last_dim=4096).then_inc(S["stack_loaded"], 16)
                    for r in range(PARTS):
                        lo = n3 * s + HD * r
                        sp.dma_start(kst[b.parity][lo:lo + HD, :, :].rearrange("p h q -> p (h q)"), k_rows[HD * s:HD * s + HD, :],
                                     max_dma_last_dim=4096).then_inc(S["stack_loaded"], 16)

            def m_rows(b):
                sp.wait_ge(S["mrow_ready"], b.count(1, 1))
                after(sp, S["mrow_loaded"], b.count(16, 0))
                sp.dma_start(max_scratch, mrow[:, :]).then_inc(S["mscratch_written"], 16)
                sp.wait_ge(S["mscratch_written"], b.count(16, 16))
                sp.dma_start(qst[b.parity][MAXROW:MAXROW + PARTS, :, :].rearrange("r h q -> r (h q)"),
                             max_scratch.rearrange("(r h) q -> r h q", r=PARTS)[:, 0:HEADS, :].rearrange("r h q -> r (h q)"), max_dma_last_dim=2048).then_inc(S["mrow_loaded"], 16)

            def c_out(b):
                sp.wait_ge(S["out_ready"], b.count(1, 1))
                sp.dma_start(dram(out_view, b), out_sb[:, :, :]).then_inc(S["stored"], 16)

            run(sp, {"gb0": load_residual, "load_x": load_x, "q": lambda b: write_parts(b, 0), "k": lambda b: write_parts(b, 1),
                     "stacks": load_stacks, "m_rows": m_rows, "c_out": c_out}, lambda *a: None)
            sp.wait_ge(S["stored"], 16 * SEQS + 1)

        @block.gpsimd
        def _(pool):
            g = nc.gpsimd
            steps = [0]

            def chain(ins):
                steps[0] += 1
                ins.then_inc(S["mask_step"], 1)
                pool.wait_ge(S["mask_step"], steps[0])

            chain(g.memset(b2f[:, :], 0.0))
            chain(g.memset(vecs[:, :], 0.0))
            chain(g.memset(vkrow[:, :], 0.0))
            g.memset(halfpow[:, :], -0.5).then_inc(S["small_zeroed"], 1)
            chain(g.memset(ident[:, :], 0.0))
            chain(g.affine_select(out=ident[:, :], in_=ident[:, :], compare_op=ALU.not_equal, fill=1.0, base=0,
                                  pattern=[[-1, P]], channel_multiplier=1))
            chain(g.tensor_copy(identb[:, :], ident[:, :]))
            chain(g.memset(ones_row[:, :], 1.0))
            g.memset(state[:, :], 0.0).then_inc(S["const_ready"], 1)
            chain(g.memset(negmask[:, :], 0.0))
            chain(g.affine_select(out=negmask[:, :], in_=negmask[:, :], compare_op=ALU.is_ge, fill=NEG, base=0,
                                  pattern=[[-1, P]], channel_multiplier=1))
            pool.wait_ge(S["ss_ready"], 1)
            chain(g.tensor_scalar(cent_rn[:, 0:1], cent_ss[:, :], NORM_EPS * NORM_EPS, None, ALU.max))
            g.tensor_tensor(cent_rn[:, 1:2], cent_rn[:, 0:1], halfpow[0:EXPERTS, 0:1], ALU.pow).then_inc(S["rn_ready"], 1)
            for n, t in enumerate((wkT[:, DS:P], wqT[:, DS:P])):
                g.memset(t, 0.0).then_inc(S["const_ready"], 1)
                pool.wait_ge(S["const_ready"], n + 2)
            for p in range(2):
                chain(g.memset(kst[p][64:P, :, :].bitcast(F32), 0.0))
                chain(g.memset(kst[p][MAXROW:MAXROW + PARTS, :, :], 1.0))
            g.memset(fence[:, :], 0.0).then_inc(S["kst_zeroed"], 1)
            pool.wait_ge(S["vaug_zeroed"], 1)
            chain(g.memset(cand[:, :, :, :], -3e38))
            chain(g.memset(gT[:, :], 0.0))
            chain(g.memset(mparts[:, :, :, :], 0.0))
            chain(g.memset(pick[:, :, :], 0.0))
            for r in range(PARTS):
                chain(g.affine_select(out=pick[:, :, :].rearrange("p c (a f) -> p c a f", a=2),
                                      in_=pick[:, :, :].rearrange("p c (a f) -> p c a f", a=2),
                                      compare_op=ALU.not_equal, fill=1.0, base=-EXPERTS * r,
                                      pattern=[[-2, NC], [-1, 2], [0, HID]], channel_multiplier=1))
            chain(g.memset(strict[:, :], 1.0))
            chain(g.affine_select(out=strict[:, :], in_=strict[:, :], compare_op=ALU.is_gt, fill=0.0, base=0,
                                  pattern=[[1, P]], channel_multiplier=-1))
            chain(g.memset(lowmask0[:, :], 0.0))
            low = lowmask0[:, :].rearrange("p (n a) -> p n a", a=2)[:, :, 0]
            chain(g.memset(low, LR))
            chain(g.affine_select(out=low, in_=low, compare_op=ALU.is_equal, fill=0.0, base=-1,
                                  pattern=[[-2, P // 2]], channel_multiplier=1))
            chain(g.memset(upmask[:, :, :], 0.0))
            for lv in range(LEVELS):
                s = 1 << lv
                nb = P // (2 * s)
                half = upmask[:, lv, :].rearrange("p (n a w) -> p n a w", a=2, w=s)[:, :, 1, :]
                chain(g.memset(half, LR))
                chain(g.affine_select(out=half, in_=half, compare_op=ALU.is_ge, fill=0.0, base=0,
                                      pattern=[[-2 * s, nb], [0, s]], channel_multiplier=1))
                chain(g.affine_select(out=half, in_=half, compare_op=ALU.is_ge, fill=0.0, base=s - 1,
                                      pattern=[[2 * s, nb], [0, s]], channel_multiplier=-1))
            g.memset(vaug[:, :, :, HD:HD + 1], 1.0).then_inc(S["const_ready"], 1)

            def ln_rstd(n, b):
                settled(pool, S[f"mv{n}"], b.count(NT, NT))
                g.tensor_scalar(vare[n][:, :], mv[n][:, :, 1], LN_EPS, None, ALU.add).then_inc(S[f"var{n}"], 1)
                pool.wait_ge(S[f"var{n}"], b.count(1, 1))
                g.tensor_tensor(rstd[n][:, :], vare[n][:, :], halfpow[:, :], ALU.pow).then_inc(S[f"rstd{n}"], 1)

            def split_rest(n, b):
                settled(pool, S["a_emptied"], b.count(A_FILLS, a_number(b, A_Q + n) + 1))
                g.tensor_copy(parts[n][:, 1, :], rest[n]).then_inc(S["mid_ready"], 1)
                pool.wait_ge(S["mid_ready"], b.count(2, n + 1))
                g.tensor_tensor(parts[n][:, 2, :], rest[n], parts[n][:, 1, :], ALU.subtract).then_inc(S["parts_ready"], 1)

            def token_norms(b):
                settled(pool, S["ss_ready"], b.count(NT, NT))
                g.tensor_scalar(ssm[:, :], ss[:, :], NORM_EPS * NORM_EPS, None, ALU.max).then_inc(S["ssm_ready"], 1)
                pool.wait_ge(S["ssm_ready"], b.count(1, 1))
                after(pool, S["cos_ready"], b.count(1, 0))
                g.tensor_tensor(rn[:, :], ssm[:, :], halfpow[:, :], ALU.pow).then_inc(S["rn_ready"], 1)

            def gates(b):
                settled(pool, S["gate_ready"], b.count(1, 1))
                g.tensor_copy(gparts[:, :, 0, :], gate[:, :, :]).then_inc(S["ghi_ready"], 1)
                pool.wait_ge(S["ghi_ready"], b.count(1, 1))
                g.tensor_tensor(grest[:, :, :], gate[:, :, :], gparts[:, :, 0, :], ALU.subtract).then_inc(S["grest_ready"], 1)
                settled(pool, S["grest_ready"], b.count(1, 1))
                g.tensor_copy(gparts[:, :, 1, :], grest[:, :, :]).then_inc(S["gmid_ready"], 1)
                pool.wait_ge(S["gmid_ready"], b.count(1, 1))
                g.tensor_tensor(gparts[:, :, 2, :], grest[:, :, :], gparts[:, :, 1, :], ALU.subtract).then_inc(S["gparts_ready"], 1)

            def m_parts(b):
                settled(pool, S["nm_ready"], b.count(1, 1))
                g.tensor_copy(mparts[:, :, 0, 0:HEADS], nm[:, :, :]).then_inc(S["mhi_ready"], 1)
                pool.wait_ge(S["mhi_ready"], b.count(1, 1))
                g.tensor_tensor(nmrest[:, :, :], nm[:, :, :], mparts[:, :, 0, 0:HEADS], ALU.subtract).then_inc(S["mrest_ready"], 1)
                settled(pool, S["mrest_ready"], b.count(1, 1))
                g.tensor_copy(mparts[:, :, 1, 0:HEADS], nmrest[:, :, :]).then_inc(S["mmid_ready"], 1)
                pool.wait_ge(S["mmid_ready"], b.count(1, 1))
                g.tensor_tensor(mparts[:, :, 2, 0:HEADS], nmrest[:, :, :], mparts[:, :, 1, 0:HEADS], ALU.subtract).then_inc(S["mparts_ready"], 1)

            def x1_piece(b):
                p = b.parity
                pool.wait_ge(S["v_emptied"], b.count(2 * GROUPS, 2 * GROUPS))
                g.tensor_tensor(att[:, :, :], att[:, :, :], gate_out[:, :, :], ALU.mult).then_inc(S["attg_ready"], 1)
                pool.wait_ge(S["attg_ready"], b.count(1, 1))
                pool.wait_ge(S["res_loaded"], b.count(16, 16))
                after(pool, S["out_ready"], b.count(1, -1))
                g.tensor_tensor(x1[p][:, :, :], x_res[:, :, :], att[:, :, :], ALU.add).then_inc(S["x1_ready"], 1)

            def c_gram(b):
                eye = bcast(ident[:, :], 1, NT)
                pool.wait_ge(S["c0_emptied"], b.count(C0_FILLS, C0_GRAM + 1))
                for n, (mask, dst) in enumerate(((lowmask0[:, :], inv[1]), (upmask[:, 0, :], invT[1]))):
                    g.tensor_tensor((sy, syg)[n][:, :, :], gram[:, :, :], bcast(mask, 1, NT), ALU.mult).then_inc(S["dtmp_ready"], 1)
                    pool.wait_ge(S["dtmp_ready"], b.count(2, n + 1))
                    g.tensor_tensor(dst[:, :, :], eye, (sy, syg)[n][:, :, :], ALU.subtract).then_inc(S["inv1_ready"], 1)
                pairs(b, 1)
                pairs(b, 2)

            def pairs(b, lv):
                if lv < LEVELS:
                    if lv > 2:
                        pool.wait_ge(S["c0_filled"], b.count(C0_FILLS, c0_a(lv - 2) + 1))
                    g.tensor_tensor(pair_up[lv % 2][:, :, :], gram[:, :, :], bcast(upmask[:, lv, :], 1, NT), ALU.mult)\
                        .then_inc(S["pair_ready"], 1)

            def c_out(b):
                pool.wait_ge(S["c1_emptied"], b.count(C1_FILLS, C1_Y + 1))
                g.tensor_tensor(syg[:, :, :], sy[:, :, :], tF[:, :].rearrange("p (i d) -> p i d", i=NT), ALU.mult)\
                    .then_inc(S["syg_ready"], 1)
                pool.wait_ge(S["syg_ready"], b.count(1, 1))
                after(pool, S["stored"], b.count(16, 0))
                g.tensor_tensor(out_sb[:, :, :], x1[b.parity][:, :, :], syg[:, :, :], ALU.add).then_inc(S["out_ready"], 1)

            levels = {f"lev_d{lv}": lambda b, lv=lv: pairs(b, lv + 2) for lv in range(1, LEVELS)}
            run(pool, levels | {"ln1_norm": lambda b: ln_rstd(0, b), "ln2_norm": lambda b: ln_rstd(1, b), "ln3_norm": lambda b: ln_rstd(2, b),
                       "q": lambda b: split_rest(0, b), "k": lambda b: split_rest(1, b), "xnt": token_norms, "gates": gates,
                       "m_parts": m_parts, "x1": x1_piece, "c_gram": c_gram, "c_out": c_out}, lambda *a: None)

        @block.tensor
        def _(pe):
            mm, tr = nc.tensor.matmul, nc.tensor.transpose
            pe.wait_ge(S["const_ready"], 1)
            pe.wait_ge(S["loaded"], LOADED)
            done = [0]

            def prep(ins, need=None):
                done[0] += 1
                ins.then_inc(S["prep_pe"], 1)

            def ready(n):
                pe.wait_ge(S["prep_out"], n)

            prep(tr(ps_a[0:QL, 0:P], nat["uq"][:, :], ident[:, :]))
            prep(tr(ps_c0[:, 0:P], nat["o"][:, :], ident[:, :]))
            ready(2)
            prep(mm(ps_c1[:, 0:P], uqT[:, :], nat["dq"][:, :], start=True, stop=True))
            prep(mm(ps_a[:, 0:P], nat["dq"][:, :], uqT[:, :], start=True, stop=True))
            prep(mm(ps_c0[0:KVL, 0:P], nat["uv"][:, :], oT[:, :], start=True, stop=True))
            ready(5)
            prep(mm(ps_c1[0:KVL, 0:P], nat["uk"][:, :], wqeT[:, :], start=True, stop=True))
            prep(mm(ps_c0[:, 0:P], nat["dkv"][:, :], veff[:, :], start=True, stop=True))
            ready(7)
            prep(mm(ps_a[:, 0:P], nat["dkv"][:, :], keffT[:, :], start=True, stop=True))
            prep(tr(ps_c0[:, 0:DS], nat["wk"][:, :], ident[0:DS, 0:DS]))
            prep(tr(ps_c1[:, 0:DS], nat["wq"][:, :], ident[0:DS, 0:DS]))
            prep(tr(ps_v[:, 0:NC + 4], vecs[:, :], ident[0:NC + 4, 0:NC + 4]))
            ready(12)
            prep(tr(ps_a[:, 0:P], nat["wv"][:, :], ident[:, :]))
            prep(tr(ps_c0[:, 0:P], nat["sg"][:, :], ident[:, :]))
            prep(mm(ps_c1[:, 0:VK], ones_row[:, :], vkrow[:, :], start=True, stop=True))
            ready(17)
            prep(tr(ps_a[:, 0:2 * EXPERTS], rw[:, :], ident[0:2 * EXPERTS, 0:2 * EXPERTS]))
            ready(PREP_OUT)
            pe.wait_ge(S["const_ready"], 4)

            def a_fill(b, n):
                after(pe, S["a_emptied"], b.count(A_FILLS, a_number(b, n)))

            def c0_fill(b, n):
                after(pe, S["c0_emptied"], b.count(C0_FILLS, n))

            def c1_fill(b, n):
                after(pe, S["c1_emptied"], b.count(C1_FILLS, n))

            def tok(i):
                return slice(i * P, (i + 1) * P)

            def xnt(b):
                a_fill(b, A_XNT)
                pe.wait_ge(S["norm0"], b.count(NT, NT))
                for i in range(NT):
                    last = tr(ps_a[:, tok(i)], xn[:, i, :], ident[:, :])
                last.then_inc(S["a_filled"], 1)

            def qk(b, n):
                a_fill(b, A_Q + n)
                mm(ps_a[:, :], (w_q, w_k)[n][:, :], xnT[b.parity][:, :], start=True, stop=True).then_inc(S["a_filled"], 1)

            def v(b):
                a_fill(b, A_V)
                for i in range(NT):
                    last = mm(ps_a[:, tok(i)], xnT[b.parity][:, tok(i)], w_v[:, :], start=True, stop=True)
                last.then_inc(S["a_filled"], 1)

            def logits(b):
                a_fill(b, A_LOGIT)
                for i in range(NT):
                    last = mm(ps_a[:, 16 * i:16 * i + 16], xnT[b.parity][:, tok(i)], rwT[:, :], start=True, stop=True)
                last.then_inc(S["a_filled"], 1)

            def gt(b):
                a_fill(b, A_GT)
                pe.wait_ge(S["gparts_ready"], b.count(1, 1))
                for i in range(NT):
                    last = tr(ps_a[:, :].bitcast(BF16)[0:PARTS * EXPERTS, tok(i)],
                              gparts[:, i, :, :].rearrange("p r e -> p (r e)"), identb[:, :])
                last.then_inc(S["a_filled"], 1)

            def h(b, c):
                a_fill(b, A_H + c)
                mm(ps_a[:, :], w1s[:, 2 * c:2 * c + 2, :].rearrange("p e f -> p (e f)"), xnT[b.parity][:, :], start=True, stop=True)\
                    .then_inc(S["a_filled"], 1)

            def gb(b, c):
                a_fill(b, A_GB + c)
                mm(ps_a[:, :], pick[:, c, :], gT[:, :], start=True, stop=True).then_inc(S["a_filled"], 1)

            def out_piece(b):
                a_fill(b, A_OUT)
                for i in range(NT):
                    for c in range(NC):
                        mm(ps_a[:, tok(i)], hid[:, c, tok(i)], w2s[:, c, :], start=(i == 0 and c == 0), stop=False,
                           skip_group_check=True)
                    for r in range(PARTS):
                        last = mm(ps_a[:, tok(i)], gT[:, tok(i)], b2p[:, r, :], start=False, stop=(r == PARTS - 1),
                                  skip_group_check=True)
                last.then_inc(S["a_filled"], 1)

            def m_rows(b):
                pe.wait_ge(S["mparts_ready"], b.count(1, 1))
                for i in range(NT):
                    last = tr(ps_s[:, 0, :].bitcast(BF16)[0:PARTS * 32, tok(i)],
                              mparts[:, i, :, :].rearrange("p r h -> p (r h)"), identb[:, :])
                last.then_inc(S["mrow_filled"], 1)

            def unit(cur, nxt, grp, u):
                if cur is not None:
                    e_unit(cur, grp, u)
                if nxt is not None:
                    s_unit(nxt, grp, u)

            def e_unit(b, grp, u):
                q, k = qst[b.parity], kst[b.parity]
                bank = u % 2
                after(pe, S["e_emptied"], b.count(GROUPS * UNITS, UNITS * grp + u - 1))
                if grp == 0 and u == 0:
                    pe.wait_ge(S["stack_loaded"], b.count(192, 192))
                    pe.wait_ge(S["mrow_loaded"], b.count(16, 16))
                todo = [(u, 0, 0)] if u < 4 else [(u - 4, 1, 0), (u - 4, 3, 384)] if u < 8 else \
                    [(2 * (u - 8), 2, 0), (2 * (u - 8) + 1, 2, 256)]
                if u < 4:
                    diag = ps_e[:, bank, 0:P].rearrange("p (a c) -> p a c", a=1)
                else:
                    step = 384 if u < 8 else 256
                    diag = ps_e[:, bank, :].rearrange("p (a c) -> p a c", c=P)[:, 0:step // P + 1:step // P, :]
                mm(diag, negmask[:, :], bcast(identb[:, :], 1, len(todo)), start=True, stop=False, skip_group_check=True)
                for hh, j, at in todo:
                    hd = GH * grp + hh
                    last = mm(ps_e[:, bank, at:at + TOK - P * j], k[:, hd, tok(j)], q[:, hd, P * j:TOK],
                              start=False, stop=True, skip_group_check=True)
                last.then_inc(S["e_filled"], 1)

            def s_unit(b, grp, u):
                q, k = qst[b.parity], kst[b.parity]
                bank = u % 2
                after(pe, S["s_emptied"], b.count(GROUPS * UNITS, UNITS * grp + u - 1))
                if grp == 0 and u == 0:
                    pe.wait_ge(S["stack_loaded"], b.count(192, 192))
                    after(pe, S["mrow_ready"], b.count(1, 0))
                diag = u < NT
                if diag:
                    mm(ps_s[:, bank, :].rearrange("p (a c) -> p a c", a=GH), identb[:, :], bcast(negmask[:, :], 1, GH),
                       start=True, stop=False, skip_group_check=True)
                i, keys, hds = S_UNIT[u]
                for n, hh in enumerate(hds):
                    w = keys[1] - keys[0]
                    hd = GH * grp + hh
                    last = mm(ps_s[:, bank, w * n:w * (n + 1)], q[0:MAXROW, hd, tok(i)], k[0:MAXROW, hd, keys[0]:keys[1]],
                              start=(n == 0 and not diag), stop=True, skip_group_check=True)
                last.then_inc(S["s_filled"], 1)

            def pv(b, grp, piece):
                if piece == 0:
                    after(pe, S["v_emptied"], b.count(2 * GROUPS, 2 * grp))
                    if grp == 0:
                        pe.wait_ge(S["a_emptied"], b.count(A_FILLS, a_number(b, A_V) + 1))
                pe.wait_ge(S["e_emptied"], b.count(GROUPS * UNITS, UNITS * grp + (4, 8, 10)[piece]))
                for j, u0, at in (((0, 0, 0),), ((1, 4, 0), (3, 4, 384)), ((2, 8, 0),))[piece]:
                    for hh in range(GH):
                        u, o = (u0 + hh, at) if j != 2 else (u0 + hh // 2, 256 * (hh % 2))
                        last = mm(ps_v[32 * hh:32 * hh + 32, P * j:TOK], vaug[:, j, GH * grp + hh, :],
                                  prob[:, u, o:o + TOK - P * j], start=(j == 0), stop=(j == 2), skip_group_check=True)
                last.then_inc(S["pv_used"], 1)

            def yt(b, grp):
                pe.wait_ge(S["v_emptied"], b.count(2 * GROUPS, 2 * grp + 1))
                for i in range(NT):
                    last = tr(ps_v[:, tok(i)], yT[:, tok(i)], ident[:, :])
                last.then_inc(S["yt_filled"], 1)

            def c_xn2t(b):
                c0_fill(b, C0_XN2T)
                pe.wait_ge(S["norm1"], b.count(NT, NT))
                for i in range(NT):
                    last = tr(ps_c0[:, tok(i)], xn2[:, i, :], ident[:, :])
                last.then_inc(S["c0_filled"], 1)

            def c_ht(b):
                c1_fill(b, C1_HT)
                pe.wait_ge(S["norm2"], b.count(NT, NT))
                for i in range(NT):
                    last = tr(ps_c1[:, tok(i)], hn[:, i, :], ident[:, :])
                last.then_inc(S["c1_filled"], 1)

            def c_kt(b):
                c0_fill(b, C0_KT)
                pe.wait_ge(S["c1_emptied"], b.count(C1_FILLS, C1_HT + 1))
                mm(ps_c0[:, :], wkT[:, :], hT[:, :], start=True, stop=True).then_inc(S["c0_filled"], 1)

            def c_qt(b):
                c1_fill(b, C1_QT)
                mm(ps_c1[:, :], wqT[:, :], hT[:, :], start=True, stop=True).then_inc(S["c1_filled"], 1)

            def c_vk(b):
                for bank, fill, filled, n in ((ps_c0, c0_fill, "c0_filled", C0_VK), (ps_c1, c1_fill, "c1_filled", C1_VK)):
                    fill(b, n)
                    for m in range(2):
                        i = m if bank is ps_c0 else 2 + m
                        last = mm(bank[:, VK * m:VK * (m + 1)], hT[:, tok(i)], wvk[:, :], start=True, stop=True)
                    last.then_inc(S[filled], 1)

            def c_gram(b):
                c0_fill(b, C0_GRAM)
                for i in range(NT):
                    last = mm(ps_c0[:, tok(i)], kT[:, tok(i)], kT[:, tok(i)], start=True, stop=True)
                last.then_inc(S["c0_filled"], 1)
                c1_fill(b, C1_KQ)
                for i in range(NT):
                    last = mm(ps_c1[:, tok(i)], kT[:, tok(i)], qT[:, tok(i)], start=True, stop=True)
                last.then_inc(S["c1_filled"], 1)

            def lev_a(b, lv):
                c0_fill(b, c0_a(lv))
                pe.wait_ge(S["pair_ready"], b.count(LEVELS - 1, lv))
                if lv == 1:
                    pe.wait_ge(S["inv1_ready"], b.count(2, 2))
                for i in range(NT):
                    last = mm(ps_c0[:, tok(i)], pair_up[lv % 2][:, i, :], inv[lv % 2][:, i, :], start=True, stop=True)
                last.then_inc(S["c0_filled"], 1)

            def lev_d(b, lv):
                c1_fill(b, c1_dt(lv))
                pe.wait_ge(S["c0_emptied"], b.count(C0_FILLS, c0_a(lv) + 1))
                for i in range(NT):
                    last = mm(ps_c1[:, tok(i)], ablk[:, i, :], invT[lv % 2][:, i, :], start=True, stop=True)
                last.then_inc(S["c1_filled"], 1)
                if lv < LEVELS - 1:
                    c0_fill(b, c0_d(lv))
                    for i in range(NT):
                        last = mm(ps_c0[:, tok(i)], invT[lv % 2][:, i, :], ablk[:, i, :], start=True, stop=True)
                    last.then_inc(S["c0_filled"], 1)

            def c_ffn(b):
                c1_fill(b, C1_FFN)
                for i in range(NT):
                    last = mm(ps_c1[:, tok(i)], xn2T[:, tok(i)], sgT[:, :], start=True, stop=True)
                last.then_inc(S["c1_filled"], 1)

            def c_r(b, c):
                c0_fill(b, c0_r(c))
                mm(ps_c0[:, 0:P], kT[:, tok(c)], state[:, :], start=True, stop=True).then_inc(S["c0_filled"], 1)

            def c_u(b, c):
                c0_fill(b, c0_u(c))
                if c == 0:
                    pe.wait_ge(S["c1_emptied"], b.count(C1_FILLS, c1_dt(LEVELS - 1) + 1))
                mm(ps_c0[:, 0:P], invT[LEVELS % 2][:, c, :], vk[:, 0, 0:P] if c == 0 else rhs[:, :], start=True, stop=True)\
                    .then_inc(S["c0_filled"], 1)

            def c_y(b, c):
                if c == 0:
                    c1_fill(b, C1_Y)
                pe.wait_ge(S["c0_emptied"], b.count(C0_FILLS, c0_u(c) + 1))
                if c > 0:
                    mm(ps_c1[:, tok(c)], qT[:, tok(c)], state[:, :], start=False, stop=False, skip_group_check=True)
                last = mm(ps_c1[:, tok(c)], kq[:, c, :], u_sb[:, :], start=(c == 0), stop=True, skip_group_check=True)
                if c == NT - 1:
                    last.then_inc(S["c1_filled"], 1)
                else:
                    mm(ps_c0[0:DS, 0:P], vk[:, c, P:VK], u_sb[:, :], start=True, stop=True).then_inc(S["c0_filled"], 1)

            pieces = {"xnt": xnt, "q": lambda b: qk(b, 0), "k": lambda b: qk(b, 1), "v": v, "logits": logits, "gt": gt,
                      "out": out_piece, "m_rows": m_rows, "pv0": lambda b, grp: pv(b, grp, 0), "pv1": lambda b, grp: pv(b, grp, 1), "pv2": lambda b, grp: pv(b, grp, 2), "yt": yt, "c_xn2t": c_xn2t, "c_ht": c_ht, "c_kt": c_kt,
                      "c_qt": c_qt, "c_vk": c_vk, "c_gram": c_gram, "c_ffn": c_ffn}
            for c in range(NC):
                pieces[f"h{c}"] = lambda b, c=c: h(b, c)
                pieces[f"gb{c}"] = lambda b, c=c: gb(b, c)
            for lv in range(1, LEVELS):
                pieces[f"lev_a{lv}"] = lambda b, lv=lv: lev_a(b, lv)
                pieces[f"lev_d{lv}"] = lambda b, lv=lv: lev_d(b, lv)
            for c in range(NT):
                pieces[f"c_r{c}"] = lambda b, c=c: c_r(b, c)
                pieces[f"c_u{c}"] = lambda b, c=c: c_u(b, c)
                pieces[f"c_y{c}"] = lambda b, c=c: c_y(b, c)
            run(pe, pieces, unit)

        @block.scalar
        def _(act):
            af = nc.scalar.activation
            copy = nc.scalar.copy
            sqrt_hd = float(HD) ** 0.5
            for n in names:
                if n not in ONCE:
                    act.sem_inc(S[n], 1)
            act.wait_ge(S["loaded"], LOADED)
            af(cent_sq[:, :], nat["cent"][:, :], ACT.Square, accum_out=cent_ss[:, :]).then_inc(S["ss_ready"], 1)

            def prep(n, dst, src, scale=None):
                act.wait_ge(S["prep_pe"], n)
                (copy(dst, src) if scale is None else nc.scalar.mul(dst, src, scale)).then_inc(S["prep_out"], 1)

            perm = lambda w: w.rearrange("c (h d) -> c d h", d=HD)
            perm_out = lambda w: w.rearrange("c (d h) -> c d h", d=HD)
            prep(1, uqT[:, :], ps_a[0:QL, 0:P])
            prep(2, oT[:, :], ps_c0[:, 0:P])
            prep(3, wqeT[:, :], ps_c1[:, 0:P])
            prep(4, perm_out(w_q[:, :]), perm(ps_a[:, 0:P]), 1.0 / sqrt_hd)
            prep(5, veff[:, :], ps_c0[0:KVL, 0:P])
            prep(6, keffT[:, :], ps_c1[0:KVL, 0:P])
            prep(7, w_v[:, :], ps_c0[:, 0:P])
            prep(8, perm_out(w_k[:, :]), perm(ps_a[:, 0:P]))
            prep(9, wkT[:, 0:DS], ps_c0[:, 0:DS])
            prep(9, wvk[:, P:P + DS], ps_c0[:, 0:DS])
            prep(10, wqT[:, 0:DS], ps_c1[:, 0:DS])
            prep(11, vecT[:, :], ps_v[:, 0:NC + 4])
            act.wait_ge(S["prep_out"], 12)
            nc.scalar.mul(bq_lr[:, :], vecT[:, NC + 3:NC + 4], LR).then_inc(S["prep_out"], 1)
            prep(12, wvk[:, 0:P], ps_a[:, 0:P])
            act.wait_ge(S["prep_pe"], 13)
            af(sgT[:, :], ps_c0[:, 0:P], ACT.Sign).then_inc(S["prep_sign"], 1)
            act.wait_ge(S["prep_sign"], 1)
            nc.scalar.mul(sgT[:, :], sgT[:, :], 0.5).then_inc(S["prep_out"], 1)
            prep(14, vkbias[:, :], ps_c1[:, 0:VK])
            act.wait_ge(S["rn_ready"], 1)
            nc.scalar.mul(rw[0:EXPERTS, :], nat["cent"][:, :], cent_rn[:, 1:2]).then_inc(S["prep_out"], 1)
            prep(15, rwT[:, :], ps_a[:, 0:2 * EXPERTS])

            def a_full(b, n):
                act.wait_ge(S["a_filled"], b.count(A_FILLS, a_number(b, n) + 1))

            def c0_full(b, n):
                act.wait_ge(S["c0_filled"], b.count(C0_FILLS, n + 1))

            def c1_full(b, n):
                act.wait_ge(S["c1_filled"], b.count(C1_FILLS, n + 1))

            def xnt(b):
                a_full(b, A_XNT)
                copy(xnT[b.parity][:, :], ps_a[:, :]).then_inc(S["a_emptied"], 1)
                after(act, S["rn_ready"], b.count(1, 0))
                for i in range(NT):
                    af(tG[:, i * P:(i + 1) * P], xn[:, i, :], ACT.Square, accum_out=ss[:, i:i + 1]).then_inc(S["ss_ready"], 1)

            def split_hi(b, n):
                a_full(b, A_Q + n)
                after(act, S["scratch_written"], b.count(32, 0))
                copy(parts[n][:, 0, :], ps_a[:, :]).then_inc(S["hi_ready"], 1)

            def v(b):
                a_full(b, A_V)
                after(act, S["pv_used"], b.count(3 * GROUPS, 0))
                copy(vaug[:, :, :, 0:HD], ps_a[:, :].rearrange("p (i h d) -> p i h d", i=NT, h=HEADS))\
                    .then_inc(S["a_emptied"], 1)

            def gates(b):
                act.wait_ge(S["dlt_ready"], b.count(1, 1))
                af(ex[:, :, :], dlt[:, :, :], ACT.Exp).then_inc(S["ex_ready"], 1)

            def gt(b):
                a_full(b, A_GT)
                copy(gT[0:PARTS * EXPERTS, :], ps_a[:, :].bitcast(BF16)[0:PARTS * EXPERTS, 0:TOK]).then_inc(S["a_emptied"], 1)

            def h(b, c):
                a_full(b, A_H + c)
                after(act, S["gelu_ready"], b.count(1, 0))
                af(hid[:, c, :], ps_a[:, :], ACT.Identity, bias=vecT[:, c:c + 1]).then_inc(S["a_emptied"], 1)

            def gelu(b):
                act.wait_ge(S["a_emptied"], b.count(A_FILLS, a_number(b, A_H + NC)))
                af(hid[:, :, :], hid[:, :, :], ACT.Gelu).then_inc(S["gelu_ready"], 1)

            def out_piece(b):
                a_full(b, A_OUT)
                af(tG[:, :], ps_a[:, :], ACT.Tanh).then_inc(S["tg_ready"], 1)

            def m_rows(b):
                act.wait_ge(S["mrow_filled"], b.count(1, 1))
                after(act, S["mscratch_written"], b.count(16, 0))
                copy(mrow[:, :], ps_s[:, 0, :].bitcast(BF16)[0:PARTS * 32, 0:TOK]).then_inc(S["mrow_ready"], 1)

            def unit(cur, nxt, grp, u):
                if cur is None:
                    return
                act.wait_ge(S["e_filled"], cur.count(GROUPS * UNITS, UNITS * grp + u + 1))
                if u in (0, 4, 8):
                    after(act, S["pv_used"], cur.count(3 * GROUPS, 3 * (grp - 1) + u // 4 + 1))
                af(prob[:, u, :], ps_e[:, u % 2, :], ACT.Exp).then_inc(S["e_emptied"], 1)

            def pv(b, grp):
                act.wait_ge(S["pv_used"], b.count(3 * GROUPS, 3 * grp + 3))
                copy(yT[:, :], ps_v[:, :]).then_inc(S["v_emptied"], 1)

            def c_xn2t(b):
                c0_full(b, C0_XN2T)
                copy(xn2T[:, :], ps_c0[:, :]).then_inc(S["c0_emptied"], 1)

            def c_ht(b):
                c1_full(b, C1_HT)
                af(hT[:, :], ps_c1[:, :], ACT.Identity, bias=vecT[:, NC + 1:NC + 2], scale=vecT[:, NC:NC + 1]).then_inc(S["c1_emptied"], 1)

            def c_kt(b):
                c0_full(b, C0_KT)
                af(kT[:, :], ps_c0[:, :], ACT.Identity, bias=vecT[:, NC + 2:NC + 3]).then_inc(S["c0_emptied"], 1)

            def c_qt(b):
                c1_full(b, C1_QT)
                af(qT[:, :], ps_c1[:, :], ACT.Identity, bias=bq_lr[:, :], scale=LR).then_inc(S["c1_emptied"], 1)

            def c_gram(b):
                c0_full(b, C0_GRAM)
                copy(gram[:, :, :].rearrange("p i d -> p (i d)"), ps_c0[:, :]).then_inc(S["c0_emptied"], 1)

            def lev_a(b, lv):
                c0_full(b, c0_a(lv))
                copy(ablk[:, :, :].rearrange("p i d -> p (i d)"), ps_c0[:, :]).then_inc(S["c0_emptied"], 1)

            def c_ffn(b):
                c1_full(b, C1_FFN)
                after(act, S["syg_ready"], b.count(1, 0))
                af(tF[:, :], ps_c1[:, :], ACT.Tanh).then_inc(S["tf_ready"], 1)

            def c_u(b, c):
                c0_full(b, c0_u(c))
                copy(u_sb[:, :], ps_c0[:, 0:P]).then_inc(S["c0_emptied"], 1)

            pieces = {"xnt": xnt, "q": lambda b: split_hi(b, 0), "k": lambda b: split_hi(b, 1), "v": v, "gates": gates, "gt": gt,
                      "gelu": gelu, "out": out_piece, "m_rows": m_rows, "pv2": pv, "c_xn2t": c_xn2t, "c_ht": c_ht, "c_kt": c_kt,
                      "c_qt": c_qt, "c_gram": c_gram, "c_ffn": c_ffn}
            for c in range(NC):
                pieces[f"h{c}"] = lambda b, c=c: h(b, c)
                pieces[f"c_u{c}"] = lambda b, c=c: c_u(b, c)
            for lv in range(1, LEVELS):
                pieces[f"lev_a{lv}"] = lambda b, lv=lv: lev_a(b, lv)
            run(act, pieces, unit)

        @block.vector
        def _(dve):
            vec = nc.vector
            for p in range(2):
                vec.memset(qst[p][64:P, :, :].bitcast(F32), 0.0)
            vec.memset(vaug[:, :, :, :], 0.0).then_inc(S["vaug_zeroed"], 1)
            dve.wait_ge(S["loaded"], LOADED)
            vec.tensor_scalar(w2s[:, :, :], w2s[:, :, :], 0.5, None, ALU.mult).then_inc(S["prep_out2"], 1)
            vec.tensor_scalar(b2r[:, 0, :], b2f[:, :], 0.5, None, ALU.mult).then_inc(S["prep_out2"], 1)
            dve.wait_ge(S["prep_out2"], 2)
            vec.tensor_copy(b2p[:, 0, :], b2r[:, 0, :]).then_inc(S["prep_out2"], 1)
            dve.wait_ge(S["prep_out2"], 3)
            vec.tensor_tensor(b2r[:, 1, :], b2r[:, 0, :], b2p[:, 0, :], ALU.subtract).then_inc(S["prep_out2"], 1)
            dve.wait_ge(S["prep_out2"], 4)
            vec.tensor_copy(b2p[:, 1, :], b2r[:, 1, :]).then_inc(S["prep_out2"], 1)
            dve.wait_ge(S["prep_out2"], 5)
            vec.tensor_tensor(b2p[:, 2, :], b2r[:, 1, :], b2p[:, 1, :], ALU.subtract).then_inc(S["prep_out2"], 1)
            dve.wait_ge(S["const_ready"], 4)
            dve.wait_ge(S["prep_out"], PREP_OUT)

            def a_full(b, n):
                dve.wait_ge(S["a_filled"], b.count(A_FILLS, a_number(b, n) + 1))

            def c0_full(b, n):
                dve.wait_ge(S["c0_filled"], b.count(C0_FILLS, n + 1))

            def c1_full(b, n):
                dve.wait_ge(S["c1_filled"], b.count(C1_FILLS, n + 1))

            def ln_stats(n, b):
                if n == 0:
                    dve.wait_ge(S["x_loaded"], b.count(16, 16))
                    src = xn
                elif n == 1:
                    dve.wait_ge(S["x1_ready"], b.count(1, 1))
                    src = x1[b.parity]
                else:
                    dve.wait_ge(S["norm1"], b.count(NT, NT))
                    src = xn2
                for i in range(NT):
                    vec.bn_stats(stats[n][:, i, :], src[:, i, :]).then_inc(S[f"stats{n}"], 1)
                settled(dve, S[f"stats{n}"], b.count(NT, NT))
                for i in range(NT):
                    vec.bn_aggr(mv[n][:, i, :], stats[n][:, i, :]).then_inc(S[f"mv{n}"], 1)

            def ln_norm(n, b):
                src, dst = ((xn, xn), (x1[b.parity], xn2), (xn2, hn))[n]
                dve.wait_ge(S[f"rstd{n}"], b.count(1, 1))
                if n == 0:
                    pass
                elif n == 1:
                    after(dve, S["c1_emptied"], b.count(C1_FILLS, 0))
                else:
                    after(dve, S["c1_filled"], b.count(C1_FILLS, 0))
                for i in range(NT):
                    vec.tensor_scalar(dst[:, i, :], src[:, i, :], mv[n][:, i, 0:1], rstd[n][:, i:i + 1], ALU.subtract, ALU.mult)\
                        .then_inc(S[f"norm{n}"], 1)

            def split_rest(b, n):
                dve.wait_ge(S["hi_ready"], b.count(2, n + 1))
                after(dve, S["parts_ready"], b.count(2, 0))
                vec.tensor_tensor(rest[n], ps_a[:, :], parts[n][:, 0, :], ALU.subtract).then_inc(S["a_emptied"], 1)

            def logits(b):
                a_full(b, A_LOGIT)
                dve.wait_ge(S["rn_ready"], b.count(1, 1))
                lg = ps_a[:, 0:2 * EXPERTS * NT].rearrange("p (i e) -> p i e", i=NT)
                vec.tensor_tensor(coss[:, :, :], lg[:, :, 0:EXPERTS], bcast(rn[:, :], 2, EXPERTS), ALU.mult).then_inc(S["cos_ready"], 1)
                dve.wait_ge(S["cos_ready"], b.count(1, 1))
                vec.tensor_tensor(logit[:, :, :], lg[:, :, EXPERTS:2 * EXPERTS], coss[:, :, :], ALU.add).then_inc(S["a_emptied"], 1)
                settled(dve, S["a_emptied"], b.count(A_FILLS, a_number(b, A_LOGIT) + 1))
                for i in range(NT):
                    vec.max(top8[:, i, :], logit[:, i, :]).then_inc(S["top_ready"], 1)

            def gates(b):
                dve.wait_ge(S["top_ready"], b.count(NT, NT))
                vec.tensor_tensor(dlt[:, :, :], logit[:, :, :], top8[:, :, 0:1].to_broadcast([P, NT, EXPERTS]), ALU.subtract)\
                    .then_inc(S["dlt_ready"], 1)
                vec.tensor_tensor(keep[:, :, :], logit[:, :, :], top8[:, :, 1:2].to_broadcast([P, NT, EXPERTS]), ALU.is_ge)\
                    .then_inc(S["keep_ready"], 1)
                dve.wait_ge(S["keep_ready"], b.count(1, 1))
                dve.wait_ge(S["ex_ready"], b.count(1, 1))
                vec.tensor_tensor(gm[:, :, :], ex[:, :, :], keep[:, :, :], ALU.mult).then_inc(S["gm_ready"], 1)
                dve.wait_ge(S["gm_ready"], b.count(1, 1))
                vec.tensor_reduce(gsum[:, :], gm[:, :, :], AX_X, ALU.add).then_inc(S["gsum_ready"], 1)
                dve.wait_ge(S["gsum_ready"], b.count(1, 1))
                vec.reciprocal(grec[:, :], gsum[:, :]).then_inc(S["grec_ready"], 1)
                dve.wait_ge(S["grec_ready"], b.count(1, 1))
                vec.tensor_tensor(gate[:, :, :], gm[:, :, :], bcast(grec[:, :], 2, EXPERTS), ALU.mult).then_inc(S["gate_ready"], 1)

            def gb(b, c):
                a_full(b, A_GB + c)
                dve.wait_ge(S["gelu_ready"], b.count(1, 1))
                vec.tensor_tensor(hid[:, c, :], hid[:, c, :], ps_a[:, :], ALU.mult).then_inc(S["a_emptied"], 1)

            def out_piece(b):
                dve.wait_ge(S["tg_ready"], b.count(1, 1))
                after(dve, S["attg_ready"], b.count(1, 0))
                vec.scalar_tensor_tensor(out=gate_out[:, :, :].rearrange("p i d -> p (i d)"), in0=tG[:, :], scalar=1.0,
                                         in1=ps_a[:, :], op0=ALU.add, op1=ALU.mult).then_inc(S["a_emptied"], 1)

            def unit(cur, nxt, mgrp, u):
                if nxt is None:
                    return
                i, keys, hds = S_UNIT[u]
                if mgrp == 0 and u == 0:
                    after(dve, S["nm_ready"], nxt.count(1, 0))
                dve.wait_ge(S["s_filled"], nxt.count(GROUPS * UNITS, UNITS * mgrp + u + 1))
                h0 = GH * mgrp + hds[0]
                vec.tensor_reduce(cand[:, i, h0:h0 + len(hds), S_SLOT[u]],
                                  ps_s[:, u % 2, :].rearrange("p (a c) -> p a c", a=len(hds)), AX_X, ALU.max)\
                    .then_inc(S["s_emptied"], 1)

            def m_parts(b):
                dve.wait_ge(S["s_emptied"], b.count(GROUPS * UNITS, GROUPS * UNITS))
                after(dve, S["mparts_ready"], b.count(1, 0))
                vec.tensor_reduce(nm[:, :, :], cand[:, :, :, :], AX_X, ALU.max, negate=True).then_inc(S["nm_ready"], 1)

            def yt(b, grp):
                dve.wait_ge(S["yt_filled"], b.count(GROUPS, grp + 1))
                y = ps_v[:, :].rearrange("p (i h e) -> p i h e", i=NT, h=GH)
                if grp == 0:
                    after(dve, S["x1_ready"], b.count(1, 0))
                after(dve, S["v_emptied"], b.count(2 * GROUPS, 2 * grp))
                vec.reciprocal(rden[:, :, :], y[:, :, :, HD]).then_inc(S["rden_ready"], 1)
                dve.wait_ge(S["rden_ready"], b.count(GROUPS, grp + 1))
                w = GH * HD
                vec.tensor_tensor(att[:, :, w * grp:w * (grp + 1)].rearrange("p i (h d) -> p i h d", h=GH), y[:, :, :, 0:HD],
                                  bcast(rden[:, :, :], 3, HD), ALU.mult).then_inc(S["v_emptied"], 1)

            def c_vk(b):
                bias = bcast(vkbias[:, :], 1, 2)
                c0_full(b, C0_VK)
                vec.tensor_tensor(vk[:, 0:2, :], ps_c0[:, 0:2 * VK].rearrange("p (i d) -> p i d", i=2), bias, ALU.add).then_inc(S["c0_emptied"], 1)
                c1_full(b, C1_VK)
                vec.tensor_tensor(vk[:, 2:4, :], ps_c1[:, 0:2 * VK].rearrange("p (i d) -> p i d", i=2), bias, ALU.add).then_inc(S["c1_emptied"], 1)

            def c_gram(b):
                c1_full(b, C1_KQ)
                vec.tensor_tensor(kq[:, :, :], ps_c1[:, :].rearrange("p (i d) -> p i d", i=NT), bcast(strict[:, :], 1, NT), ALU.mult)\
                    .then_inc(S["c1_emptied"], 1)

            def lev_d(b, lv):
                old, new = lv % 2, (lv + 1) % 2
                flat = lambda t: t[:, :, :].rearrange("p i d -> p (i d)")
                if lv == 1:
                    dve.wait_ge(S["inv1_ready"], b.count(2, 2))
                c1_full(b, c1_dt(lv))
                vec.tensor_tensor(flat(invT[new]), flat(invT[old]), ps_c1[:, :], ALU.subtract).then_inc(S["c1_emptied"], 1)
                if lv < LEVELS - 1:
                    c0_full(b, c0_d(lv))
                    vec.tensor_tensor(flat(inv[new]), flat(inv[old]), ps_c0[:, :], ALU.subtract).then_inc(S["c0_emptied"], 1)

            def c_ffn(b):
                dve.wait_ge(S["tf_ready"], b.count(1, 1))
                after(dve, S["syg_ready"], b.count(1, 0))
                vec.scalar_tensor_tensor(out=tF[:, :], in0=tF[:, :], scalar=1.0, in1=ps_c1[:, :], op0=ALU.add, op1=ALU.mult)\
                    .then_inc(S["c1_emptied"], 1)

            def c_r(b, c):
                c0_full(b, c0_r(c))
                vec.scalar_tensor_tensor(out=rhs[:, :], in0=ps_c0[:, 0:P], scalar=-LR, in1=vk[:, c, 0:P], op0=ALU.mult, op1=ALU.add)\
                    .then_inc(S["c0_emptied"], 1)

            def c_y(b, c):
                if c == 0:
                    c0_full(b, c0_s(c))
                    vec.tensor_copy(state[0:DS, :], ps_c0[0:DS, 0:P]).then_inc(S["c0_emptied"], 1)
                elif c < NT - 1:
                    c0_full(b, c0_s(c))
                    vec.tensor_tensor(state[0:DS, :], state[0:DS, :], ps_c0[0:DS, 0:P], ALU.add).then_inc(S["c0_emptied"], 1)
                else:
                    c1_full(b, C1_Y)
                    after(dve, S["syg_ready"], b.count(1, 0))
                    vec.tensor_tensor(sy[:, :, :], ps_c1[:, :].rearrange("p (i d) -> p i d", i=NT), xn2[:, :, :], ALU.add)\
                        .then_inc(S["c1_emptied"], 1)

            pieces = {"ln1_stats": lambda b: ln_stats(0, b), "ln2_stats": lambda b: ln_stats(1, b), "ln3_stats": lambda b: ln_stats(2, b),
                      "ln1_norm": lambda b: ln_norm(0, b), "ln2_norm": lambda b: ln_norm(1, b), "ln3_norm": lambda b: ln_norm(2, b),
                      "q": lambda b: split_rest(b, 0), "k": lambda b: split_rest(b, 1), "logits": logits, "gates": gates,
                      "out": out_piece, "m_parts": m_parts, "yt": yt, "c_vk": c_vk, "c_gram": c_gram, "c_ffn": c_ffn}
            for c in range(NC):
                pieces[f"gb{c}"] = lambda b, c=c: gb(b, c)
                pieces[f"c_r{c}"] = lambda b, c=c: c_r(b, c)
                pieces[f"c_y{c}"] = lambda b, c=c: c_y(b, c)
            for lv in range(1, LEVELS):
                pieces[f"lev_d{lv}"] = lambda b, lv=lv: lev_d(b, lv)
            run(dve, pieces, unit)


ONCE = ("const_ready", "mask_step", "loaded", "prep_pe", "prep_out", "prep_out2", "prep_sign", "small_zeroed", "kst_zeroed", "vaug_zeroed",
        "ss_ready", "rn_ready")
PREP_OUT = 18
S_UNIT = [(i, (P * i, P * i + P), (0, 1, 2, 3)) for i in range(4)] + [
    (1, (0, 128), (0, 1, 2, 3)), (2, (0, 256), (0, 1)), (2, (0, 256), (2, 3)),
    (3, (0, 256), (0, 1)), (3, (0, 256), (2, 3)), (3, (256, 384), (0, 1, 2, 3))]
S_SLOT = [0, 0, 0, 0, 1, 1, 1, 1, 1, 2]

_INS = ["L0_attn_x", "L0_attn_W_dq", "L0_attn_W_uq", "L0_attn_W_dkv", "L0_attn_W_uk", "L0_attn_W_uv", "L0_attn_W_o",
        "L0_ffn_w1", "L0_ffn_b1", "L0_ffn_w2", "L0_ffn_b2", "L0_ffn_centroids", "L0_ffn_w_route",
        "L1_attn_Wk", "L1_attn_bk", "L1_attn_Wv", "L1_attn_bv", "L1_attn_Wq", "L1_attn_bq", "L1_attn_gamma", "L1_attn_beta",
        "L1_ffn_weight"]


def kernel(**inputs):
    import numpy as _np
    import concourse.bacc as _bacc
    from concourse import mybir as _mybir
    from concourse.bass_utils import run_bass_kernel_spmd as _run

    nc = _bacc.Bacc("TRN2", target_bir_lowering=False, num_devices=1)
    arrays, args = {}, []
    for name in _INS:
        a = _np.ascontiguousarray(inputs[name])
        arrays[f"in_{name}_dram"] = a
        args.append(nc.dram_tensor(f"in_{name}_dram", a.shape, _mybir.dt.from_np(a.dtype), kind="ExternalInput").ap())
    shape = tuple(inputs["L0_attn_x"].shape)
    args.append(nc.dram_tensor("out_dram", shape, _mybir.dt.float32, kind="ExternalOutput").ap())
    nc.disable_value_cache = True
    two_layers(nc, *args)
    r = _run(nc, [arrays], core_ids=[0])
    return r.results[0]["out_dram"]
```

```python
from contextlib import ExitStack

import concourse.bass as bass
from concourse import mybir

ALU = mybir.AluOpType
ACT = mybir.ActivationFunctionType
F32 = mybir.dt.float32
BF16 = mybir.dt.bfloat16
AX_X = mybir.AxisListType.X

P = 128
HEADS, HD = 16, 8
EXPERTS, HID = 8, 64
DS = 64
VK = 128 + DS
LR = 0.01
LN_EPS = 1e-5
NORM_EPS = 1e-12
NEG = -1e30
PARTS = 3
PAIRS = PARTS * PARTS * HD
FINE = 32
MAXROW = 96
HALF_HEADS = 8
GROUPS, GH = 4, 4
UNITS = 10
ONES = 1 + 0x3F80 / 2 ** 23
LEVELS = 7

A_FILLS = 17
A_XNT, A_Q, A_K = -11, -10, -9
A_LOGIT, A_GT, A_M0, A_H, A_V = 3, 4, 5, 9, 13
A_GB, A_M1, A_OUT = 14, 18, 19
C0_FILLS, C1_FILLS = 25, 12
C0_XN2T, C0_KT, C0_VK, C0_GRAM = 0, 1, 2, 3
C1_HT, C1_QT, C1_VK, C1_KQ, C1_FFN, C1_Y = 0, 1, 2, 3, 4, 11


def c0_a(k):
    return 4 + 2 * (k - 1)


def c0_d(k):
    return 5 + 2 * (k - 1)


def c1_dt(k):
    return 5 + (k - 1)


def c0_r(c):
    return 17 + 3 * (c - 1)


def c0_u(c):
    return 15 if c == 0 else 18 + 3 * (c - 1)


def c0_s(c):
    return 16 if c == 0 else 19 + 3 * (c - 1)


PLAN = {
    (0, 0): ["c_y2"], (0, 1): ["c_r3", "gb0"], (0, 2): ["ln2_stats", "c_u3"], (0, 3): ["c_y3"], (0, 4): ["gb1", "ln2_norm"],
    (0, 6): ["pv0", "c_xn2t", "ln3_stats", "c_out", "gb2"], (0, 7): ["ln3_norm"], (0, 8): ["gb3"], (0, 9): ["pv1", "c_ht"],
    (1, 0): ["load_x", "c_kt", "c_qt", "m_rows1"], (1, 1): ["c_vk", "out"], (1, 2): ["c_gram", "pv2"], (1, 3): ["logits"],
    (1, 4): ["yt", "c_ffn", "gates"], (1, 5): ["lev_a1"], (1, 6): ["pv0"], (1, 7): ["lev_d1"], (1, 8): ["gt"],
    (1, 9): ["pv1", "lev_a2"], (2, 0): ["ln1_stats", "lev_d2", "m_parts0"], (2, 2): ["ln1_norm", "lev_a3", "pv2"], (2, 3): ["lev_d3"],
    (2, 4): ["yt", "m_rows0", "zero"], (2, 5): ["lev_a4", "xnt"], (2, 6): ["pv0", "q", "lev_d4"], (2, 8): ["lev_a5", "k"],
    (2, 9): ["pv1", "lev_d5"], (3, 0): ["stacks0", "h0"], (3, 1): ["lev_a6"], (3, 2): ["h1", "lev_d6", "pv2"], (3, 3): ["c_u0"],
    (3, 4): ["h2", "yt", "c_y0"], (3, 5): ["c_r1"], (3, 6): ["pv0", "c_u1"], (3, 7): ["c_y1", "h3"], (3, 8): ["c_r2"],
    (3, 9): ["pv1", "c_u2"], (4, 0): ["m_parts1", "gelu", "stacks1"], (4, 1): ["pv2"], (4, 2): ["v"], (4, 3): ["yt", "x1"],
}
LAST_PLAN = {
    (0, 0): ["last:zero_state", "c_y2"], (0, 1): ["c_r3"], (0, 2): ["gb0", "ln2_stats", "c_u3"], (0, 3): ["c_y3"], (0, 4): ["gb1"],
    (0, 5): ["ln2_norm", "c_out"], (0, 6): ["pv0", "gb2"], (0, 8): ["gb3"], (0, 9): ["pv1", "c_xn2t", "ln3_stats"],
    (1, 0): ["m_rows1"], (1, 1): ["out"], (1, 2): ["pv2"], (1, 4): ["yt", "ln3_norm"], (1, 6): ["pv0"], (1, 7): ["c_ht"],
    (1, 9): ["pv1"], (2, 0): ["c_kt", "c_qt"], (2, 2): ["pv2"], (2, 3): ["c_vk"], (2, 4): ["yt"], (2, 5): ["c_gram"], (2, 6): ["pv0"],
    (2, 8): ["c_ffn"], (2, 9): ["pv1"], (3, 2): ["pv2"], (3, 4): ["yt"], (3, 6): ["pv0"], (3, 9): ["pv1"], (4, 0): ["lev_a1"],
    (4, 1): ["lev_d1"], (4, 2): ["pv2", "lev_a2"], (4, 3): ["yt", "x1", "lev_d2"], (4, 4): ["lev_a3"],
    (4, 5): ["lev_d3", "last:ln2_stats"], (4, 6): ["lev_a4", "last:ln2_norm"], (4, 7): ["lev_d4", "last:c_xn2t"],
    (4, 8): ["lev_a5", "last:ln3_stats"], (4, 9): ["lev_d5", "last:ln3_norm"], (5, 0): ["lev_a6", "last:c_ht"], (5, 1): ["lev_d6"],
    (5, 2): ["c_u0", "last:c_kt", "last:c_qt"], (5, 3): ["c_y0", "last:c_vk"], (5, 4): ["c_r1", "last:c_gram"],
    (5, 5): ["c_u1", "last:c_ffn"], (5, 6): ["c_y1", "last:lev_a1"], (5, 7): ["c_r2", "last:lev_d1"], (5, 8): ["c_u2", "last:lev_a2"],
    (5, 9): ["prev:c_y2", "last:lev_d2"], (6, 0): ["prev:c_r3", "last:lev_a3"], (6, 1): ["prev:c_u3", "last:lev_d3", "last:lev_a4"],
    (6, 2): ["prev:c_y3", "last:lev_d4"], (6, 3): ["prev:c_out", "last:lev_a5"], (6, 4): ["last:lev_d5"], (6, 5): ["last:lev_a6"],
    (6, 6): ["last:lev_d6"], (6, 7): ["last:c_u0"], (6, 8): ["last:c_y0"], (6, 9): ["last:c_r1"], (7, 0): ["last:c_u1", "last:c_y1"],
    (7, 1): ["last:c_r2"], (7, 2): ["last:c_u2"], (7, 3): ["last:c_y2"], (7, 4): ["last:c_r3"], (7, 5): ["last:c_u3"],
    (7, 6): ["last:c_y3"], (7, 7): ["last:c_out"],
}
PLAN_SECOND = ("load_x", "ln1_stats", "ln1_norm", "xnt", "q", "k", "stacks0", "stacks1", "zero")
PLAN_NEXT = ("logits", "gates", "gt", "h0", "h1", "h2", "h3", "gelu", "v", "m_parts0", "m_rows0", "m_parts1")
PLAN_OLDER = ("c_y2", "c_r3", "c_u3", "c_y3", "c_out")
PLAN_CURRENT = ("gb0", "gb1", "gb2", "gb3", "out", "pv0", "pv1", "pv2", "yt", "x1", "m_rows1", "zero_state")
SEQUENCES = 8


class SecondLayer:

    TILES3, TILES2 = 11, 5

    def __init__(self, tiles3, tiles2, vk, squares, small, banks):
        (self.xn2, self.hn, self.kq, up0, up1,
         self.inv, self.invT,
         self.ablk, self.sy, self.syg, self.out_sb) = tiles3
        self.pair_up = (up0, up1)
        self.gram = self.hn
        self.xn2T, self.hT, self.kT, self.qT, self.tF = tiles2
        self.vk = vk
        self.rhs, self.u_sb, self.state = squares
        self.stats, self.mv, self.vare, self.rstd = small
        self.ps_c0, self.ps_c1 = banks


class Seq:

    def __init__(self, pair, c):
        self.pair, self.c, self.parity = pair, c, c % 2

    def count(self, per, k):
        if self.pair is None:
            return self.c * per + k + 1
        return self.pair * (2 * per) + (self.c * per + k + 1)

    def index(self):
        return self.c if self.pair is None else self.pair * 2 + self.c


def a_number(b, n):
    if b.pair is None and b.c == 0 and n < 0:
        return n - A_XNT
    if b.pair is None and b.c == SEQUENCES - 1 and n >= A_H:
        return n - 3
    return n


def after(eng, sem, value):
    if not (isinstance(value, int) and value <= 1):
        eng.wait_ge(sem, value)


def two_layers(nc, x_in, W_dq, W_uq, W_dkv, W_uk, W_uv, W_o, w1_in, b1_in, w2_in, b2_in, cent_in, route_in,
               Wk_in, bk_in, Wv_in, bv_in, Wq_in, bq_in, gamma_in, beta_in, sign_in, out):
    SEQS, TOK, D = x_in.shape
    NT = TOK // P
    QL = W_dq.shape[0]
    KVL = W_dkv.shape[0]
    NC = EXPERTS * HID // P
    assert D == P and NT == 4 and SEQS == SEQUENCES and NC == 4

    with ExitStack() as ctx:
        def sb(name, shape, dt=F32):
            return ctx.enter_context(nc.sbuf_tensor(name, shape, dt))

        def psum(name, shape, dt=F32):
            return ctx.enter_context(nc.psum_tensor(name, shape, dt))

        def sem(name):
            return ctx.enter_context(nc.semaphore(name))

        ps_s = psum("ps_s", [P, 2, 512])
        ps_e = psum("ps_e", [P, 2, 512])
        ps_v = psum("ps_v", [P, 512])
        ps_a = psum("ps_a", [P, 512])
        ps_c0 = psum("ps_c0", [P, 512])
        ps_c1 = psum("ps_c1", [P, 512])

        ident = sb("ident", [P, P])
        coarse = sb("coarse", [TOK // FINE - 1, 2, TOK], BF16)
        identb = sb("identb", [P, P], BF16)
        negmask = sb("negmask", [P, P], BF16)
        lowmask0 = sb("lowmask0", [P, P])
        upmask = sb("upmask", [P, LEVELS, P])
        left_minus = sb("left_minus", [P, LEVELS])
        strict = sb("strict", [P, P])
        pick = sb("pick", [MAXROW, NC, P], BF16)
        halfpow = sb("halfpow", [P, 4])
        ones_row = sb("ones_row", [1, P])
        fence = sb("fence", [1, P])
        nat = {n: sb("nat_" + n, s) for n, s in (
            ("dq", [QL, P]), ("uq", [P, QL]), ("dkv", [KVL, P]), ("uk", [P, KVL]), ("uv", [P, KVL]), ("o", [P, P]),
            ("wk", [DS, P]), ("wv", [P, P]), ("wq", [DS, P]), ("sg", [P, P]), ("cent", [EXPERTS, P]))}
        uqT = sb("uqT", [QL, P])
        oT = sb("oT", [P, P])
        wqeT = sb("wqeT", [P, P])
        keffT = sb("keffT", [KVL, P])
        veff = sb("veff", [KVL, P])
        w_q = sb("w_q", [P, P])
        w_k = sb("w_k", [P, P])
        w_v = sb("w_v", [P, P])
        rw = sb("rw", [2 * EXPERTS, P])
        rwT = sb("rwT", [P, 2 * EXPERTS])
        cent_ss = sb("cent_ss", [EXPERTS, 1])
        cent_sq = sb("cent_sq", [EXPERTS, P])
        cent_rn = sb("cent_rn", [EXPERTS, 2])
        w1s = sb("w1s", [P, EXPERTS, HID])
        vecs = sb("vecs", [NC + 4, P])
        vecT = sb("vecT", [P, NC + 4])
        w2s = sb("w2s", [P, NC, P])
        b2f = sb("b2f", [MAXROW, P])
        b2r = sb("b2r", [MAXROW, 2, P])
        b2p = sb("b2p", [MAXROW, PARTS, P], BF16)
        wkT = sb("wkT", [P, P])
        wqT = sb("wqT", [P, P])
        wvk = sb("wvk", [P, VK])
        sgT = sb("sgT", [P, P])
        bq_lr = sb("bq_lr", [P, 1])
        vkrow = sb("vkrow", [1, VK])
        vkbias = sb("vkbias", [P, VK])

        x_res = sb("x_res", [P, NT, P])
        x1 = [sb(f"x1_{p}", [P, NT, P]) for p in range(2)]
        gate_out = sb("gate_out", [P, NT, P])
        qst = [sb(f"qst{p}", [P, HEADS, TOK], BF16) for p in range(2)]
        kst = [sb(f"kst{p}", [P, HEADS, TOK], BF16) for p in range(2)]
        vaug = sb("vaug", [P, NT, HEADS, 32])
        stats = [sb(f"stats{n}", [P, NT, 6]) for n in range(3)]
        mv = [sb(f"mv{n}", [P, NT, 2]) for n in range(3)]
        vare = [sb(f"vare{n}", [P, NT]) for n in range(3)]
        rstd = [sb(f"rstd{n}", [P, NT]) for n in range(3)]
        xn = sb("xn", [P, NT, P])
        xnT = [sb(f"xnT{p}", [P, TOK]) for p in range(2)]
        ss = sb("ss", [P, NT])
        ssm = sb("ssm", [P, NT])
        rn = sb("rn", [P, NT])
        parts = [sb(n, [P, PARTS, TOK], BF16) for n in ("qparts", "kparts")]
        rest = [xn[:, :, :].rearrange("p i d -> p (i d)"), sb("krest", [P, TOK])[:, :]]
        coss = sb("coss", [P, NT, EXPERTS])
        logit = sb("logit", [P, NT, EXPERTS])
        top8 = sb("top8", [P, NT, EXPERTS])
        keep = sb("keep", [P, NT, EXPERTS])
        dlt = sb("dlt", [P, NT, EXPERTS])
        ex = sb("ex", [P, NT, EXPERTS])
        gm = sb("gm", [P, NT, EXPERTS])
        gsum = sb("gsum", [P, NT])
        grec = sb("grec", [P, NT])
        gate = sb("gate", [P, NT, EXPERTS])
        grest = sb("grest", [P, NT, EXPERTS])
        gparts = sb("gparts", [P, NT, PARTS, EXPERTS], BF16)
        gT = sb("gT", [MAXROW, TOK], BF16)
        hid = sb("hid", [P, NC, TOK])
        tG = sb("tG", [P, TOK])
        cand = sb("cand", [P, NT, HEADS, 3])
        nm = sb("nm", [P, NT, HALF_HEADS])
        nmrest = sb("nmrest", [P, NT, HALF_HEADS])
        mparts = sb("mparts", [P, NT, PARTS, 32], BF16)
        mrow = sb("mrow", [PARTS * 32, TOK], BF16)
        prob = sb("prob", [P, UNITS, 512])
        yT = sb("yT", [P, TOK])
        rden = sb("rden", [P, NT, GH])
        att = sb("att", [P, NT, P])

        def tile3(t):
            return t.rearrange("p (i d) -> p i d", i=NT)

        small = (stats, mv, vare, rstd)
        body = SecondLayer([tile3(sb(f"second{n}", [P, TOK])[:, :]) for n in range(SecondLayer.TILES3)],
                           [sb(f"second_flat{n}", [P, TOK])[:, :] for n in range(SecondLayer.TILES2)],
                           sb("vk", [P, NT, VK])[:, :, :], [sb(n, [P, P])[:, :] for n in ("rhs", "u_sb", "state")], small,
                           (ps_c0[:, :], ps_c1[:, :]))
        done = [t[:, 2 * n:2 * n + 2, :].bitcast(F32) for t in (qst[0], kst[0]) for n in range(HEADS // 2)]
        small = [[None] + [sb(f"last_{n}{m}", [P, NT] + shape) for m in (1, 2)]
                 for n, shape in (("stats", [6]), ("mv", [2]), ("vare", []), ("rstd", []))]
        last = SecondLayer([t.rearrange("p a (x d) -> p (a x) d", d=P) for t in done[:SecondLayer.TILES3]],
                           [t.rearrange("p a c -> p (a c)") for t in done[SecondLayer.TILES3:]],
                           parts[0][:, :, :].rearrange("p r q -> p (r q)").bitcast(F32).rearrange("p (i d) -> p i d", i=NT),
                           [rest[1][:, P * n:P * n + P] for n in range(3)], small, (ps_s[:, 0, :], ps_s[:, 1, :]))

        max_scratch = nc.dram_tensor("max_scratch", (PARTS * 32, TOK), BF16).ap()
        scratch = nc.dram_tensor("split_scratch", (2, PARTS, P, TOK), BF16).ap()

        names = """const_ready mask_step loaded prep_pe prep_out prep_out2 prep_sign small_zeroed stack_zeroed0 stack_zeroed1
        first_loaded masks_ready left_ready coarse_ready coarse_loaded
        x_loaded res_loaded scratch_written stack_loaded0 stack_loaded1 mscratch_written mrow_loaded stored
        a_filled a_emptied c0_filled c0_emptied c1_filled c1_emptied pv_used yt_filled v_emptied
        s_filled s_emptied e_filled e_emptied
        stats0 stats1 stats2 mv0 mv1 mv2 var0 var1 var2 rstd0 rstd1 rstd2 norm0 norm1 norm2
        ss_ready ssm_ready rn_ready hi_ready mid_ready parts_ready
        cos_ready top_ready keep_ready dlt_ready ex_ready gm_ready gsum_ready grec_ready gate_ready
        ghi_ready grest_ready gmid_ready gparts_ready gelu_ready tg_ready
        nm_ready mhi_ready mrest_ready mmid_ready mparts_ready
        rden_ready attg_ready x1_ready
        dtmp_ready dtmpt_ready inv1_ready invt1_ready pair_ready tf_ready syg_ready out_ready""".split()
        S = {n: sem(n) for n in names}
        second_names = """c0_filled c0_emptied c1_filled c1_emptied stats1 stats2 mv1 mv2 var1 var2 rstd1 rstd2 norm1 norm2
        dtmp_ready dtmpt_ready inv1_ready invt1_ready pair_ready tf_ready syg_ready out_ready stored""".split()
        body.S = S
        last.S = {n: sem("last_" + n) for n in second_names}

        def second_layer(b):
            return (last, Seq(None, 0)) if b.pair is None and b.c == SEQS - 1 else (body, b)

        block = ctx.enter_context(nc.Block())

        fences = [0]

        def settled(eng, sem, value):
            eng.wait_ge(sem, value)
            if not isinstance(value, int):
                fences[0] += 1
                spot = fence[0:1, fences[0]:fences[0] + 1]
                eng.tensor_tensor(spot, ident[0:1, 0:1], ident[0:1, 0:1], ALU.mult)

        def half(t, lv, a):
            return t[:, :, :].rearrange("p i (n a w) -> p i n a w", a=2, w=1 << lv)[:, :, :, a, :]

        def half_bank(bank, lv, a):
            return bank[:, :].rearrange("p (i n a w) -> p i n a w", i=NT, a=2, w=1 << lv)[:, :, :, a, :]

        def bcast(ap, axis, n):
            ap = ap.unsqueeze(axis)
            shape = list(ap.shape)
            shape[axis] = n
            return ap.to_broadcast(shape)

        def run(eng, pieces, unit, prepare=None, settle=None):
            def iteration(second, nxt, cur, prev, older, plan=PLAN):
                for step in range(1 + max(at[0] for at in plan)):
                    for u in range(UNITS):
                        if step < GROUPS:
                            unit(cur, nxt, step, u)
                        for name in plan.get((step, u), []):
                            of = second if name in PLAN_SECOND else nxt if name in PLAN_NEXT else \
                                cur if name in PLAN_CURRENT or name.startswith("last:") else \
                                older if name in PLAN_OLDER else prev
                            name = name.removeprefix("last:").removeprefix("prev:")
                            if of is not None and name in pieces:
                                if name in ("pv0", "pv1"):
                                    pieces[name](of, step)
                                elif name in ("pv2", "yt"):
                                    pieces[name](of, step - 1)
                                else:
                                    pieces[name](of)

            seqs = [Seq(None, c) for c in range(SEQS)]
            iteration(seqs[0], None, None, None, None)
            if prepare is not None:
                prepare()
            iteration(seqs[1], seqs[0], None, None, None)
            if settle is not None:
                settle()
            iteration(seqs[2], seqs[1], seqs[0], None, None)
            iteration(seqs[3], seqs[2], seqs[1], seqs[0], None)
            with eng.Fori(0, (SEQS - 4) // 2) as pair:
                for odd in range(2):
                    iteration(*(Seq(pair, ahead + odd) for ahead in (4, 3, 2, 1, 0)))
            iteration(None, *seqs[:SEQS - 5:-1])
            iteration(None, None, *seqs[:SEQS - 4:-1], plan=LAST_PLAN)

        x_view = x_in.rearrange("b (i p) d -> b p i d", p=P)
        out_view = out.rearrange("b (i p) d -> b p i d", p=P)

        def row(v):
            return v.rearrange("(o d) -> o d", o=1)

        first_loads = [
            (nat["uq"][:, :], W_uq), (nat["o"][:, :], W_o), (nat["dq"][:, :], W_dq), (nat["dkv"][:, :], W_dkv), (nat["uk"][:, :], W_uk),
            (nat["uv"][:, :], W_uv), (nat["cent"][:, :], cent_in)]
        loads = [
            (rw[EXPERTS:2 * EXPERTS, :], route_in), (w1s[:, :, :], w1_in.rearrange("e d f -> d e f")),
            (w2s[:, :, :], w2_in.rearrange("(c a) f d -> (a f) c d", a=2)),
            (nat["wk"][:, :], Wk_in), (nat["wv"][:, :], Wv_in), (nat["wq"][:, :], Wq_in), (nat["sg"][:, :], sign_in)]
        zero_loads = [(b2f[EXPERTS * r:EXPERTS * (r + 1), :], b2_in) for r in range(PARTS)] + [
            (vecs[0:NC, :], b1_in.rearrange("(c a) f -> c (a f)", a=2)), (vecs[NC:NC + 1, :], row(gamma_in)),
            (vecs[NC + 1:NC + 2, :], row(beta_in)), (vecs[NC + 2:NC + 3, 0:DS], row(bk_in)), (vecs[NC + 3:NC + 4, 0:DS], row(bq_in)),
            (vkrow[:, 0:P], row(bv_in)), (vkrow[:, P:P + DS], row(bk_in))]
        FIRST_LOADED = 16 * len(first_loads)
        LOADED = 16 * (len(loads) + len(zero_loads))

        @block.sync
        def _(sp):
            sp.dma_start(xn[:, :, :], x_view[0]).then_inc(S["x_loaded"], 16)
            for dst, src in first_loads:
                sp.dma_start(dst, src).then_inc(S["first_loaded"], 16)
            for dst, src in loads:
                sp.dma_start(dst, src).then_inc(S["loaded"], 16)
            sp.wait_ge(S["small_zeroed"], 1)
            for dst, src in zero_loads:
                sp.dma_start(dst, src).then_inc(S["loaded"], 16)

            def dram(view, b):
                if b.pair is None:
                    return view[b.index()]
                return view[bass.ds(b.index(), 1)].rearrange("o p i d -> (o p) i d")

            def load_residual(b):
                after(sp, S["x1_ready"], b.count(1, 0))
                sp.dma_start(x_res[:, :, :], dram(x_view, b)).then_inc(S["res_loaded"], 16)

            def load_x(b):
                if b.pair is None and b.c == 0:
                    return
                after(sp, S["parts_ready"], b.count(2, 0))
                sp.dma_start(xn[:, :, :], dram(x_view, b)).then_inc(S["x_loaded"], 16)

            def coarse_rows(b):
                if b.pair is None and b.c < 2:
                    n = TOK // FINE - 1
                    sp.wait_ge(S["coarse_ready"], 2)
                    sp.wait_ge(S[f"stack_zeroed{b.c}"], 2)
                    for m, stack in enumerate((qst, kst)):
                        sp.dma_start(stack[b.c][PAIRS:PAIRS + n, :, :], coarse[:, m:m + 1, :].to_broadcast([n, HEADS, TOK]))\
                            .then_inc(S["coarse_loaded"], 16)

            def write_parts(b, n):
                after(sp, S["stack_loaded1"], b.count(192, 0))
                sp.wait_ge(S["parts_ready"], b.count(2, n + 1))
                sp.dma_start(scratch[n].rearrange("r s q -> s r q"), parts[n][:, :, :]).then_inc(S["scratch_written"], 16)

            def load_stacks(b, half):
                heads = slice(HALF_HEADS * half, HALF_HEADS * (half + 1))
                span = slice(HALF_HEADS * TOK * half, HALF_HEADS * TOK * (half + 1))
                loaded = S[f"stack_loaded{half}"]
                sp.wait_ge(S[f"stack_zeroed{b.parity}"], 3)
                after(sp, S["e_filled"], b.count(GROUPS * UNITS, GROUPS * UNITS * (half - 3) // 2))
                sp.wait_ge(S["scratch_written"], b.count(32, 32))
                q_rows = scratch[0].rearrange("r (d h) q -> (r d) (h q)", d=HD)[:, span]
                k_rows = scratch[1].rearrange("r (d h) q -> (r d) (h q)", d=HD)[:, span]
                n3 = PARTS * HD
                for s in range(PARTS):
                    sp.dma_start(qst[b.parity][n3 * s:n3 * s + n3, heads, :].rearrange("p h q -> p (h q)"), q_rows,
                                 max_dma_last_dim=4096).then_inc(loaded, 16)
                    for r in range(PARTS):
                        lo = n3 * s + HD * r
                        sp.dma_start(kst[b.parity][lo:lo + HD, heads, :].rearrange("p h q -> p (h q)"), k_rows[HD * s:HD * s + HD, :],
                                     max_dma_last_dim=4096).then_inc(loaded, 16)

            def m_rows(b, half):
                sp.wait_ge(S["a_emptied"], b.count(A_FILLS, a_number(b, (A_M0, A_M1)[half]) + 1))
                after(sp, S["mrow_loaded"], b.count(32, 16 * half))
                sp.dma_start(max_scratch, mrow[:, :]).then_inc(S["mscratch_written"], 16)
                sp.wait_ge(S["mscratch_written"], b.count(32, 16 * half + 16))
                sp.dma_start(qst[b.parity][MAXROW:MAXROW + PARTS, HALF_HEADS * half:HALF_HEADS * (half + 1), :].rearrange("r h q -> r (h q)"),
                             max_scratch.rearrange("(r h) q -> r h q", r=PARTS)[:, 0:HALF_HEADS, :].rearrange("r h q -> r (h q)"),
                             max_dma_last_dim=4096).then_inc(S["mrow_loaded"], 16)

            def c_out(b):
                r, o = second_layer(b)
                sp.wait_ge(r.S["out_ready"], o.count(1, 1))
                sp.dma_start(dram(out_view, b), r.out_sb[:, :, :]).then_inc(r.S["stored"], 16)

            run(sp, {"zero": coarse_rows, "gb0": load_residual, "load_x": load_x, "q": lambda b: write_parts(b, 0), "k": lambda b: write_parts(b, 1),
                     "stacks0": lambda b: load_stacks(b, 0), "stacks1": lambda b: load_stacks(b, 1),
                     "m_rows0": lambda b: m_rows(b, 0), "m_rows1": lambda b: m_rows(b, 1), "c_out": c_out}, lambda *a: None)
            sp.wait_ge(body.S["stored"], 16 * (SEQS - 1) + 1)
            sp.wait_ge(last.S["stored"], 16 + 1)

        @block.gpsimd
        def _(pool):
            g = nc.gpsimd
            steps = [0]

            def chain(ins):
                steps[0] += 1
                ins.then_inc(S["mask_step"], 1)
                pool.wait_ge(S["mask_step"], steps[0])

            chain(g.memset(b2f[:, :], 0.0))
            chain(g.memset(vecs[:, :], 0.0))
            chain(g.memset(vkrow[:, :], 0.0))
            g.memset(halfpow[:, :], -0.5).then_inc(S["small_zeroed"], 1)
            chain(g.memset(ident[:, :], 0.0))
            chain(g.affine_select(out=ident[:, :], in_=ident[:, :], compare_op=ALU.not_equal, fill=1.0, base=0,
                                  pattern=[[-1, P]], channel_multiplier=1))
            chain(g.tensor_copy(identb[:, :], ident[:, :]))
            chain(g.memset(ones_row[:, :], 1.0))
            g.memset(body.state, 0.0).then_inc(S["const_ready"], 1)
            chain(g.memset(negmask[:, :], 0.0))
            chain(g.affine_select(out=negmask[:, :], in_=negmask[:, :], compare_op=ALU.is_ge, fill=NEG, base=0,
                                  pattern=[[-1, P]], channel_multiplier=1))
            chain(g.memset(coarse[:, 0, :], NEG))
            chain(g.memset(coarse[:, 1, :], 1.0))
            g.affine_select(out=coarse[:, 0, :], in_=coarse[:, 0, :], compare_op=ALU.is_gt, fill=0.0, base=FINE,
                            pattern=[[-1, TOK]], channel_multiplier=FINE).then_inc(S["coarse_ready"], 1)
            pool.wait_ge(S["coarse_ready"], 1)
            blocks = coarse[:, 1, :].rearrange("p (n w) -> p n w", w=FINE)
            g.affine_select(out=blocks, in_=blocks, compare_op=ALU.is_equal, fill=0.0, base=-1,
                            pattern=[[1, TOK // FINE], [0, FINE]], channel_multiplier=-1).then_inc(S["coarse_ready"], 1)
            pool.wait_ge(S["coarse_ready"], 2)
            pool.wait_ge(S["ss_ready"], 1)
            chain(g.tensor_scalar(cent_rn[:, 0:1], cent_ss[:, :], NORM_EPS * NORM_EPS, None, ALU.max))
            g.tensor_tensor(cent_rn[:, 1:2], cent_rn[:, 0:1], halfpow[0:EXPERTS, 0:1], ALU.pow).then_inc(S["rn_ready"], 1)
            for n, t in enumerate((wkT[:, DS:P], wqT[:, DS:P])):
                g.memset(t, 0.0).then_inc(S["const_ready"], 1)
                pool.wait_ge(S["const_ready"], n + 2)
            chain(g.memset(fence[:, :], 0.0))
            chain(g.memset(cand[:, :, :, :], -3e38))
            chain(g.memset(mparts[:, :, :, :], 0.0))
            g.memset(gT[:, :], 0.0).then_inc(S["const_ready"], 1)

            def masks():
                chain(g.memset(vaug[:, :, :, :], 0.0))
                chain(g.memset(vaug[:, :, :, HD:HD + 1], 1.0))
                chain(g.memset(pick[:, :, :], 0.0))
                for r in range(PARTS):
                    chain(g.affine_select(out=pick[:, :, :].rearrange("p c (a f) -> p c a f", a=2),
                                          in_=pick[:, :, :].rearrange("p c (a f) -> p c a f", a=2),
                                          compare_op=ALU.not_equal, fill=1.0, base=-EXPERTS * r,
                                          pattern=[[-2, NC], [-1, 2], [0, HID]], channel_multiplier=1))
                chain(g.memset(strict[:, :], 1.0))
                chain(g.affine_select(out=strict[:, :], in_=strict[:, :], compare_op=ALU.is_gt, fill=0.0, base=0,
                                      pattern=[[1, P]], channel_multiplier=-1))
                chain(g.memset(lowmask0[:, :], 0.0))
                low = lowmask0[:, :].rearrange("p (n a) -> p n a", a=2)[:, :, 0]
                chain(g.memset(low, LR))
                chain(g.affine_select(out=low, in_=low, compare_op=ALU.is_equal, fill=0.0, base=-1,
                                      pattern=[[-2, P // 2]], channel_multiplier=1))
                chain(g.memset(upmask[:, :, :], 0.0))
                for lv in range(LEVELS):
                    w = 1 << lv
                    nb = P // (2 * w)
                    second = upmask[:, lv, :].rearrange("p (n a w) -> p n a w", a=2, w=w)[:, :, 1, :]
                    chain(g.memset(second, LR))
                    chain(g.affine_select(out=second, in_=second, compare_op=ALU.is_ge, fill=0.0, base=0,
                                          pattern=[[-2 * w, nb], [0, w]], channel_multiplier=1))
                    chain(g.affine_select(out=second, in_=second, compare_op=ALU.is_ge, fill=0.0, base=w - 1,
                                          pattern=[[2 * w, nb], [0, w]], channel_multiplier=-1))
                pool.sem_inc(S["masks_ready"], 1)

            def ln_rstd(n, b):
                r, o = second_layer(b) if n else (body, b)
                settled(pool, r.S[f"mv{n}"], o.count(NT, NT))
                g.tensor_scalar(r.vare[n][:, :], r.mv[n][:, :, 1], LN_EPS, None, ALU.add).then_inc(r.S[f"var{n}"], 1)
                pool.wait_ge(r.S[f"var{n}"], o.count(1, 1))
                g.tensor_tensor(r.rstd[n][:, :], r.vare[n][:, :], halfpow[:, :], ALU.pow).then_inc(r.S[f"rstd{n}"], 1)

            def split_rest(n, b):
                settled(pool, S["a_emptied"], b.count(A_FILLS, a_number(b, A_Q + n) + 1))
                g.tensor_copy(parts[n][:, 1, :], rest[n]).then_inc(S["mid_ready"], 1)
                pool.wait_ge(S["mid_ready"], b.count(2, n + 1))
                g.tensor_tensor(parts[n][:, 2, :], rest[n], parts[n][:, 1, :], ALU.subtract).then_inc(S["parts_ready"], 1)

            def token_norms(b):
                settled(pool, S["ss_ready"], b.count(NT, NT))
                g.tensor_scalar(ssm[:, :], ss[:, :], NORM_EPS * NORM_EPS, None, ALU.max).then_inc(S["ssm_ready"], 1)
                pool.wait_ge(S["ssm_ready"], b.count(1, 1))
                after(pool, S["cos_ready"], b.count(1, 0))
                g.tensor_tensor(rn[:, :], ssm[:, :], halfpow[:, :], ALU.pow).then_inc(S["rn_ready"], 1)

            def gates(b):
                settled(pool, S["gate_ready"], b.count(1, 1))
                g.tensor_copy(gparts[:, :, 0, :], gate[:, :, :]).then_inc(S["ghi_ready"], 1)
                pool.wait_ge(S["ghi_ready"], b.count(1, 1))
                g.tensor_tensor(grest[:, :, :], gate[:, :, :], gparts[:, :, 0, :], ALU.subtract).then_inc(S["grest_ready"], 1)
                settled(pool, S["grest_ready"], b.count(1, 1))
                g.tensor_copy(gparts[:, :, 1, :], grest[:, :, :]).then_inc(S["gmid_ready"], 1)
                pool.wait_ge(S["gmid_ready"], b.count(1, 1))
                g.tensor_tensor(gparts[:, :, 2, :], grest[:, :, :], gparts[:, :, 1, :], ALU.subtract).then_inc(S["gparts_ready"], 1)

            def m_parts(b, half):
                H = HALF_HEADS
                settled(pool, S["nm_ready"], b.count(2, half + 1))
                if half or b.pair is not None or b.c > 0:
                    settled(pool, S["a_filled"], b.count(A_FILLS, a_number(b, (A_M1 - A_FILLS, A_M0)[half]) + 1))
                g.tensor_copy(mparts[:, :, 0, 0:H], nm[:, :, :]).then_inc(S["mhi_ready"], 1)
                pool.wait_ge(S["mhi_ready"], b.count(2, half + 1))
                g.tensor_tensor(nmrest[:, :, :], nm[:, :, :], mparts[:, :, 0, 0:H], ALU.subtract).then_inc(S["mrest_ready"], 1)
                settled(pool, S["mrest_ready"], b.count(2, half + 1))
                g.tensor_copy(mparts[:, :, 1, 0:H], nmrest[:, :, :]).then_inc(S["mmid_ready"], 1)
                pool.wait_ge(S["mmid_ready"], b.count(2, half + 1))
                g.tensor_tensor(mparts[:, :, 2, 0:H], nmrest[:, :, :], mparts[:, :, 1, 0:H], ALU.subtract).then_inc(S["mparts_ready"], 1)

            def x1_piece(b):
                p = b.parity
                pool.wait_ge(S["v_emptied"], b.count(2 * GROUPS, 2 * GROUPS))
                g.tensor_tensor(att[:, :, :], att[:, :, :], gate_out[:, :, :], ALU.mult).then_inc(S["attg_ready"], 1)
                pool.wait_ge(S["attg_ready"], b.count(1, 1))
                pool.wait_ge(S["res_loaded"], b.count(16, 16))
                after(pool, S["out_ready"], b.count(1, -1))
                g.tensor_tensor(x1[p][:, :, :], x_res[:, :, :], att[:, :, :], ALU.add).then_inc(S["x1_ready"], 1)

            def c_gram(b):
                r, o = second_layer(b)
                if o.pair is not None or o.c > 0:
                    settled(pool, r.S["c1_filled"], o.count(C1_FILLS, c1_dt(LEVELS - 1) + 1 - C1_FILLS))
                g.memset(r.ablk[:, :, :], 0.0).then_inc(r.S["inv1_ready"], 1)
                eye = bcast(ident[:, :], 1, NT)
                pool.wait_ge(r.S["c0_emptied"], o.count(C0_FILLS, C0_GRAM + 1))
                g.tensor_tensor(r.sy[:, :, :], r.gram[:, :, :], bcast(lowmask0[:, :], 1, NT), ALU.mult).then_inc(r.S["dtmp_ready"], 1)
                pool.wait_ge(r.S["dtmp_ready"], o.count(1, 1))
                g.tensor_tensor(r.inv[:, :, :], eye, r.sy[:, :, :], ALU.subtract).then_inc(r.S["inv1_ready"], 1)
                pairs(b, 1)
                pairs(b, 2)

            def pairs(b, lv):
                r, o = second_layer(b)
                if lv < LEVELS:
                    if lv > 2:
                        pool.wait_ge(r.S["c0_filled"], o.count(C0_FILLS, c0_a(lv - 2) + 1))
                    g.tensor_tensor(r.pair_up[lv % 2][:, :, :], r.gram[:, :, :], bcast(upmask[:, lv, :], 1, NT), ALU.mult)\
                        .then_inc(r.S["pair_ready"], 1)

            def c_out(b):
                r, o = second_layer(b)
                pool.wait_ge(r.S["c1_emptied"], o.count(C1_FILLS, C1_Y + 1))
                g.tensor_tensor(r.syg[:, :, :], r.sy[:, :, :], r.tF[:, :].rearrange("p (i d) -> p i d", i=NT), ALU.mult)\
                    .then_inc(r.S["syg_ready"], 1)
                pool.wait_ge(r.S["syg_ready"], o.count(1, 1))
                after(pool, r.S["stored"], o.count(16, 0))
                g.tensor_tensor(r.out_sb[:, :, :], x1[b.parity][:, :, :], r.syg[:, :, :], ALU.add).then_inc(r.S["out_ready"], 1)

            levels = {f"lev_d{lv}": lambda b, lv=lv: pairs(b, lv + 2) for lv in range(1, LEVELS)}
            run(pool, levels | {"ln1_norm": lambda b: ln_rstd(0, b), "ln2_norm": lambda b: ln_rstd(1, b), "ln3_norm": lambda b: ln_rstd(2, b),
                       "q": lambda b: split_rest(0, b), "k": lambda b: split_rest(1, b), "xnt": token_norms, "gates": gates,
                       "m_parts0": lambda b: m_parts(b, 0), "m_parts1": lambda b: m_parts(b, 1), "x1": x1_piece, "c_gram": c_gram, "c_out": c_out,
                       "zero_state": lambda b: g.memset(last.state, 0.0)}, lambda *a: None, masks)

        @block.tensor
        def _(pe):
            mm, tr = nc.tensor.matmul, nc.tensor.transpose
            pe.wait_ge(S["const_ready"], 1)
            pe.wait_ge(S["first_loaded"], FIRST_LOADED)
            done = [0]

            def prep(ins):
                done[0] += 1
                ins.then_inc(S["prep_pe"], 1)

            def ready(n):
                pe.wait_ge(S["prep_out"], n)

            prep(tr(ps_a[0:QL, 0:P], nat["uq"][:, :], ident[:, :]))
            prep(tr(ps_c0[:, 0:P], nat["o"][:, :], ident[:, :]))
            ready(2)
            prep(mm(ps_c1[:, 0:P], uqT[:, :], nat["dq"][:, :], start=True, stop=True))
            prep(mm(ps_a[:, 0:P], nat["dq"][:, :], uqT[:, :], start=True, stop=True))
            prep(mm(ps_c0[0:KVL, 0:P], nat["uv"][:, :], oT[:, :], start=True, stop=True))
            ready(5)
            prep(mm(ps_c1[0:KVL, 0:P], nat["uk"][:, :], wqeT[:, :], start=True, stop=True))
            prep(mm(ps_c0[:, 0:P], nat["dkv"][:, :], veff[:, :], start=True, stop=True))
            ready(7)
            prep(mm(ps_a[:, 0:P], nat["dkv"][:, :], keffT[:, :], start=True, stop=True))
            ready(8)

            def prepare():
                pe.wait_ge(S["const_ready"], 4)
                pe.wait_ge(S["loaded"], LOADED)
                pe.wait_ge(S["coarse_loaded"], 32)
                prep(tr(ps_c0[:, 0:DS], nat["wk"][:, :], ident[0:DS, 0:DS]))
                prep(tr(ps_c1[:, 0:DS], nat["wq"][:, :], ident[0:DS, 0:DS]))
                prep(tr(ps_v[:, 0:NC + 4], vecs[:, :], ident[0:NC + 4, 0:NC + 4]))
                prep(tr(ps_s[:, 0, 0:P], nat["wv"][:, :], ident[:, :]))
                prep(tr(ps_s[:, 1, 0:P], nat["sg"][:, :], ident[:, :]))
                prep(mm(ps_e[:, 0, 0:VK], ones_row[:, :], vkrow[:, :], start=True, stop=True))
                ready(17)
                prep(tr(ps_e[:, 1, 0:2 * EXPERTS], rw[:, :], ident[0:2 * EXPERTS, 0:2 * EXPERTS]))
                ready(PREP_OUT)

            def settle():
                pe.wait_ge(S["masks_ready"], 1)
                pe.wait_ge(S["coarse_loaded"], 64)

            def a_fill(b, n):
                after(pe, S["a_emptied"], b.count(A_FILLS, a_number(b, n)))

            def c0_fill(b, n):
                r, o = second_layer(b)
                after(pe, r.S["c0_emptied"], o.count(C0_FILLS, n))

            def c1_fill(b, n):
                r, o = second_layer(b)
                after(pe, r.S["c1_emptied"], o.count(C1_FILLS, n))

            def tok(i):
                return slice(i * P, (i + 1) * P)

            def xnt(b):
                a_fill(b, A_XNT)
                pe.wait_ge(S["norm0"], b.count(NT, NT))
                for i in range(NT):
                    last = tr(ps_a[:, tok(i)], xn[:, i, :], ident[:, :])
                last.then_inc(S["a_filled"], 1)

            def qk(b, n):
                a_fill(b, A_Q + n)
                mm(ps_a[:, :], (w_q, w_k)[n][:, :], xnT[b.parity][:, :], start=True, stop=True).then_inc(S["a_filled"], 1)

            def v(b):
                a_fill(b, A_V)
                for i in range(NT):
                    last = mm(ps_a[:, tok(i)], xnT[b.parity][:, tok(i)], w_v[:, :], start=True, stop=True)
                last.then_inc(S["a_filled"], 1)

            def logits(b):
                a_fill(b, A_LOGIT)
                for i in range(NT):
                    last = mm(ps_a[:, 16 * i:16 * i + 16], xnT[b.parity][:, tok(i)], rwT[:, :], start=True, stop=True)
                last.then_inc(S["a_filled"], 1)

            def gt(b):
                a_fill(b, A_GT)
                pe.wait_ge(S["gparts_ready"], b.count(1, 1))
                for i in range(NT):
                    last = tr(ps_a[:, :].bitcast(BF16)[0:PARTS * EXPERTS, tok(i)],
                              gparts[:, i, :, :].rearrange("p r e -> p (r e)"), identb[:, :])
                last.then_inc(S["a_filled"], 1)

            def h(b, c):
                a_fill(b, A_H + c)
                mm(ps_a[:, :], w1s[:, 2 * c:2 * c + 2, :].rearrange("p e f -> p (e f)"), xnT[b.parity][:, :], start=True, stop=True)\
                    .then_inc(S["a_filled"], 1)

            def gb(b, c):
                a_fill(b, A_GB + c)
                mm(ps_a[:, :], pick[:, c, :], gT[:, :], start=True, stop=True).then_inc(S["a_filled"], 1)

            def out_piece(b):
                a_fill(b, A_OUT)
                for i in range(NT):
                    for c in range(NC):
                        mm(ps_a[:, tok(i)], hid[:, c, tok(i)], w2s[:, c, :], start=(i == 0 and c == 0), stop=False,
                           skip_group_check=True)
                    for r in range(PARTS):
                        last = mm(ps_a[:, tok(i)], gT[:, tok(i)], b2p[:, r, :], start=False, stop=(r == PARTS - 1),
                                  skip_group_check=True)
                last.then_inc(S["a_filled"], 1)

            def m_rows(b, half):
                a_fill(b, (A_M0, A_M1)[half])
                pe.wait_ge(S["mparts_ready"], b.count(2, half + 1))
                for i in range(NT):
                    last = tr(ps_a[:, :].bitcast(BF16)[0:PARTS * 32, tok(i)],
                              mparts[:, i, :, :].rearrange("p r h -> p (r h)"), identb[:, :])
                last.then_inc(S["a_filled"], 1)

            def unit(cur, nxt, grp, u):
                if cur is not None:
                    e_unit(cur, grp, u)
                if nxt is not None:
                    s_unit(nxt, grp, u)

            def e_unit(b, grp, u):
                q, k = qst[b.parity], kst[b.parity]
                bank = u % 2
                after(pe, S["e_emptied"], b.count(GROUPS * UNITS, UNITS * grp + u - 1))
                if grp % 2 == 0 and u == 0:
                    pe.wait_ge(S["mrow_loaded"], b.count(32, 8 * grp + 16))
                todo = [(u, 0, 0)] if u < 4 else [(u - 4, 1, 0), (u - 4, 3, 384)] if u < 8 else \
                    [(2 * (u - 8), 2, 0), (2 * (u - 8) + 1, 2, 256)]
                if u < 4:
                    diag = ps_e[:, bank, 0:P].rearrange("p (a c) -> p a c", a=1)
                else:
                    step = 384 if u < 8 else 256
                    diag = ps_e[:, bank, :].rearrange("p (a c) -> p a c", c=P)[:, 0:step // P + 1:step // P, :]
                mm(diag, negmask[:, :], bcast(identb[:, :], 1, len(todo)), start=True, stop=False, skip_group_check=True)
                for hh, j, at in todo:
                    hd = GH * grp + hh
                    last = mm(ps_e[:, bank, at:at + TOK - P * j], k[:, hd, tok(j)], q[:, hd, P * j:TOK],
                              start=False, stop=True, skip_group_check=True)
                last.then_inc(S["e_filled"], 1)

            def s_unit(b, grp, u):
                q, k = qst[b.parity], kst[b.parity]
                bank = u % 2
                after(pe, S["s_emptied"], b.count(GROUPS * UNITS, UNITS * grp + u - 1))
                if grp % 2 == 0 and u == 0:
                    pe.wait_ge(S[f"stack_loaded{grp // 2}"], b.count(192, 192))
                i, keys, hds = S_UNIT[u]
                for n, hh in enumerate(hds):
                    w = keys[1] - keys[0]
                    hd = GH * grp + hh
                    last = mm(ps_s[:, bank, w * n:w * (n + 1)], q[0:MAXROW, hd, tok(i)], k[0:MAXROW, hd, keys[0]:keys[1]],
                              start=(n == 0), stop=True, skip_group_check=True)
                if u < NT:
                    for lo in range(0, P, FINE):
                        last = mm(ps_s[lo:lo + FINE, bank, :].rearrange("p (a c) -> p a c", a=GH)[:, :, lo:lo + FINE],
                                  identb[0:FINE, 0:FINE], bcast(negmask[0:FINE, 0:FINE], 1, GH), start=False, stop=True,
                                  skip_group_check=True)
                last.then_inc(S["s_filled"], 1)

            def pv(b, grp, piece):
                if piece == 0:
                    after(pe, S["v_emptied"], b.count(2 * GROUPS, 2 * grp))
                    if grp == 0:
                        pe.wait_ge(S["a_emptied"], b.count(A_FILLS, a_number(b, A_V) + 1))
                pe.wait_ge(S["e_emptied"], b.count(GROUPS * UNITS, UNITS * grp + (4, 8, 10)[piece]))
                for j, u0, at in (((0, 0, 0),), ((1, 4, 0), (3, 4, 384)), ((2, 8, 0),))[piece]:
                    for hh in range(GH):
                        u, o = (u0 + hh, at) if j != 2 else (u0 + hh // 2, 256 * (hh % 2))
                        last = mm(ps_v[32 * hh:32 * hh + 32, P * j:TOK], vaug[:, j, GH * grp + hh, :],
                                  prob[:, u, o:o + TOK - P * j], start=(j == 0), stop=(j == 2), skip_group_check=True)
                last.then_inc(S["pv_used"], 1)

            def yt(b, grp):
                pe.wait_ge(S["v_emptied"], b.count(2 * GROUPS, 2 * grp + 1))
                for i in range(NT):
                    last = tr(ps_v[:, tok(i)], yT[:, tok(i)], ident[:, :])
                last.then_inc(S["yt_filled"], 1)

            def c_xn2t(b):
                r, o = second_layer(b)
                c0_fill(b, C0_XN2T)
                pe.wait_ge(r.S["norm1"], o.count(NT, NT))
                for i in range(NT):
                    last = tr(r.ps_c0[:, tok(i)], r.xn2[:, i, :], ident[:, :])
                last.then_inc(r.S["c0_filled"], 1)

            def c_ht(b):
                r, o = second_layer(b)
                c1_fill(b, C1_HT)
                pe.wait_ge(r.S["norm2"], o.count(NT, NT))
                for i in range(NT):
                    last = tr(r.ps_c1[:, tok(i)], r.hn[:, i, :], ident[:, :])
                last.then_inc(r.S["c1_filled"], 1)

            def c_kt(b):
                r, o = second_layer(b)
                c0_fill(b, C0_KT)
                pe.wait_ge(r.S["c1_emptied"], o.count(C1_FILLS, C1_HT + 1))
                mm(r.ps_c0[:, :], wkT[:, :], r.hT[:, :], start=True, stop=True).then_inc(r.S["c0_filled"], 1)

            def c_qt(b):
                r, o = second_layer(b)
                c1_fill(b, C1_QT)
                mm(r.ps_c1[:, :], wqT[:, :], r.hT[:, :], start=True, stop=True).then_inc(r.S["c1_filled"], 1)

            def c_vk(b):
                r, o = second_layer(b)
                for bank, fill, filled, n in ((r.ps_c0, c0_fill, "c0_filled", C0_VK), (r.ps_c1, c1_fill, "c1_filled", C1_VK)):
                    fill(b, n)
                    for m in range(2):
                        i = m if bank is r.ps_c0 else 2 + m
                        last = mm(bank[:, VK * m:VK * (m + 1)], r.hT[:, tok(i)], wvk[:, :], start=True, stop=True)
                    last.then_inc(r.S[filled], 1)

            def c_gram(b):
                r, o = second_layer(b)
                c0_fill(b, C0_GRAM)
                for i in range(NT):
                    last = mm(r.ps_c0[:, tok(i)], r.kT[:, tok(i)], r.kT[:, tok(i)], start=True, stop=True)
                last.then_inc(r.S["c0_filled"], 1)
                c1_fill(b, C1_KQ)
                for i in range(NT):
                    last = mm(r.ps_c1[:, tok(i)], r.kT[:, tok(i)], r.qT[:, tok(i)], start=True, stop=True)
                last.then_inc(r.S["c1_filled"], 1)

            def lev_a(b, lv):
                r, o = second_layer(b)
                c0_fill(b, c0_a(lv))
                pe.wait_ge(r.S["pair_ready"], o.count(LEVELS - 1, lv))
                if lv == 1:
                    pe.wait_ge(r.S["inv1_ready"], o.count(2, 2))
                for i in range(NT):
                    last = mm(r.ps_c0[:, tok(i)], r.pair_up[lv % 2][:, i, :], r.inv[:, i, :], start=True, stop=True)
                last.then_inc(r.S["c0_filled"], 1)

            def lev_d(b, lv):
                r, o = second_layer(b)
                c1_fill(b, c1_dt(lv))
                pe.wait_ge(r.S["c0_emptied"], o.count(C0_FILLS, c0_a(lv) + 1))
                if lv == 1:
                    pe.wait_ge(r.S["invt1_ready"], o.count(1, 1))
                if lv < LEVELS - 1:
                    c0_fill(b, c0_d(lv))
                    for i in range(NT):
                        last = mm(r.ps_c0[:, tok(i)], r.invT[:, i, :], r.ablk[:, i, :], start=True, stop=True)
                    last.then_inc(r.S["c0_filled"], 1)
                for i in range(NT):
                    last = mm(r.ps_c1[:, tok(i)], r.ablk[:, i, :], r.invT[:, i, :], start=True, stop=True)
                last.then_inc(r.S["c1_filled"], 1)

            def c_ffn(b):
                r, o = second_layer(b)
                c1_fill(b, C1_FFN)
                for i in range(NT):
                    last = mm(r.ps_c1[:, tok(i)], r.xn2T[:, tok(i)], sgT[:, :], start=True, stop=True)
                last.then_inc(r.S["c1_filled"], 1)

            def c_r(b, c):
                r, o = second_layer(b)
                c0_fill(b, c0_r(c))
                mm(r.ps_c0[:, 0:P], r.kT[:, tok(c)], r.state[:, :], start=True, stop=True).then_inc(r.S["c0_filled"], 1)

            def c_u(b, c):
                r, o = second_layer(b)
                c0_fill(b, c0_u(c))
                if c == 0:
                    pe.wait_ge(r.S["c1_emptied"], o.count(C1_FILLS, c1_dt(LEVELS - 1) + 1))
                mm(r.ps_c0[:, 0:P], r.invT[:, c, :], r.vk[:, 0, 0:P] if c == 0 else r.rhs[:, :], start=True, stop=True)\
                    .then_inc(r.S["c0_filled"], 1)

            def c_y(b, c):
                r, o = second_layer(b)
                if c == 0:
                    c1_fill(b, C1_Y)
                pe.wait_ge(r.S["c0_emptied"], o.count(C0_FILLS, c0_u(c) + 1))
                if c > 0:
                    mm(r.ps_c1[:, tok(c)], r.qT[:, tok(c)], r.state[:, :], start=False, stop=False, skip_group_check=True)
                last = mm(r.ps_c1[:, tok(c)], r.kq[:, c, :], r.u_sb[:, :], start=(c == 0), stop=True, skip_group_check=True)
                if c == NT - 1:
                    last.then_inc(r.S["c1_filled"], 1)
                else:
                    mm(r.ps_c0[0:DS, 0:P], r.vk[:, c, P:VK], r.u_sb[:, :], start=True, stop=True).then_inc(r.S["c0_filled"], 1)

            pieces = {"xnt": xnt, "q": lambda b: qk(b, 0), "k": lambda b: qk(b, 1), "v": v, "logits": logits, "gt": gt,
                      "out": out_piece, "m_rows0": lambda b: m_rows(b, 0), "m_rows1": lambda b: m_rows(b, 1), "pv0": lambda b, grp: pv(b, grp, 0), "pv1": lambda b, grp: pv(b, grp, 1), "pv2": lambda b, grp: pv(b, grp, 2), "yt": yt, "c_xn2t": c_xn2t, "c_ht": c_ht, "c_kt": c_kt,
                      "c_qt": c_qt, "c_vk": c_vk, "c_gram": c_gram, "c_ffn": c_ffn}
            for c in range(NC):
                pieces[f"h{c}"] = lambda b, c=c: h(b, c)
                pieces[f"gb{c}"] = lambda b, c=c: gb(b, c)
            for lv in range(1, LEVELS):
                pieces[f"lev_a{lv}"] = lambda b, lv=lv: lev_a(b, lv)
                pieces[f"lev_d{lv}"] = lambda b, lv=lv: lev_d(b, lv)
            for c in range(NT):
                pieces[f"c_r{c}"] = lambda b, c=c: c_r(b, c)
                pieces[f"c_u{c}"] = lambda b, c=c: c_u(b, c)
                pieces[f"c_y{c}"] = lambda b, c=c: c_y(b, c)
            run(pe, pieces, unit, prepare, settle)

        @block.scalar
        def _(act):
            af = nc.scalar.activation
            copy = nc.scalar.copy
            sqrt_hd = float(HD) ** 0.5
            for n in names:
                if n not in ONCE:
                    act.sem_inc(S[n], 1)
            for n in second_names:
                act.sem_inc(last.S[n], 1)
            act.wait_ge(S["first_loaded"], FIRST_LOADED)
            af(cent_sq[:, :], nat["cent"][:, :], ACT.Square, accum_out=cent_ss[:, :]).then_inc(S["ss_ready"], 1)

            def prep(n, dst, src, scale=None):
                act.wait_ge(S["prep_pe"], n)
                (copy(dst, src) if scale is None else nc.scalar.mul(dst, src, scale)).then_inc(S["prep_out"], 1)

            perm = lambda w: w.rearrange("c (h d) -> c d h", d=HD)
            perm_out = lambda w: w.rearrange("c (d h) -> c d h", d=HD)
            prep(1, uqT[:, :], ps_a[0:QL, 0:P])
            prep(2, oT[:, :], ps_c0[:, 0:P])
            prep(3, wqeT[:, :], ps_c1[:, 0:P])
            prep(4, perm_out(w_q[:, :]), perm(ps_a[:, 0:P]), 1.0 / sqrt_hd)
            prep(5, veff[:, :], ps_c0[0:KVL, 0:P])
            prep(6, keffT[:, :], ps_c1[0:KVL, 0:P])
            prep(7, w_v[:, :], ps_c0[:, 0:P])
            prep(8, perm_out(w_k[:, :]), perm(ps_a[:, 0:P]))
            def prepare():
                for stack in (qst, kst):
                    af(stack[1][64:P, :, :].bitcast(F32), ident[64:P, 0:1].unsqueeze(2).to_broadcast([64, HEADS, TOK // 2]),
                       ACT.Copy, scale=0.0).then_inc(S["stack_zeroed1"], 1)
                act.wait_ge(S["loaded"], LOADED)
                act.wait_ge(S["const_ready"], 4)
                prep(9, wkT[:, 0:DS], ps_c0[:, 0:DS])
                prep(9, wvk[:, P:P + DS], ps_c0[:, 0:DS])
                prep(10, wqT[:, 0:DS], ps_c1[:, 0:DS])
                prep(11, vecT[:, :], ps_v[:, 0:NC + 4])
                act.wait_ge(S["prep_out"], 12)
                nc.scalar.mul(bq_lr[:, :], vecT[:, NC + 3:NC + 4], LR).then_inc(S["prep_out"], 1)
                prep(12, wvk[:, 0:P], ps_s[:, 0, 0:P])
                act.wait_ge(S["prep_pe"], 13)
                af(sgT[:, :], ps_s[:, 1, 0:P], ACT.Sign).then_inc(S["prep_sign"], 1)
                act.wait_ge(S["prep_sign"], 1)
                nc.scalar.mul(sgT[:, :], sgT[:, :], 0.5).then_inc(S["prep_out"], 1)
                prep(14, vkbias[:, :], ps_e[:, 0, 0:VK])
                act.wait_ge(S["rn_ready"], 1)
                nc.scalar.mul(rw[0:EXPERTS, :], nat["cent"][:, :], cent_rn[:, 1:2]).then_inc(S["prep_out"], 1)
                prep(15, rwT[:, :], ps_e[:, 1, 0:2 * EXPERTS])

            def a_full(b, n):
                act.wait_ge(S["a_filled"], b.count(A_FILLS, a_number(b, n) + 1))

            def c0_full(b, n):
                r, o = second_layer(b)
                act.wait_ge(r.S["c0_filled"], o.count(C0_FILLS, n + 1))

            def c1_full(b, n):
                r, o = second_layer(b)
                act.wait_ge(r.S["c1_filled"], o.count(C1_FILLS, n + 1))

            def xnt(b):
                a_full(b, A_XNT)
                copy(xnT[b.parity][:, :], ps_a[:, :]).then_inc(S["a_emptied"], 1)
                after(act, S["rn_ready"], b.count(1, 0))
                for i in range(NT):
                    af(tG[:, i * P:(i + 1) * P], xn[:, i, :], ACT.Square, accum_out=ss[:, i:i + 1]).then_inc(S["ss_ready"], 1)

            def split_hi(b, n):
                a_full(b, A_Q + n)
                after(act, S["scratch_written"], b.count(32, 0))
                copy(parts[n][:, 0, :], ps_a[:, :]).then_inc(S["hi_ready"], 1)

            def v(b):
                a_full(b, A_V)
                after(act, S["pv_used"], b.count(3 * GROUPS, 0))
                copy(vaug[:, :, :, 0:HD], ps_a[:, :].rearrange("p (i h d) -> p i h d", i=NT, h=HEADS))\
                    .then_inc(S["a_emptied"], 1)

            def gates(b):
                act.wait_ge(S["dlt_ready"], b.count(1, 1))
                af(ex[:, :, :], dlt[:, :, :], ACT.Exp).then_inc(S["ex_ready"], 1)

            def gt(b):
                a_full(b, A_GT)
                copy(gT[0:PARTS * EXPERTS, :], ps_a[:, :].bitcast(BF16)[0:PARTS * EXPERTS, 0:TOK]).then_inc(S["a_emptied"], 1)

            def h(b, c):
                a_full(b, A_H + c)
                after(act, S["gelu_ready"], b.count(1, 0))
                af(hid[:, c, :], ps_a[:, :], ACT.Identity, bias=vecT[:, c:c + 1]).then_inc(S["a_emptied"], 1)

            def gelu(b):
                act.wait_ge(S["a_emptied"], b.count(A_FILLS, a_number(b, A_H + NC)))
                af(hid[:, :, :], hid[:, :, :], ACT.Gelu).then_inc(S["gelu_ready"], 1)

            def out_piece(b):
                a_full(b, A_OUT)
                af(tG[:, :], ps_a[:, :], ACT.Tanh).then_inc(S["tg_ready"], 1)

            def m_rows(b, half):
                a_full(b, (A_M0, A_M1)[half])
                after(act, S["mscratch_written"], b.count(32, 16 * half))
                copy(mrow[:, :], ps_a[:, :].bitcast(BF16)[0:PARTS * 32, 0:TOK]).then_inc(S["a_emptied"], 1)

            def unit(cur, nxt, grp, u):
                if cur is None:
                    return
                act.wait_ge(S["e_filled"], cur.count(GROUPS * UNITS, UNITS * grp + u + 1))
                if u in (0, 4, 8):
                    after(act, S["pv_used"], cur.count(3 * GROUPS, 3 * (grp - 1) + u // 4 + 1))
                af(prob[:, u, :], ps_e[:, u % 2, :], ACT.Exp).then_inc(S["e_emptied"], 1)

            def pv(b, grp):
                if grp == GROUPS - 1:
                    return
                act.wait_ge(S["pv_used"], b.count(3 * GROUPS, 3 * grp + 3))
                copy(yT[:, :], ps_v[:, :]).then_inc(S["v_emptied"], 1)

            def c_xn2t(b):
                r, o = second_layer(b)
                c0_full(b, C0_XN2T)
                copy(r.xn2T[:, :], r.ps_c0[:, :]).then_inc(r.S["c0_emptied"], 1)

            def c_ht(b):
                r, o = second_layer(b)
                c1_full(b, C1_HT)
                af(r.hT[:, :], r.ps_c1[:, :], ACT.Identity, bias=vecT[:, NC + 1:NC + 2], scale=vecT[:, NC:NC + 1]).then_inc(r.S["c1_emptied"], 1)

            def c_kt(b):
                r, o = second_layer(b)
                c0_full(b, C0_KT)
                af(r.kT[:, :], r.ps_c0[:, :], ACT.Identity, bias=vecT[:, NC + 2:NC + 3]).then_inc(r.S["c0_emptied"], 1)

            def c_qt(b):
                r, o = second_layer(b)
                c1_full(b, C1_QT)
                af(r.qT[:, :], r.ps_c1[:, :], ACT.Identity, bias=bq_lr[:, :], scale=LR).then_inc(r.S["c1_emptied"], 1)

            def c_gram(b):
                r, o = second_layer(b)
                c0_full(b, C0_GRAM)
                copy(r.gram[:, :, :].rearrange("p i d -> p (i d)"), r.ps_c0[:, :]).then_inc(r.S["c0_emptied"], 1)

            def lev_a(b, lv):
                r, o = second_layer(b)
                c0_full(b, c0_a(lv))
                copy(half(r.ablk, lv, 0), half_bank(r.ps_c0, lv, 0)).then_inc(r.S["c0_emptied"], 1)

            def c_ffn(b):
                r, o = second_layer(b)
                c1_full(b, C1_FFN)
                after(act, r.S["syg_ready"], o.count(1, 0))
                af(r.tF[:, :], r.ps_c1[:, :], ACT.Tanh).then_inc(r.S["tf_ready"], 1)

            def c_u(b, c):
                r, o = second_layer(b)
                c0_full(b, c0_u(c))
                copy(r.u_sb[:, :], r.ps_c0[:, 0:P]).then_inc(r.S["c0_emptied"], 1)

            pieces = {"xnt": xnt, "q": lambda b: split_hi(b, 0), "k": lambda b: split_hi(b, 1), "v": v, "gates": gates, "gt": gt,
                      "gelu": gelu, "out": out_piece, "m_rows0": lambda b: m_rows(b, 0), "m_rows1": lambda b: m_rows(b, 1), "pv2": pv, "c_xn2t": c_xn2t, "c_ht": c_ht, "c_kt": c_kt,
                      "c_qt": c_qt, "c_gram": c_gram, "c_ffn": c_ffn}
            for c in range(NC):
                pieces[f"h{c}"] = lambda b, c=c: h(b, c)
                pieces[f"c_u{c}"] = lambda b, c=c: c_u(b, c)
            for lv in range(1, LEVELS):
                pieces[f"lev_a{lv}"] = lambda b, lv=lv: lev_a(b, lv)
            run(act, pieces, unit, prepare)

        @block.vector
        def _(dve):
            vec = nc.vector
            def zero_rows(stack, p):
                vec.memset(stack[p][64:P, :, :].bitcast(F32), 0.0).then_inc(S[f"stack_zeroed{p}"], 1)

            def ones_rows(p):
                dve.wait_ge(S[f"stack_zeroed{p}"], 2)
                vec.memset(kst[p][MAXROW:MAXROW + PARTS, :, :].bitcast(F32), ONES).then_inc(S[f"stack_zeroed{p}"], 1)

            zero_rows(qst, 0)

            def zero_piece(b):
                if b.pair is None and b.c == 0:
                    zero_rows(kst, 0)

            def prepare():
                ones_rows(0)
                ones_rows(1)
                dve.wait_ge(S["loaded"], LOADED)
                vec.tensor_scalar(w2s[:, :, :], w2s[:, :, :], 0.5, None, ALU.mult).then_inc(S["prep_out2"], 1)
                vec.tensor_scalar(b2r[:, 0, :], b2f[:, :], 0.5, None, ALU.mult).then_inc(S["prep_out2"], 1)
                dve.wait_ge(S["prep_out2"], 2)
                vec.tensor_copy(b2p[:, 0, :], b2r[:, 0, :]).then_inc(S["prep_out2"], 1)
                dve.wait_ge(S["prep_out2"], 3)
                vec.tensor_tensor(b2r[:, 1, :], b2r[:, 0, :], b2p[:, 0, :], ALU.subtract).then_inc(S["prep_out2"], 1)
                dve.wait_ge(S["prep_out2"], 4)
                vec.tensor_copy(b2p[:, 1, :], b2r[:, 1, :]).then_inc(S["prep_out2"], 1)
                dve.wait_ge(S["prep_out2"], 5)
                vec.tensor_tensor(b2p[:, 2, :], b2r[:, 1, :], b2p[:, 1, :], ALU.subtract).then_inc(S["prep_out2"], 1)
                dve.wait_ge(S["const_ready"], 4)
                dve.wait_ge(S["prep_out"], PREP_OUT)

            def settle():
                dve.wait_ge(S["masks_ready"], 1)
                vec.tensor_reduce(left_minus[:, :], upmask[:, :, :], AX_X, ALU.max).then_inc(S["left_ready"], 1)
                dve.wait_ge(S["left_ready"], 1)
                vec.tensor_scalar(left_minus[:, :], left_minus[:, :], 0.0, -1.0, ALU.is_gt, ALU.mult).then_inc(S["left_ready"], 1)
                dve.wait_ge(S["left_ready"], 2)

            def a_full(b, n):
                dve.wait_ge(S["a_filled"], b.count(A_FILLS, a_number(b, n) + 1))

            def c0_full(b, n):
                r, o = second_layer(b)
                dve.wait_ge(r.S["c0_filled"], o.count(C0_FILLS, n + 1))

            def c1_full(b, n):
                r, o = second_layer(b)
                dve.wait_ge(r.S["c1_filled"], o.count(C1_FILLS, n + 1))

            def ln_stats(n, b):
                r, o = second_layer(b) if n else (body, b)
                if n == 0:
                    dve.wait_ge(S["x_loaded"], o.count(16, 16))
                    src = xn
                elif n == 1:
                    dve.wait_ge(S["x1_ready"], b.count(1, 1))
                    src = x1[b.parity]
                else:
                    dve.wait_ge(r.S["norm1"], o.count(NT, NT))
                    src = r.xn2
                for i in range(NT):
                    vec.bn_stats(r.stats[n][:, i, :], src[:, i, :]).then_inc(r.S[f"stats{n}"], 1)
                settled(dve, r.S[f"stats{n}"], o.count(NT, NT))
                for i in range(NT):
                    vec.bn_aggr(r.mv[n][:, i, :], r.stats[n][:, i, :]).then_inc(r.S[f"mv{n}"], 1)

            def ln_norm(n, b):
                r, o = second_layer(b) if n else (body, b)
                src, dst = ((xn, xn), (x1[b.parity], r.xn2), (r.xn2, r.hn))[n]
                dve.wait_ge(r.S[f"rstd{n}"], o.count(1, 1))
                if n == 1:
                    after(dve, r.S["c1_emptied"], o.count(C1_FILLS, 0))
                elif n == 2:
                    after(dve, r.S["c1_filled"], o.count(C1_FILLS, 0))
                for i in range(NT):
                    vec.tensor_scalar(dst[:, i, :], src[:, i, :], r.mv[n][:, i, 0:1], r.rstd[n][:, i:i + 1], ALU.subtract, ALU.mult)\
                        .then_inc(r.S[f"norm{n}"], 1)

            def split_rest(b, n):
                dve.wait_ge(S["hi_ready"], b.count(2, n + 1))
                after(dve, S["parts_ready"], b.count(2, 0))
                vec.tensor_tensor(rest[n], ps_a[:, :], parts[n][:, 0, :], ALU.subtract).then_inc(S["a_emptied"], 1)

            def logits(b):
                a_full(b, A_LOGIT)
                dve.wait_ge(S["rn_ready"], b.count(1, 1))
                lg = ps_a[:, 0:2 * EXPERTS * NT].rearrange("p (i e) -> p i e", i=NT)
                vec.tensor_tensor(coss[:, :, :], lg[:, :, 0:EXPERTS], bcast(rn[:, :], 2, EXPERTS), ALU.mult).then_inc(S["cos_ready"], 1)
                dve.wait_ge(S["cos_ready"], b.count(1, 1))
                vec.tensor_tensor(logit[:, :, :], lg[:, :, EXPERTS:2 * EXPERTS], coss[:, :, :], ALU.add).then_inc(S["a_emptied"], 1)
                settled(dve, S["a_emptied"], b.count(A_FILLS, a_number(b, A_LOGIT) + 1))
                for i in range(NT):
                    vec.max(top8[:, i, :], logit[:, i, :]).then_inc(S["top_ready"], 1)

            def gates(b):
                dve.wait_ge(S["top_ready"], b.count(NT, NT))
                vec.tensor_tensor(dlt[:, :, :], logit[:, :, :], top8[:, :, 0:1].to_broadcast([P, NT, EXPERTS]), ALU.subtract)\
                    .then_inc(S["dlt_ready"], 1)
                vec.tensor_tensor(keep[:, :, :], logit[:, :, :], top8[:, :, 1:2].to_broadcast([P, NT, EXPERTS]), ALU.is_ge)\
                    .then_inc(S["keep_ready"], 1)
                dve.wait_ge(S["keep_ready"], b.count(1, 1))
                dve.wait_ge(S["ex_ready"], b.count(1, 1))
                vec.tensor_tensor(gm[:, :, :], ex[:, :, :], keep[:, :, :], ALU.mult).then_inc(S["gm_ready"], 1)
                dve.wait_ge(S["gm_ready"], b.count(1, 1))
                vec.tensor_reduce(gsum[:, :], gm[:, :, :], AX_X, ALU.add).then_inc(S["gsum_ready"], 1)
                dve.wait_ge(S["gsum_ready"], b.count(1, 1))
                vec.reciprocal(grec[:, :], gsum[:, :]).then_inc(S["grec_ready"], 1)
                dve.wait_ge(S["grec_ready"], b.count(1, 1))
                vec.tensor_tensor(gate[:, :, :], gm[:, :, :], bcast(grec[:, :], 2, EXPERTS), ALU.mult).then_inc(S["gate_ready"], 1)

            def gb(b, c):
                a_full(b, A_GB + c)
                dve.wait_ge(S["gelu_ready"], b.count(1, 1))
                vec.tensor_tensor(hid[:, c, :], hid[:, c, :], ps_a[:, :], ALU.mult).then_inc(S["a_emptied"], 1)

            def out_piece(b):
                dve.wait_ge(S["tg_ready"], b.count(1, 1))
                after(dve, S["attg_ready"], b.count(1, 0))
                vec.scalar_tensor_tensor(out=gate_out[:, :, :].rearrange("p i d -> p (i d)"), in0=tG[:, :], scalar=1.0,
                                         in1=ps_a[:, :], op0=ALU.add, op1=ALU.mult).then_inc(S["a_emptied"], 1)

            def unit(cur, nxt, mgrp, u):
                if nxt is None:
                    return
                i, keys, hds = S_UNIT[u]
                if mgrp == 0 and u == 0:
                    after(dve, S["nm_ready"], nxt.count(2, 0))
                dve.wait_ge(S["s_filled"], nxt.count(GROUPS * UNITS, UNITS * mgrp + u + 1))
                h0 = GH * mgrp + hds[0]
                vec.tensor_reduce(cand[:, i, h0:h0 + len(hds), S_SLOT[u]],
                                  ps_s[:, u % 2, :].rearrange("p (a c) -> p a c", a=len(hds)), AX_X, ALU.max)\
                    .then_inc(S["s_emptied"], 1)

            def m_parts(b, half):
                dve.wait_ge(S["s_emptied"], b.count(GROUPS * UNITS, GROUPS * UNITS * (half + 1) // 2))
                after(dve, S["mparts_ready"], b.count(2, half))
                vec.tensor_reduce(nm[:, :, :], cand[:, :, HALF_HEADS * half:HALF_HEADS * (half + 1), :], AX_X, ALU.max, negate=True)\
                    .then_inc(S["nm_ready"], 1)

            def pv(b, grp):
                if grp == GROUPS - 1:
                    dve.wait_ge(S["pv_used"], b.count(3 * GROUPS, 3 * grp + 3))
                    vec.tensor_copy(yT[:, :], ps_v[:, :]).then_inc(S["v_emptied"], 1)

            def yt(b, grp):
                dve.wait_ge(S["yt_filled"], b.count(GROUPS, grp + 1))
                y = ps_v[:, :].rearrange("p (i h e) -> p i h e", i=NT, h=GH)
                if grp == 0:
                    after(dve, S["x1_ready"], b.count(1, 0))
                after(dve, S["v_emptied"], b.count(2 * GROUPS, 2 * grp))
                vec.reciprocal(rden[:, :, :], y[:, :, :, HD]).then_inc(S["rden_ready"], 1)
                dve.wait_ge(S["rden_ready"], b.count(GROUPS, grp + 1))
                w = GH * HD
                vec.tensor_tensor(att[:, :, w * grp:w * (grp + 1)].rearrange("p i (h d) -> p i h d", h=GH), y[:, :, :, 0:HD],
                                  bcast(rden[:, :, :], 3, HD), ALU.mult).then_inc(S["v_emptied"], 1)

            def c_vk(b):
                r, o = second_layer(b)
                bias = bcast(vkbias[:, :], 1, 2)
                c0_full(b, C0_VK)
                vec.tensor_tensor(r.vk[:, 0:2, :], r.ps_c0[:, 0:2 * VK].rearrange("p (i d) -> p i d", i=2), bias, ALU.add).then_inc(r.S["c0_emptied"], 1)
                c1_full(b, C1_VK)
                vec.tensor_tensor(r.vk[:, 2:4, :], r.ps_c1[:, 0:2 * VK].rearrange("p (i d) -> p i d", i=2), bias, ALU.add).then_inc(r.S["c1_emptied"], 1)

            def c_gram(b):
                r, o = second_layer(b)
                c1_full(b, C1_KQ)
                vec.tensor_tensor(r.kq[:, :, :], r.ps_c1[:, :].rearrange("p (i d) -> p i d", i=NT), bcast(strict[:, :], 1, NT), ALU.mult)\
                    .then_inc(r.S["c1_emptied"], 1)
                dve.wait_ge(r.S["c0_emptied"], o.count(C0_FILLS, C0_GRAM + 1))
                after(dve, r.S["out_ready"], o.count(1, 0))
                vec.tensor_tensor(r.syg[:, :, :], r.gram[:, :, :], bcast(upmask[:, 0, :], 1, NT), ALU.mult).then_inc(r.S["dtmpt_ready"], 1)
                dve.wait_ge(r.S["dtmpt_ready"], o.count(1, 1))
                vec.tensor_tensor(r.invT[:, :, :], bcast(ident[:, :], 1, NT), r.syg[:, :, :], ALU.subtract).then_inc(r.S["invt1_ready"], 1)

            def lev_d(b, lv):
                r, o = second_layer(b)
                if lv == 1:
                    dve.wait_ge(r.S["inv1_ready"], o.count(2, 2))
                if lv < LEVELS - 1:
                    c0_full(b, c0_d(lv))
                    vec.tensor_tensor(half(r.inv, lv, 0), half(r.inv, lv, 0), half_bank(r.ps_c0, lv, 0), ALU.subtract).then_inc(r.S["c0_emptied"], 1)
                c1_full(b, c1_dt(lv))
                vec.scalar_tensor_tensor(out=half(r.invT, lv, 1), in0=half_bank(r.ps_c1, lv, 1), scalar=left_minus[:, lv:lv + 1],
                                         in1=half(r.invT, lv, 1), op0=ALU.mult, op1=ALU.add).then_inc(r.S["c1_emptied"], 1)

            def c_ffn(b):
                r, o = second_layer(b)
                dve.wait_ge(r.S["tf_ready"], o.count(1, 1))
                after(dve, r.S["syg_ready"], o.count(1, 0))
                vec.scalar_tensor_tensor(out=r.tF[:, :], in0=r.tF[:, :], scalar=1.0, in1=r.ps_c1[:, :], op0=ALU.add, op1=ALU.mult)\
                    .then_inc(r.S["c1_emptied"], 1)

            def c_r(b, c):
                r, o = second_layer(b)
                c0_full(b, c0_r(c))
                vec.scalar_tensor_tensor(out=r.rhs[:, :], in0=r.ps_c0[:, 0:P], scalar=-LR, in1=r.vk[:, c, 0:P], op0=ALU.mult, op1=ALU.add)\
                    .then_inc(r.S["c0_emptied"], 1)

            def c_y(b, c):
                r, o = second_layer(b)
                if c == 0:
                    c0_full(b, c0_s(c))
                    vec.tensor_copy(r.state[0:DS, :], r.ps_c0[0:DS, 0:P]).then_inc(r.S["c0_emptied"], 1)
                elif c < NT - 1:
                    c0_full(b, c0_s(c))
                    vec.tensor_tensor(r.state[0:DS, :], r.state[0:DS, :], r.ps_c0[0:DS, 0:P], ALU.add).then_inc(r.S["c0_emptied"], 1)
                else:
                    c1_full(b, C1_Y)
                    after(dve, r.S["syg_ready"], o.count(1, 0))
                    vec.tensor_tensor(r.sy[:, :, :], r.ps_c1[:, :].rearrange("p (i d) -> p i d", i=NT), r.xn2[:, :, :], ALU.add)\
                        .then_inc(r.S["c1_emptied"], 1)

            pieces = {"ln1_stats": lambda b: ln_stats(0, b), "ln2_stats": lambda b: ln_stats(1, b), "ln3_stats": lambda b: ln_stats(2, b),
                      "ln1_norm": lambda b: ln_norm(0, b), "ln2_norm": lambda b: ln_norm(1, b), "ln3_norm": lambda b: ln_norm(2, b),
                      "q": lambda b: split_rest(b, 0), "k": lambda b: split_rest(b, 1), "logits": logits, "gates": gates, "zero": zero_piece,
                      "out": out_piece, "m_parts0": lambda b: m_parts(b, 0), "m_parts1": lambda b: m_parts(b, 1), "pv2": pv, "yt": yt, "c_vk": c_vk, "c_gram": c_gram, "c_ffn": c_ffn}
            for c in range(NC):
                pieces[f"gb{c}"] = lambda b, c=c: gb(b, c)
                pieces[f"c_r{c}"] = lambda b, c=c: c_r(b, c)
                pieces[f"c_y{c}"] = lambda b, c=c: c_y(b, c)
            for lv in range(1, LEVELS):
                pieces[f"lev_d{lv}"] = lambda b, lv=lv: lev_d(b, lv)
            run(dve, pieces, unit, prepare, settle)


ONCE = ("const_ready", "mask_step", "loaded", "prep_pe", "prep_out", "prep_out2", "prep_sign", "small_zeroed", "stack_zeroed0", "stack_zeroed1",
        "first_loaded", "masks_ready", "left_ready", "coarse_ready", "coarse_loaded",
        "ss_ready", "rn_ready")
PREP_OUT = 18
S_UNIT = [(i, (P * i, P * i + P), (0, 1, 2, 3)) for i in range(4)] + [
    (1, (0, 128), (0, 1, 2, 3)), (2, (0, 256), (0, 1)), (2, (0, 256), (2, 3)),
    (3, (0, 256), (0, 1)), (3, (0, 256), (2, 3)), (3, (256, 384), (0, 1, 2, 3))]
S_SLOT = [0, 0, 0, 0, 1, 1, 1, 1, 1, 2]

_INS = ["L0_attn_x", "L0_attn_W_dq", "L0_attn_W_uq", "L0_attn_W_dkv", "L0_attn_W_uk", "L0_attn_W_uv", "L0_attn_W_o",
        "L0_ffn_w1", "L0_ffn_b1", "L0_ffn_w2", "L0_ffn_b2", "L0_ffn_centroids", "L0_ffn_w_route",
        "L1_attn_Wk", "L1_attn_bk", "L1_attn_Wv", "L1_attn_bv", "L1_attn_Wq", "L1_attn_bq", "L1_attn_gamma", "L1_attn_beta",
        "L1_ffn_weight"]


def kernel(**inputs):
    import numpy as _np
    import concourse.bacc as _bacc
    from concourse import mybir as _mybir
    from concourse.bass_utils import run_bass_kernel_spmd as _run

    nc = _bacc.Bacc("TRN2", target_bir_lowering=False, num_devices=1)
    arrays, args = {}, []
    for name in _INS:
        a = _np.ascontiguousarray(inputs[name])
        arrays[f"in_{name}_dram"] = a
        args.append(nc.dram_tensor(f"in_{name}_dram", a.shape, _mybir.dt.from_np(a.dtype), kind="ExternalInput").ap())
    shape = tuple(inputs["L0_attn_x"].shape)
    args.append(nc.dram_tensor("out_dram", shape, _mybir.dt.float32, kind="ExternalOutput").ap())
    nc.disable_value_cache = True
    two_layers(nc, *args)
    r = _run(nc, [arrays], core_ids=[0])
    return r.results[0]["out_dram"]
```
